# Optimizing a Trainium2 kernel written in Bass

```python
import numpy as np
import jax
import jax.numpy as jnp

def _softmax(x, axis=-1):
    return jax.nn.softmax(x, axis=axis)

def _gelu(x):
    return jax.nn.gelu(x, approximate=True)

def _silu(x):
    return jax.nn.silu(x)

def _sigmoid(x):
    return jax.nn.sigmoid(x)

def _layernorm(x, axis=-1, eps=1e-05):
    m = jnp.mean(x, axis=axis, keepdims=True)
    v = jnp.var(x, axis=axis, keepdims=True)
    return (x - m) / jnp.sqrt(v + eps)

def _scatter_add(tgt, idx, src, axis=0):
    return tgt.at[idx].add(src)

def _segment_sum(src, seg, n):
    return jax.ops.segment_sum(src, seg, n)
kernel_name = 'mk_perceiver_d2_seqx_r8_11345d'

def setup_inputs(seed: int=0):
    np.random.seed(seed)
    _w = jnp.asarray

    def _rec_inputs():
        import jax
        import jax.numpy as jnp
        _rk = jax.random.key(seed)
        x = 7.22e-05 + 1 * jax.random.normal(jax.random.fold_in(_rk, 1), (4, 128, 128), jnp.float32)
        _lenS = 128 - jax.random.randint(jax.random.fold_in(_rk, 7), (4,), 0, max(1, 128 // 4) + 1, jnp.int32)
        _lenS2 = 2048 - jax.random.randint(jax.random.fold_in(_rk, 8), (4,), 0, max(1, 2048 // 4) + 1, jnp.int32)
        _ctx_1024P = jax.random.normal(jax.random.fold_in(_rk, 11), (4, 16, 128), jnp.float32)
        _ctx_1024c = jax.random.dirichlet(jax.random.fold_in(_rk, 511), 0.3 * jnp.ones((16,), jnp.float32), (4, 2048))
        _ctx_1024t = jnp.einsum('bsk,bkd->bsd', _ctx_1024c, _ctx_1024P)
        _ctx_1024t = _ctx_1024t * jax.lax.rsqrt(jnp.mean(jnp.square(_ctx_1024t)) + 1e-12) * 0.953939
        ctx_1024 = 4.13588e-05 + 0.999923 * (_ctx_1024t + 0.3 * jax.random.normal(jax.random.fold_in(_rk, 611), (4, 2048, 128), jnp.float32))
        _validS = jnp.arange(128)[None, :] < _lenS[:, None]
        _validS2 = jnp.arange(2048)[None, :] < _lenS2[:, None]
        _causal = jnp.tril(jnp.ones((128, 128), dtype=bool))
        mask_Bx1xSxS2_ik1 = jnp.where(jnp.broadcast_to(_validS2[:, None, None, :], (4, 1, 128, 2048)), 1, 0).astype(jnp.int32)
        return (x, ctx_1024, mask_Bx1xSxS2_ik1)
    x, ctx_1024, mask_Bx1xSxS2_ik1 = _rec_inputs()

    def _L0_xattn_setup():
        import jax, jax.numpy as jnp
        import numpy as np
        H, D, DIM = (8, 128, 128)
        QB, N = (16, 64)

        def layer_norm(x, g, b, eps=1e-05):
            mu = x.mean(-1, keepdims=True)
            var = ((x - mu) ** 2).mean(-1, keepdims=True)
            return (x - mu) / jnp.sqrt(var + eps) * g + b
        key = jax.random.key(seed)
        ks = jax.random.split(key, 8)
        rn = lambda k, shape, s=1.0: jax.random.normal(k, shape, jnp.float32) * s
        return {'q': rn(ks[0], (QB, N, DIM)), 'k': rn(ks[1], (QB, N, DIM)), 'v': rn(ks[2], (QB, N, DIM)), 'ln_g': jnp.ones(DIM, jnp.float32), 'ln_b': jnp.zeros(DIM, jnp.float32), 'w_in': rn(ks[3], (H * D, DIM), 0.02), 'wp_w1': rn(ks[4], (D, 2 * D), 0.05), 'wp_b1': jnp.zeros(D, jnp.float32), 'wp_ln_g': jnp.ones(D, jnp.float32), 'wp_ln_b': jnp.zeros(D, jnp.float32), 'wp_w2': rn(ks[5], (3, D), 0.05), 'wp_b2': jnp.zeros(3, jnp.float32), 'w_out': rn(ks[6], (DIM, H * D), 0.02), 'b_out': jnp.zeros(DIM, jnp.float32)}
    _L0_xattn_all = _L0_xattn_setup()
    _L0_xattn_in = {k: v for k, v in _L0_xattn_all.items() if k in ('ln_g', 'ln_b', 'w_in', 'wp_w1', 'wp_b1', 'wp_ln_g', 'wp_ln_b', 'wp_w2', 'wp_b2', 'w_out', 'b_out')}
    del _L0_xattn_all

    def _L0_attn_setup():
        import jax, jax.numpy as jnp
        import numpy as np
        B, S, D = (4, 256, 128)

        def _gaussian_mask(seq_len, dtype):
            pos = jnp.arange(seq_len, dtype=dtype)
            center = seq_len / 2
            sigma = seq_len / 4
            m = jnp.exp(-0.5 * ((pos - center) / sigma) ** 2)
            return m[None, None, :]
        key = jax.random.key(seed)
        ks = jax.random.split(key, 9)
        sc = 1.0 / np.sqrt(D)
        return {'x': jax.random.normal(ks[0], (B, S, D), dtype=jnp.float32), 'Wq': jax.random.normal(ks[1], (D, D), dtype=jnp.float32) * sc, 'bq': jnp.zeros((D,), dtype=jnp.float32), 'Wk': jax.random.normal(ks[2], (D, D), dtype=jnp.float32) * sc, 'bk': jnp.zeros((D,), dtype=jnp.float32), 'Wv': jax.random.normal(ks[3], (D, D), dtype=jnp.float32) * sc, 'bv': jnp.zeros((D,), dtype=jnp.float32), 'Wo': jax.random.normal(ks[4], (D, D), dtype=jnp.float32) * sc, 'bo': jnp.zeros((D,), dtype=jnp.float32)}
    _L0_attn_all = _L0_attn_setup()
    _L0_attn_in = {k: v for k, v in _L0_attn_all.items() if k in ('Wq', 'bq', 'Wk', 'bk', 'Wv', 'bv', 'Wo', 'bo')}
    del _L0_attn_all

    def _L0_ffn_setup():
        import jax, jax.numpy as jnp
        import numpy as np
        B, S, D, E, K = (4, 256, 128, 8, 2)
        H = 4 * D
        key = jax.random.key(seed)
        k0, k1, k2, k3 = jax.random.split(key, 4)
        x = jax.random.normal(k0, (B, S, D), dtype=jnp.float32)
        router_w = jax.random.normal(k1, (E, D), dtype=jnp.float32) * 0.02
        w1 = jax.random.normal(k2, (E, H, D), dtype=jnp.float32) * 0.02
        w2 = jax.random.normal(k3, (E, D, H), dtype=jnp.float32) * 0.02
        return {'x': x, 'router_w': router_w, 'w1': w1, 'w2': w2}
    _L0_ffn_all = _L0_ffn_setup()
    _L0_ffn_in = {k: v for k, v in _L0_ffn_all.items() if k in ('router_w', 'w1', 'w2')}
    del _L0_ffn_all

    def _L1_xattn_setup():
        import jax, jax.numpy as jnp
        import numpy as np
        EMBED = 128
        HEADS = 16
        HEAD_DIM = EMBED // HEADS
        key = jax.random.key(seed)
        ks = jax.random.split(key, 6)
        N, S, E = (2, 256, EMBED)
        value = jax.random.normal(ks[0], (N, S, E), dtype=jnp.float32)
        k = jax.random.normal(ks[1], (N, S, E), dtype=jnp.float32)
        q = jax.random.normal(ks[2], (N, S, E), dtype=jnp.float32)
        mask = jax.random.randint(ks[3], (N, 1, S, S), 0, 2, dtype=jnp.int32)
        W_fc = jax.random.normal(ks[4], (E, E), dtype=jnp.float32) * (1.0 / np.sqrt(E))
        b_fc = jax.random.normal(ks[5], (E,), dtype=jnp.float32) * 0.01
        return {'value': value, 'key': k, 'query': q, 'mask': mask, 'W_fc': W_fc, 'b_fc': b_fc}
    _L1_xattn_all = _L1_xattn_setup()
    _L1_xattn_in = {k: v for k, v in _L1_xattn_all.items() if k in ('W_fc', 'b_fc')}
    del _L1_xattn_all

    def _L1_attn_setup():
        import jax, jax.numpy as jnp
        import numpy as np
        EPS = 1e-08

        def rms_norm_multihead(x, weight):
            x32 = x.astype(jnp.float32)
            normed = x32 * jax.lax.rsqrt(jnp.mean(x32 * x32, axis=-1, keepdims=True) + EPS)
            return normed.astype(x.dtype) * weight
        key = jax.random.key(seed)
        k0, k1, k2 = jax.random.split(key, 3)
        B, L, D, H = (2, 128, 128, 16)
        d = D // H
        X = jax.random.normal(k0, (B, L, D), dtype=jnp.float32)
        Wq = jax.random.normal(k1, (D, D), dtype=jnp.float32) * 0.02
        Wv = jax.random.normal(k2, (D, D), dtype=jnp.float32) * 0.02
        q_norm_w = jnp.ones((H, d), dtype=jnp.float32)
        v_norm_w = jnp.ones((H, d), dtype=jnp.float32)
        return {'X': X, 'Wq': Wq, 'Wv': Wv, 'q_norm_w': q_norm_w, 'v_norm_w': v_norm_w}
    _L1_attn_all = _L1_attn_setup()
    _L1_attn_in = {k: v for k, v in _L1_attn_all.items() if k in ('Wq', 'Wv', 'q_norm_w', 'v_norm_w')}
    del _L1_attn_all

    def _L1_ffn_setup():
        import jax, jax.numpy as jnp
        import numpy as np
        B, S, DIM, FFN, E = (4, 256, 128, 512, 8)
        key = jax.random.key(seed)
        k0, k1, k2, k3 = jax.random.split(key, 4)
        scale = 0.02
        return {'hidden_states': jax.random.normal(k0, (B, S, DIM), jnp.float32), 'router_w': jax.random.normal(k1, (DIM, E), jnp.float32) * scale, 'router_b': jnp.zeros((E,), jnp.float32), 'w1': jax.random.normal(k2, (E, DIM, 2 * FFN), jnp.float32) * scale, 'w2': jax.random.normal(k3, (E, FFN, DIM), jnp.float32) * scale}
    _L1_ffn_all = _L1_ffn_setup()
    _L1_ffn_in = {k: v for k, v in _L1_ffn_all.items() if k in ('router_w', 'router_b', 'w1', 'w2')}
    del _L1_ffn_all
    return {'x': x, 'ctx_1024': ctx_1024, 'mask_Bx1xSxS2_ik1': mask_Bx1xSxS2_ik1, 'L0_xattn_ln_g': _L0_xattn_in['ln_g'], 'L0_xattn_ln_b': _L0_xattn_in['ln_b'], 'L0_xattn_w_in': _L0_xattn_in['w_in'], 'L0_xattn_wp_w1': _L0_xattn_in['wp_w1'], 'L0_xattn_wp_b1': _L0_xattn_in['wp_b1'], 'L0_xattn_wp_ln_g': _L0_xattn_in['wp_ln_g'], 'L0_xattn_wp_ln_b': _L0_xattn_in['wp_ln_b'], 'L0_xattn_wp_w2': _L0_xattn_in['wp_w2'], 'L0_xattn_wp_b2': _L0_xattn_in['wp_b2'], 'L0_xattn_w_out': _L0_xattn_in['w_out'], 'L0_xattn_b_out': _L0_xattn_in['b_out'], 'L0_attn_Wq': _L0_attn_in['Wq'], 'L0_attn_bq': _L0_attn_in['bq'], 'L0_attn_Wk': _L0_attn_in['Wk'], 'L0_attn_bk': _L0_attn_in['bk'], 'L0_attn_Wv': _L0_attn_in['Wv'], 'L0_attn_bv': _L0_attn_in['bv'], 'L0_attn_Wo': _L0_attn_in['Wo'], 'L0_attn_bo': _L0_attn_in['bo'], 'L0_ffn_router_w': _L0_ffn_in['router_w'], 'L0_ffn_w1': _L0_ffn_in['w1'], 'L0_ffn_w2': _L0_ffn_in['w2'], 'L1_xattn_W_fc': _L1_xattn_in['W_fc'], 'L1_xattn_b_fc': _L1_xattn_in['b_fc'], 'L1_attn_Wq': _L1_attn_in['Wq'], 'L1_attn_Wv': _L1_attn_in['Wv'], 'L1_attn_q_norm_w': _L1_attn_in['q_norm_w'], 'L1_attn_v_norm_w': _L1_attn_in['v_norm_w'], 'L1_ffn_router_w': _L1_ffn_in['router_w'], 'L1_ffn_router_b': _L1_ffn_in['router_b'], 'L1_ffn_w1': _L1_ffn_in['w1'], 'L1_ffn_w2': _L1_ffn_in['w2']}

def reference(x, ctx_1024, mask_Bx1xSxS2_ik1, L0_xattn_ln_g, L0_xattn_ln_b, L0_xattn_w_in, L0_xattn_wp_w1, L0_xattn_wp_b1, L0_xattn_wp_ln_g, L0_xattn_wp_ln_b, L0_xattn_wp_w2, L0_xattn_wp_b2, L0_xattn_w_out, L0_xattn_b_out, L0_attn_Wq, L0_attn_bq, L0_attn_Wk, L0_attn_bk, L0_attn_Wv, L0_attn_bv, L0_attn_Wo, L0_attn_bo, L0_ffn_router_w, L0_ffn_w1, L0_ffn_w2, L1_xattn_W_fc, L1_xattn_b_fc, L1_attn_Wq, L1_attn_Wv, L1_attn_q_norm_w, L1_attn_v_norm_w, L1_ffn_router_w, L1_ffn_router_b, L1_ffn_w1, L1_ffn_w2):
    import jax
    import jax.numpy as jnp

    def _L0_xattn_ref(q, k, v, ln_g, ln_b, w_in, wp_w1, wp_b1, wp_ln_g, wp_ln_b, wp_w2, wp_b2, w_out, b_out):
        import jax, jax.numpy as jnp
        import numpy as np
        H, D, DIM = (8, 128, 128)
        QB, N = (16, 64)

        def layer_norm(x, g, b, eps=1e-05):
            mu = x.mean(-1, keepdims=True)
            var = ((x - mu) ** 2).mean(-1, keepdims=True)
            return (x - mu) / jnp.sqrt(var + eps) * g + b

        def proj(t):
            x = layer_norm(t, ln_g, ln_b) @ w_in.T
            Qd, Nd = (t.shape[0], t.shape[1])
            return x.reshape(Qd, Nd, H, D).transpose(2, 0, 1, 3)
        f_q, f_k, f_v = (proj(q), proj(k), proj(v))
        dots = jnp.einsum('hqnd,hqmd->hqnm', f_q, f_k)
        qn = jnp.linalg.norm(f_q, axis=-1)
        kn = jnp.linalg.norm(f_k, axis=-1)
        cosine_sim = dots / (qn[..., :, None] * kn[..., None, :])
        q_centered = f_q - f_q.mean(-1, keepdims=True)
        q_var = jnp.var(f_q, axis=-1, ddof=1)
        k_var = jnp.var(f_k, axis=-1, ddof=1)
        q_ratio = 2.0 * jnp.minimum(q_var, 1.0) / (q_var + 1.0)
        k_ratio = 2.0 * jnp.minimum(k_var, 1.0) / (k_var + 1.0)
        var_component = jnp.einsum('hqn,hqm->hqnm', q_ratio, k_ratio)
        q_flat = q_centered.reshape(H, -1, D)
        feat_corr = jnp.einsum('hnd,hne->hde', q_flat, q_flat) / q_flat.shape[1]
        feat_corr = feat_corr * (1.0 - jnp.eye(D, dtype=feat_corr.dtype))
        decorr_score = jnp.linalg.norm(feat_corr, axis=(-2, -1)) / (D * D)
        decorr_scale = jnp.exp(-5.0 * decorr_score)[:, None, None, None]
        cov_component = cosine_sim * decorr_scale
        q_global = f_q.mean(axis=(1, 2))
        k_global = f_k.mean(axis=(1, 2))
        feats = jnp.concatenate([q_global, k_global], axis=-1)
        h1 = jnp.maximum(layer_norm(feats @ wp_w1.T + wp_b1, wp_ln_g, wp_ln_b), 0.0)
        weights = jax.nn.softmax(h1 @ wp_w2.T + wp_b2, axis=-1)
        cw = weights[:, 0][:, None, None, None]
        vw = weights[:, 1][:, None, None, None]
        ww = weights[:, 2][:, None, None, None]
        mixed = cw * cosine_sim + vw * cov_component + ww * var_component
        out = jnp.einsum('hqnm,hqmd->hqnd', mixed, f_v)
        out = out.transpose(1, 2, 0, 3).reshape(q.shape[0], q.shape[1], H * D)
        return out @ w_out.T + b_out

    def _L0_attn_ref(x, Wq, bq, Wk, bk, Wv, bv, Wo, bo):
        import jax, jax.numpy as jnp
        import numpy as np
        B, S, D = (4, 256, 128)

        def _gaussian_mask(seq_len, dtype):
            pos = jnp.arange(seq_len, dtype=dtype)
            center = seq_len / 2
            sigma = seq_len / 4
            m = jnp.exp(-0.5 * ((pos - center) / sigma) ** 2)
            return m[None, None, :]
        d = x.shape[-1]
        Q = x @ Wq.T + bq
        K = x @ Wk.T + bk
        V = x @ Wv.T + bv
        scores = jnp.einsum('bqd,bkd->bqk', Q, K) / jnp.sqrt(jnp.asarray(d, x.dtype))
        scores = scores * _gaussian_mask(x.shape[1], x.dtype)
        attn = jax.nn.softmax(scores, axis=-1)
        out = jnp.einsum('bqk,bkd->bqd', attn, V)
        return out @ Wo.T + bo

    def _L0_ffn_ref(x, router_w, w1, w2):
        import jax, jax.numpy as jnp
        import numpy as np
        B, S, D, E, K = (4, 256, 128, 8, 2)
        H = 4 * D
        b, s, d = x.shape
        e = router_w.shape[0]
        logits = jnp.einsum('bsd,ed->bse', x, router_w)
        probs = jax.nn.softmax(logits, axis=-1)
        topk_vals, topk_idx = jax.lax.top_k(probs, K)
        x_flat = x.reshape(b * s, d)
        vals = topk_vals.reshape(b * s, K)
        idx = topk_idx.reshape(b * s, K)
        out = jnp.zeros_like(x_flat)
        for eid in range(e):
            w = jnp.sum(jnp.where(idx == eid, vals, jnp.zeros((), x.dtype)), axis=-1)
            h = jax.nn.gelu(x_flat @ w1[eid].T, approximate=False)
            y = h @ w2[eid].T
            out = out + w[:, None] * y
        return out.reshape(b, s, d)

    def _L1_xattn_ref(value, key, query, mask, W_fc, b_fc):
        import jax, jax.numpy as jnp
        import numpy as np
        EMBED = 128
        HEADS = 16
        HEAD_DIM = EMBED // HEADS
        N, Sq, E = query.shape
        Sk = key.shape[1]
        Sv = value.shape[1]
        v = value.reshape(N, Sv, HEADS, HEAD_DIM)
        k = key.reshape(N, Sk, HEADS, HEAD_DIM)
        q = query.reshape(N, Sq, HEADS, HEAD_DIM)
        energy = jnp.einsum('nqhd,nkhd->nhqk', q, k)
        energy = jnp.where(mask == 0, jnp.float32(-1e+20), energy)
        attention = jax.nn.softmax(energy / jnp.sqrt(jnp.float32(E)), axis=3)
        out = jnp.einsum('nhql,nlhd->nqhd', attention, v).reshape(N, Sq, E)
        out = out @ W_fc.T + b_fc
        return out

    def _L1_attn_ref(X, Wq, Wv, q_norm_w, v_norm_w):
        import jax, jax.numpy as jnp
        import numpy as np
        EPS = 1e-08

        def rms_norm_multihead(x, weight):
            x32 = x.astype(jnp.float32)
            normed = x32 * jax.lax.rsqrt(jnp.mean(x32 * x32, axis=-1, keepdims=True) + EPS)
            return normed.astype(x.dtype) * weight
        B, L, D = X.shape
        H, d = q_norm_w.shape
        K = X.reshape(B, L, H, d)
        Q = rms_norm_multihead((X @ Wq.T).reshape(B, L, H, d), q_norm_w)
        V = rms_norm_multihead((X @ Wv.T).reshape(B, L, H, d), v_norm_w)
        W = jnp.cumsum(jnp.einsum('blhd,blhe->blhde', K, V), axis=1)
        out = jnp.einsum('blhd,blhde->blhe', Q, W).reshape(B, L, D)
        return out

    def _L1_ffn_ref(hidden_states, router_w, router_b, w1, w2):
        import jax, jax.numpy as jnp
        import numpy as np
        B, S, DIM, FFN, E = (4, 256, 128, 512, 8)
        b, s, d = hidden_states.shape
        x = hidden_states.reshape(-1, d)
        logits = x @ router_w + router_b
        route = jax.nn.softmax(logits, axis=1)
        max_prob = jnp.max(route, axis=1, keepdims=True)
        max_ind = jnp.argmax(route, axis=1)
        out = jnp.zeros_like(x)
        num_experts = w1.shape[0]
        for e in range(num_experts):
            h = x @ w1[e]
            a, g = jnp.split(h, 2, axis=1)
            y = jax.nn.silu(a) * g @ w2[e]
            out = jnp.where((max_ind == e)[:, None], y, out)
        out = out * max_prob
        return out.reshape(b, s, d)
    x = x + _L0_xattn_ref(_layernorm(x, axis=-1), ctx_1024, ctx_1024, L0_xattn_ln_g, L0_xattn_ln_b, L0_xattn_w_in, L0_xattn_wp_w1, L0_xattn_wp_b1, L0_xattn_wp_ln_g, L0_xattn_wp_ln_b, L0_xattn_wp_w2, L0_xattn_wp_b2, L0_xattn_w_out, L0_xattn_b_out)
    x = x + _L0_attn_ref(_layernorm(x, axis=-1), L0_attn_Wq, L0_attn_bq, L0_attn_Wk, L0_attn_bk, L0_attn_Wv, L0_attn_bv, L0_attn_Wo, L0_attn_bo)
    x = x + _L0_ffn_ref(_layernorm(x, axis=-1), L0_ffn_router_w, L0_ffn_w1, L0_ffn_w2)
    x = x + _L1_xattn_ref(ctx_1024, ctx_1024, _layernorm(x, axis=-1), mask_Bx1xSxS2_ik1, L1_xattn_W_fc, L1_xattn_b_fc)
    x = x + _L1_attn_ref(_layernorm(x, axis=-1), L1_attn_Wq, L1_attn_Wv, L1_attn_q_norm_w, L1_attn_v_norm_w)
    x = x + _L1_ffn_ref(_layernorm(x, axis=-1), L1_ffn_router_w, L1_ffn_router_b, L1_ffn_w1, L1_ffn_w2)
    return x

_drawn_inputs = setup_inputs


def setup_inputs(seed=0):
    import zlib

    import numpy as np

    out = dict(_drawn_inputs(seed))
    spreads = {'L0_xattn_ln_g': (1.0, 0.2),
     'L0_xattn_ln_b': (0.0, 0.1),
     'L0_xattn_wp_b1': (0.0, 0.1),
     'L0_xattn_wp_ln_g': (1.0, 0.547),
     'L0_xattn_wp_ln_b': (0.0, 0.399),
     'L0_xattn_wp_b2': (0.0, 0.8),
     'L0_xattn_b_out': (0.0, 0.387),
     'L0_attn_bq': (0.0, 0.8),
     'L0_attn_bk': (0.0, 0.8),
     'L0_attn_bv': (0.0, 0.464),
     'L0_attn_bo': (0.0, 0.417),
     'L1_attn_q_norm_w': (1.0, 0.2),
     'L1_attn_v_norm_w': (1.0, 0.2),
     'L1_ffn_router_b': (0.0, 0.8)}
    factors = {'L0_ffn_router_w': 8.0,
     'L0_ffn_w1': 8.0,
     'L0_ffn_w2': 8.0,
     'L1_xattn_b_fc': 8.0,
     'L1_ffn_router_w': 8.0,
     'L1_ffn_w1': 8.0,
     'L1_ffn_w2': 8.0}
    for name, (base, spread) in spreads.items():
        noise = np.random.default_rng([zlib.crc32(name.encode()), seed]).standard_normal(out[name].shape)
        drawn = base * np.exp(spread * noise) if base else spread * noise
        out[name] = jnp.asarray(drawn.astype(out[name].dtype))
    for name, factor in factors.items():
        out[name] = (out[name] * factor).astype(out[name].dtype)
    return out
```

```python
from contextlib import ExitStack

import concourse.bass as bass
from concourse import mybir

ALU = mybir.AluOpType
ACT = mybir.ActivationFunctionType
AX = mybir.AxisListType
F32 = mybir.dt.float32
F32R = mybir.dt.float32r
BF16 = mybir.dt.bfloat16
I32 = mybir.dt.int32

P = 128
EPS = 1e-5
RMS_EPS = 1e-8
MASKED = -1e20
LOWEST = -3.0e38


ONCE = {
    "pool": ["consts", "ln0_rstd", "ln0b_rstd", "kp_ones", "q_inv", "wp_rstd", "ln1_rstd", "ln2_rstd", "ln3_rstd",
             "ln4_rstd", "rms_q_inv", "rms_v_inv", "ln5_rstd"],
    "act": ["xq_T", "cov_norm", "decorr", "wp_exp", "gauss", "ln1_T", "sc_exp", "pT", "oT", "ln2_T",
            "r0_exp", "xo_T", "ln4_T", "q1_T", "ln5_T", "r1_exp"],
    "dve": ["ln0_var", "ln0", "ln0b_var", "xq", "wbar", "q_ss", "qratio", "small_cp", "covsum", "meanx",
            "cov_ss", "feats", "wp_var", "h1", "h1T", "wp_logit", "coef8", "coef", "x1", "gauss_sq",
            "ln1_var", "ln1", "qk", "v0", "sc_max", "probs", "ln2_var", "ln2", "r0_max", "acc0", "x3",
            "ln3_var", "ln3", "qpack", "ln4_var", "ln4", "rms_q_ms", "rms_q", "rms_v_ms", "rms_v",
            "ln5_var", "ln5", "r1_max", "acc1", "x6"],
    "pe": ["xq_T_ps", "small_ps", "comb_ps", "cov_tot", "feats_ps", "h1_ps", "h1T_ps", "wp_ps", "coef_ps",
           "ln1_T_ps", "qk_ps", "v_ps", "sc_ps", "pT_ps", "oT_ps", "o0_ps", "ln2_T_ps", "r0_ps", "xo_T_ps",
           "fc_ps", "ln4_T_ps", "rms_q_ps", "rms_v_ps", "q1_T_ps", "ln5_T_ps", "r1_ps"],
}


FROM_ONE = {
    "pool": ["vaug"],
    "act": ["a_ev", "sq", "e0_T0", "e0_T1", "e0_h", "pexp"],
    "dve": ["k_row", "ssum", "msum", "t_ev", "e0_add0", "e0_add1", "e1_add0", "e1_add1", "e1_h", "ct_lo", "smx",
            "orow0", "orow1", "orow2", "orow3"],
    "pe": ["a_ps", "e0_y0", "e0_y1", "e1_y0", "e1_y1", "ct_ps", "pv", "st_ps", "st_unit0", "st_unit1", "st_unit2",
           "st_unit3"],
}


class Chain:

    def __init__(self, eng, sem):
        self.eng, self.sem, self.base, self.n = eng, sem, 0, 0

    def __call__(self, ins):
        self.n += 1
        ins.then_inc(self.sem, 1)
        self.eng.wait_ge(self.sem, self.base + self.n)

    def loop(self, i, per):
        self.start = self.base + self.n
        self.base, self.n, self.per = i * per + self.start, 0, per

    def end_loop(self, count):
        assert self.n == self.per, self.n
        self.base, self.n = self.start + count * self.per, 0


def perceiver_two_layers(nc, T, out):
    x_d, ctx_d, mask_d = T["x"], T["ctx_1024"], T["mask_Bx1xSxS2_ik1"]
    B, S, D = x_d.shape
    S2 = ctx_d.shape[1]
    assert S == P and D == P
    H = T["L0_xattn_w_in"].shape[0] // D
    KT = S2 // P
    NQ = 4
    QUADS = KT // NQ
    NH = T["L1_attn_q_norm_w"].shape[0]
    HD = D // NH
    G = 4
    HG = NH // G
    VC = HD + 1
    E = T["L0_ffn_router_w"].shape[0]
    FC = T["L0_ffn_w1"].shape[1] // P
    assert QUADS == 4 and G == 4 and HG == 4 and FC == 4 and H == 8 and B == 4

    ctx_stack = ExitStack()
    with ctx_stack as stack:
        def sb(name, shape, dt=F32):
            return stack.enter_context(nc.sbuf_tensor("sb_" + name, shape, dt))

        sems = {}

        def sem(name):
            if name not in sems:
                sems[name] = stack.enter_context(nc.semaphore("s_" + name))
            return sems[name]

        once = {}
        for who, names in ONCE.items():
            for n, name in enumerate(names):
                once[name] = (who, n + 1)
        from_one = {name for names in FROM_ONE.values() for name in names}

        def start(eng, who):
            for name in FROM_ONE[who]:
                eng.sem_inc(sem(name), 1)

        given = {who: 0 for who in ONCE}

        def at(name, value=1):
            if name in once:
                who, n = once[name]
                return sem(who + "_once"), n
            return sem(name), value + (name in from_one)

        def mark(name):
            if name not in once:
                return sem(name)
            who, n = once[name]
            given[who] += 1
            assert given[who] == n, (name, n, given[who])
            return sem(who + "_once")

        PS = stack.enter_context(nc.psum_tensor("banks", [P, 8, 512], F32))

        ident = sb("ident", [P, P])
        identb = sb("identb", [P, P], BF16)
        offdiag = sb("offdiag", [P, P])
        ones = sb("ones", [P, P])
        neghalf = sb("neghalf", [P, B * NH])
        groupmask = sb("groupmask", [P, HG])
        headmask = sb("headmask", [P, NH])
        causal = sb("causal", [P, P])
        lastfirst = sb("lastfirst", [P, E])
        gauss = sb("gauss", [P, S])

        W_IN, W_OUT, WQ, WK, WV, WO, WFC, WQ1, WV1, WP1, NW = 0, H, 2 * H, 2 * H + 1, 2 * H + 2, 2 * H + 3, \
            2 * H + 4, 2 * H + 5, 2 * H + 6, 2 * H + 7, 2 * H + 9
        w = sb("w", [P, NW, P])
        wT = sb("wT", [P, NW, P])
        small = sb("small", [32, 2, P])
        rwT = sb("rwT", [P, E])
        wp2T = sb("wp2T", [P, 3])
        rw1 = sb("rw1", [P, E])
        wbar = sb("wbar", [P, H])
        G_, B_, BOUT, BV, BO, BFC, QW, VW, WPB1, WPG, WPB, NB = range(12)
        rows = sb("rows", [P, NB, P])
        wpb2 = sb("wpb2", [P, 3])
        rb1 = sb("rb1", [P, E])
        bcol = sb("bcol", [P, 2])

        xs = sb("xs", [P, B, D])
        xn = sb("xn", [P, B, D])
        xnT = sb("xnT", [P, B * S])
        stats = sb("stats", [P, B, 6])
        mv = sb("mv", [P, B, 2])
        vpe = sb("vpe", [P, B])
        rstd = sb("rstd", [P, B])

        vaug = sb("vaug", [P, G, KT, HG, VC])
        ctxT_hi = sb("ctxT_hi", [P, S2], F32R)
        ctxT_lo = sb("ctxT_lo", [P, S2], F32R)
        kp = sb("kp", [P, G, S2], F32R)
        a_all = sb("a_all", [P, B, H * D])
        maskb = a_all[:, :, :].rearrange("p b n -> p (b n)").bitcast(BF16) \
            .rearrange("p (b n) -> p b n", b=B)
        mnow = sb("mnow", [P, S2], BF16)
        mnext = sb("mnext", [P, S2], BF16)
        maskT = sb("maskT", [P, B * KT, S], BF16)

        arena = sb("arena", [P, 12288])
        used = [0]

        def view(shape, dims=None):
            n = 1
            for s in shape:
                n *= s
            a = arena[:, used[0]:used[0] + n]
            used[0] += n
            assert used[0] <= 12288, used[0]
            if len(shape) == 2:
                a = a.rearrange("p (a b) -> p a b", b=shape[1])
            if len(shape) == 3:
                a = a.rearrange("p (a b c) -> p a b c", b=shape[1], c=shape[2])
            return a

        t_all = sb("t_all", [P, B, H + 1])

        mask_i = arena[:, 2 * S2:4 * S2].bitcast(I32).rearrange("p (a n) -> p a n", a=2)
        used[0] = 0
        cx = view([KT, D])
        X = view([KT, D])
        XT = view([2, NQ * P])
        sq = view([2, H * D])
        Y = view([NQ, H * D])
        kst = sb("kst", [P, NQ, 6])
        kmv = sb("kmv", [P, NQ, 2])
        kvpe = sb("kvpe", [P, NQ])
        krstd = sb("krstd", [P, NQ])
        ss = sb("ss", [P, NQ, H])
        kw = sb("kw", [P, NQ, H])
        msum = sb("msum", [P, NQ, H])
        kt1 = sb("kt1", [P, NQ, H])
        kt2 = sb("kt2", [P, NQ, H])
        kr = sb("kr", [P, NQ, H + 1])
        used[0] = 0
        fq = view([B, H * D])
        fqT = view([H, B * S])
        sqb = view([H * D])
        zt = view([2, B * S])
        tmpU = view([2, B * S])
        qsum = sb("qsum", [P, B * H])
        qss = sb("qss", [P, B * H])
        qinv = sb("qinv", [P, B * H])
        qratio = sb("qratio", [P, B * H])
        q1 = sb("q1", [P, B * H])
        q2 = sb("q2", [P, B * H])
        covsum = sb("covsum", [P, H])
        meanx = sb("meanx", [P, 2])
        feats = sb("feats", [P, 2 * H])
        h8 = sb("h8", [8, 3, P])
        h8s = sb("h8s", [8, 6])
        h8m = sb("h8m", [8, 2])
        h8r = sb("h8r", [8, 2])
        h1T = sb("h1T", [P, H])
        sm8 = sb("sm8", [8, 16])
        coef = sb("coef", [P, 2 * H])
        wt_t = sb("wt_t", [P, B, H])
        comb = view([H, D])
        used[0] = 0
        qT = view([B * S])
        kT = view([B * S])
        vv = view([B, D])
        sc = view([B, S])
        pT = view([B * S])
        oT = view([B * S])
        used[0] = 0
        q1r = view([B, D])
        v1r = view([B, D])
        t1r = view([B, D])
        xT1 = view([B * S])
        qT1 = view([B * S])
        qbd = view([NH, S])
        sT1 = view([2, NH * S])
        used[0] = 0
        raw1 = view([2, FC * P])
        raw2 = view([2, FC * P])
        w1T = view([2, FC * P])
        w2T = view([2, FC * P])
        hT = view([2, FC * B * S])
        acc = view([B * D])
        ytmp = view([B * D])
        sil = view([2, B * S])
        wide1 = arena[:, 0:4 * FC * P].rearrange("p (a n) -> p a n", a=2)
        warm = sb("warm", [P, 3])
        gate = sb("gate", [P, 4 + G])
        mx = sb("mx", [P, 2 * HG])
        s4 = sb("s4", [P, B])
        r4 = sb("r4", [P, B])
        lg = sb("lg", [P, B, E])
        pr = sb("pr", [P, B, E])
        oh = sb("oh", [P, B, E])
        oh2 = sb("oh2", [P, B, E])
        wgt = sb("wgt", [P, E, B])
        used[0] = 0
        pexp = view([2, 2 * HG * S])
        junk = view([1024])
        qpack = view([G * B, P])
        qTall = view([G * B, S])
        nm = view([P])
        qs2 = view([P])
        q_one = view([B * D])
        cx2 = view([KT, D])
        orow = view([B, D])
        rec4 = sb("rec4", [P, HG])
        nmax = sb("nmax", [P, HG])
        q_ms = sb("q_ms", [P, B * NH])
        q_rms = sb("q_rms", [P, B * NH])
        qp1 = sb("qp1", [P, 2, HG * S], F32R)
        qp2 = sb("qp2", [P, 2, HG * S], F32R)

        block = stack.enter_context(nc.Block())

        def bc(ap, shape):
            return ap.to_broadcast(shape)

        LNS = ["ln0", "ln0b", "ln1", "ln2", "ln3", "ln4", "ln5"]
        ROUTED = ["r0", "r1"]

        def row_of(name):
            return T[name].rearrange("(a n) -> a n", a=1)

        @block.sync
        def _(sp):
            sp.dma_start(xs[:, :, :], x_d.rearrange("b s d -> s b d")).then_inc(mark("x_in"), 16)
            sp.dma_start(w[:, W_IN:W_IN + H, :], T["L0_xattn_w_in"].rearrange("(h d) n -> d h n", h=H)) \
                .then_inc(mark("w_in"), 16)
            with sp.Fori(0, B) as b:
                sp.wait_ge(*at("k_row", b * QUADS))
                for c in range(QUADS):
                    sp.dma_start(cx[:, c * NQ:(c + 1) * NQ, :],
                                 ctx_d[bass.ds(b, 1), c * NQ * P:(c + 1) * NQ * P, :]
                                 .rearrange("a (t p) d -> p (a t) d", p=P)).then_inc(mark("ctx%d" % c), 16)
            sp.wait_ge(*at("x1"))
            for b in range(B):
                if b >= 2:
                    sp.wait_ge(*at("maskb", b - 1))
                sp.dma_start(mask_i[:, b % 2, :], mask_d[b, 0, :, :]).then_inc(mark("mask%d" % b), 16)
            sp.wait_ge(*at("r0_max"))
            with sp.Fori(0, E // 2) as i:
                for p in range(2):
                    sp.wait_ge(*at("e0_T%d" % p, i * 2))
                    sp.dma_start(raw1[:, p, :].rearrange("p (c d) -> p c d", c=FC),
                                 T["L0_ffn_w1"][bass.ds(i * 2 + p, 1), :, :]
                                 .rearrange("a (c p) d -> p (a c) d", p=P)).then_inc(mark("w1_0_%d" % p), 16)
                    sp.dma_start(raw2[:, p, :], T["L0_ffn_w2"][bass.ds(i * 2 + p, 1), :, :]
                                 .rearrange("a d n -> d (a n)")).then_inc(mark("w2_0_%d" % p), 16)
            sp.wait_ge(*at("x3"))
            sp.wait_ge(*at("kp_ones"))
            with sp.Fori(1, B + 1) as b1:
                b = b1 - 1
                sp.wait_ge(*at("ct_ps", b * QUADS))
                sp.wait_ge(*at("vaug", b * G))
                for c in range(QUADS):
                    sp.dma_start(cx2[:, c * NQ:(c + 1) * NQ, :],
                                 ctx_d[bass.ds(b, 1), c * NQ * P:(c + 1) * NQ * P, :]
                                 .rearrange("a (t p) d -> p (a t) d", p=P)).then_inc(mark("cx2"), 16)
                sp.wait_ge(*at("ct_lo", b1 * QUADS))
                for g in range(G):
                    sp.wait_ge(*at("st_unit%d" % g, b1 - 1))
                    for j in range(HG):
                        for t, src in enumerate((ctxT_hi, ctxT_hi, ctxT_lo)):
                            r = 32 * j + 2 + HD * t
                            k0 = (HG * g + j) * HD
                            sp.dma_start(kp[r:r + HD, g, :].bitcast(F32), src[k0:k0 + HD, :].bitcast(F32)) \
                                .then_inc(mark("kp%d" % g), 16)
            sp.wait_ge(*at("r1_max"))
            with sp.Fori(0, E // 2) as i:
                for p in range(2):
                    sp.wait_ge(*at("e1_y%d" % p, i))
                    sp.dma_start(wide1[:, p, :], T["L1_ffn_w1"][bass.ds(i * 2 + p, 1), :, :]
                                 .rearrange("a d n -> d (a n)")).then_inc(mark("w1_1_%d" % p), 16)
                    sp.dma_start(w2T[:, p, :].rearrange("p (c d) -> p c d", c=FC),
                                 T["L1_ffn_w2"][bass.ds(i * 2 + p, 1), :, :]
                                 .rearrange("a (c p) d -> p (a c) d", p=P)).then_inc(mark("w2_1_%d" % p), 16)
            sp.wait_ge(*at("x6"))
            sp.dma_start(out.rearrange("b s d -> s b d"), xs[:, :, :]).then_inc(mark("out"), 16)
            sp.wait_ge(*at("out", 16))

        @block.gpsimd
        def _(pool):
            start(pool, "pool")
            ch = Chain(pool, sem("pool_chain"))
            ch(pool.memset(ident[:, :], 0.0))
            pool.memset(offdiag[:, :], 1.0)
            pool.memset(neghalf[:, :], -0.5)
            pool.memset(ones[:, :], 1.0)
            pool.memset(headmask[:, :], 1.0)
            pool.memset(groupmask[:, :], 0.0)
            ch(pool.memset(causal[:, :], 1.0))
            ch(pool.affine_select(out=ident[:, :], in_=ident[:, :], compare_op=ALU.not_equal, fill=1.0,
                                  base=0, pattern=[[-1, P]], channel_multiplier=1))
            pool.affine_select(out=offdiag[:, :], in_=offdiag[:, :], compare_op=ALU.not_equal, fill=0.0,
                               base=0, pattern=[[-1, P]], channel_multiplier=1)
            pool.affine_select(out=causal[:, :], in_=causal[:, :], compare_op=ALU.is_ge, fill=0.0,
                               base=0, pattern=[[1, P]], channel_multiplier=-1)
            ch(pool.affine_select(out=headmask[:, :], in_=headmask[:, :], compare_op=ALU.is_ge, fill=0.0,
                                  base=0, pattern=[[-HD, NH]], channel_multiplier=1))
            ch(pool.affine_select(out=headmask[:, :], in_=headmask[:, :], compare_op=ALU.is_ge, fill=0.0,
                                  base=HD - 1, pattern=[[HD, NH]], channel_multiplier=-1))
            for j in range(HG):
                ch(pool.memset(groupmask[32 * j:32 * j + 32, j:j + 1], 1.0))
            pool.iota(lastfirst[:, :], pattern=[[-1, E]], base=E, channel_multiplier=0,
                      allow_small_or_imprecise_dtypes=True)
            ch(pool.iota(gauss[:, :], pattern=[[1, S]], base=-(S // 2), channel_multiplier=0,
                         allow_small_or_imprecise_dtypes=True))
            pool.tensor_copy(identb[:, :], ident[:, :]).then_inc(mark("consts"), 1)
            ch(pool.memset(vaug[:, :, :, :, :], 1.0))

            def rstd_of(name):
                pool.wait_ge(*at(name + "_var"))
                pool.tensor_tensor(rstd[:, :], vpe[:, :], neghalf[:, 0:B], ALU.pow) \
                    .then_inc(mark(name + "_rstd"), 1)

            rstd_of("ln0")
            rstd_of("ln0b")
            pool.wait_ge(*at("rows_in", 16 * NB))

            def ctx_rows(G0, c):
                pool.wait_ge(*at("k_var", G0 + 1))
                pool.tensor_tensor(krstd[:, :], kvpe[:, :], neghalf[:, 0:NQ], ALU.pow).then_inc(mark("k_rstd"), 1)
                pool.wait_ge(*at("k_row", G0 + 1))
                xq = X[:, c * NQ:(c + 1) * NQ, :]
                ch(pool.tensor_tensor(xq, xq, bc(rows[:, G_:G_ + 1, :], [P, NQ, D]), ALU.mult))
                pool.tensor_tensor(xq, xq, bc(rows[:, B_:B_ + 1, :], [P, NQ, D]), ALU.add) \
                    .then_inc(mark("k_x"), 1)

            with pool.Fori(0, B) as b:
                ch.loop(b, QUADS)
                ctx_rows(b * QUADS, 0)
                for c in range(QUADS):
                    if c + 1 < QUADS:
                        ctx_rows(b * QUADS + (c + 1), c + 1)
                    pool.wait_ge(*at("k_ss", b * QUADS + (c + 1)))
                    pool.tensor_tensor(kw[:, :, :], ss[:, :, :],
                                       neghalf[:, 0:NQ * H].rearrange("p (a b) -> p a b", a=NQ), ALU.pow) \
                        .then_inc(mark("k_w"), 1)
                ch.end_loop(B)
            ch(pool.memset(kp[:, :, :].bitcast(F32), 0.0))
            for j in range(HG - 1):
                ch(pool.memset(kp[32 * j:32 * j + 2, :, :].bitcast(F32), 1.0))
            pool.memset(kp[96:98, :, :].bitcast(F32), 1.0).then_inc(mark("kp_ones"), 1)
            pool.wait_ge(*at("kp_ones"))
            pool.wait_ge(*at("q_ss"))
            pool.tensor_tensor(qinv[:, :], qss[:, :], neghalf[:, 0:B * H], ALU.pow).then_inc(mark("q_inv"), 1)
            pool.wait_ge(*at("wp_var"))
            pool.tensor_tensor(h8r[:, 0:1], h8m[:, 1:2], neghalf[0:8, 0:1], ALU.pow).then_inc(mark("wp_rstd"), 1)
            for name in ("ln1", "ln2", "ln3"):
                rstd_of(name)
            pool.wait_ge(*at("maskb", B))

            def values(b, g):
                pool.wait_ge(*at("orow%d" % g, b))
                pool.tensor_tensor(gate[:, 2 + g:3 + g], neghalf[:, 0:1], neghalf[:, 0:1], ALU.add)
                for j in range(HG):
                    k0 = (g * HG + j) * HD
                    ins = pool.tensor_copy(vaug[:, g, :, j, 0:HD], cx2[:, :, k0:k0 + HD])
                ins.then_inc(mark("vaug"), 1)

            gate_of = {"mnow": 2 + G, "mnext": 3 + G}

            def mask_of(dst, b, b_dyn, maxima, done):
                pool.wait_ge(*at("smx", maxima))
                pool.tensor_tensor(gate[:, gate_of[done]:gate_of[done] + 1], neghalf[:, 0:1], neghalf[:, 0:1], ALU.add)
                pool.tensor_copy(dst[:, :], maskb[:, bass.ds(b_dyn, 1), :].rearrange("p a n -> p (a n)")) \
                    .then_inc(mark(done), 1)

            def feed(b, last):
                pool.wait_ge(*at("cx2", b * (16 * QUADS) + 16 * QUADS))
                for g in range(G - 1):
                    values(b, g)
                mask_of(mnow, b, b, b * (G * 2 * HG), "mnow")
                values(b, G - 1)
                if not last:
                    mask_of(mnext, b, b + 1, b * (G * 2 * HG) + 2 * HG, "mnext")

            with pool.Fori(0, B - 1) as b:
                feed(b, False)
            feed(B - 1, True)
            rstd_of("ln4")
            for name in ("rms_q", "rms_v"):
                pool.wait_ge(*at(name + "_ms"))
                pool.tensor_tensor(q_rms[:, :], q_ms[:, :], neghalf[:, 0:B * NH], ALU.pow) \
                    .then_inc(mark(name + "_inv"), 1)
            rstd_of("ln5")

        @block.scalar
        def _(act):
            start(act, "act")
            act.dma_start(w[:, W_OUT:W_OUT + H, :], T["L0_xattn_w_out"].rearrange("n (h d) -> n h d", h=H)) \
                .then_inc(mark("w_all"), 16)
            for n, name in ((WQ, "L0_attn_Wq"), (WK, "L0_attn_Wk"), (WV, "L0_attn_Wv"), (WO, "L0_attn_Wo"),
                            (WFC, "L1_xattn_W_fc"), (WQ1, "L1_attn_Wq"), (WV1, "L1_attn_Wv")):
                act.dma_start(w[:, n, :], T[name]).then_inc(mark("w_all"), 16)
            act.dma_start(w[:, WP1:WP1 + 2, :], T["L0_xattn_wp_w1"].rearrange("n (a d) -> n a d", a=2)) \
                .then_inc(mark("w_all"), 16)
            act.dma_start(small[0:E, 0, :], T["L0_ffn_router_w"]).then_inc(mark("w_all"), 16)
            act.dma_start(small[0:3, 1, :], T["L0_xattn_wp_w2"]).then_inc(mark("w_all"), 16)
            act.dma_start(rw1[:, :], T["L1_ffn_router_w"]).then_inc(mark("w_all"), 16)
            for n, name in ((G_, "L0_xattn_ln_g"), (B_, "L0_xattn_ln_b"), (BOUT, "L0_xattn_b_out"),
                            (BV, "L0_attn_bv"), (BO, "L0_attn_bo"), (BFC, "L1_xattn_b_fc"),
                            (WPB1, "L0_xattn_wp_b1"), (WPG, "L0_xattn_wp_ln_g"), (WPB, "L0_xattn_wp_ln_b")):
                act.dma_start(rows[:, n, :], row_of(name).to_broadcast([P, P])).then_inc(mark("rows_in"), 16)
            for n, name in ((QW, "L1_attn_q_norm_w"), (VW, "L1_attn_v_norm_w")):
                act.dma_start(rows[:, n, :], T[name].rearrange("(a h) d -> a (h d)", a=1).to_broadcast([P, P])) \
                    .then_inc(mark("rows_in"), 16)
            act.dma_start(wpb2[:, :], row_of("L0_xattn_wp_b2").to_broadcast([P, 3])).then_inc(mark("w_all"), 16)
            act.dma_start(rb1[:, :], row_of("L1_ffn_router_b").to_broadcast([P, E])).then_inc(mark("w_all"), 16)
            with nc.allow_non_contiguous_dma(reason="two bias vectors, one element a partition"):
                for n, name in enumerate(("L0_attn_bq", "L0_attn_bk")):
                    act.dma_start(bcol[:, n:n + 1], T[name].rearrange("(n a) -> n a", a=1)) \
                        .then_inc(mark("w_all"), 16)

            def copy(dst, src, wait, value, done):
                act.wait_ge(*at(wait, value))
                act.activation(dst, src, ACT.Copy).then_inc(mark(done), 1)

            for k in range(2):
                copy(wT[:, 4 * k:4 * k + 4, :], PS[:, k, :].rearrange("p (a n) -> p a n", a=4),
                     "wT_ps", k + 1, "wT")
            def xt(G0, c):
                act.wait_ge(*at("xt_ps", G0 + 1))
                act.activation(XT[:, c % 2, :], PS[:, 0, :], ACT.Copy).then_inc(mark("xt"), 1)

            with act.Fori(0, B) as b:
                xt(b * QUADS, 0)
                for c in range(QUADS):
                    for j in range(NQ):
                        t = c * NQ + j
                        act.wait_ge(*at("f_ps", b * KT + (t + 1)))
                        act.wait_ge(*at("ssum", b * KT + max(t - 1, 0)))
                        act.activation(sq[:, t % 2, :], PS[:, 1 + 2 * (t % 2):3 + 2 * (t % 2), :]
                                       .rearrange("p a n -> p (a n)"), ACT.Square).then_inc(mark("sq"), 1)
                        if j == 2 and c + 1 < QUADS:
                            xt(b * QUADS + (c + 1), c + 1)
                act.wait_ge(*at("a_ps", b * KT + KT))
                act.activation(a_all[:, bass.ds(b, 1), :].rearrange("p a n -> p (a n)"),
                               PS[:, 5:7, :].rearrange("p a n -> p (a n)"), ACT.Copy).then_inc(mark("a_ev"), 1)

            for k in range(2, 7):
                m = min(4, NW - 4 * k)
                copy(wT[:, 4 * k:4 * k + m, :], PS[:, k % 2, 0:m * P].rearrange("p (a n) -> p a n", a=m),
                     "wT_ps", k + 1, "wT")
            copy(xnT[:, :], PS[:, 2, :], "xq_T_ps", 1, "xq_T")
            for b in range(B):
                copy(fq[:, b, :], PS[:, 4 + 2 * (b % 2):6 + 2 * (b % 2), :].rearrange("p a n -> p (a n)"),
                     "fq_ps", b + 1, "fq")
            for h in range(H):
                copy(fqT[:, h, :], PS[:, h % 2, :], "fqT_ps", h + 1, "fqT")
            copy(comb[:, 0:4, :], PS[:, 4, :].rearrange("p (a n) -> p a n", a=4), "comb_ps", 1, "comb")
            copy(comb[:, 4:8, :], PS[:, 5, :].rearrange("p (a n) -> p a n", a=4), "comb_ps", 1, "comb")
            act.wait_ge(*at("cov_ss"))
            act.activation(sm8[:, 2:3], sm8[:, 0:1], ACT.Sqrt).then_inc(mark("cov_norm"), 1)
            act.wait_ge(*at("cov_norm"))
            act.activation(sm8[:, 3:4], sm8[:, 2:3], ACT.Exp, scale=-5.0 / (D * D) / (B * S)) \
                .then_inc(mark("decorr"), 1)
            act.wait_ge(*at("wp_logit"))
            act.activation(sm8[:, 8:11], sm8[:, 4:7], ACT.Exp).then_inc(mark("wp_exp"), 1)
            for h in range(H):
                copy(zt[:, h % 2, :], PS[:, 2 + h % 2, :], "zt_ps", h + 1, "zt")

            for n in range(B * KT // 8):
                copy(maskT[:, 8 * n:8 * n + 8, :],
                     PS[:, 6 + n % 2, :].bitcast(BF16).rearrange("p (a n) -> p a n", a=8),
                     "maskT_ps", n + 1, "maskT")

            act.wait_ge(*at("gauss_sq"))
            act.activation(gauss[:, :], gauss[:, :], ACT.Exp, scale=-0.5).then_inc(mark("gauss"), 1)
            copy(xnT[:, :], PS[:, 0, :], "ln1_T_ps", 1, "ln1_T")
            act.wait_ge(*at("sc_max"))
            act.activation(sc[:, :, :], sc[:, :, :], ACT.Exp).then_inc(mark("sc_exp"), 1)
            copy(pT[:, :], PS[:, 0, :], "pT_ps", 1, "pT")
            copy(oT[:, :], PS[:, 1, :], "oT_ps", 1, "oT")

            copy(xnT[:, :], PS[:, 0, :], "ln2_T_ps", 1, "ln2_T")
            act.wait_ge(*at("r0_max"))
            act.activation(pr[:, :, :], lg[:, :, :], ACT.Exp).then_inc(mark("r0_exp"), 1)

            act.activation(warm[:, 0:1], ones[:, 0:1], ACT.Gelu)
            with act.Fori(0, E // 2) as i:
                for p in range(2):
                    act.wait_ge(*at("e0_y%d" % p, i))
                    act.wait_ge(*at("e0_T_ps", i * 4 + (2 * p + 1)))
                    act.activation(w1T[:, p, :], PS[:, 0, :], ACT.Copy).then_inc(mark("e0_T%d" % p), 1)
                    act.wait_ge(*at("e0_T_ps", i * 4 + (2 * p + 2)))
                    act.activation(w2T[:, p, :], PS[:, 1, :], ACT.Copy).then_inc(mark("e0_T%d" % p), 1)
                    for c in range(FC):
                        act.wait_ge(*at("e0_h_ps", i * 2 * FC + (p * FC + c + 1)))
                        act.activation(hT[:, p, c * B * S:(c + 1) * B * S], PS[:, 2 + c, :], ACT.Gelu) \
                            .then_inc(mark("e0_h"), 1)

            copy(qTall[:, 0:4, :], PS[:, 0, :].rearrange("p (a n) -> p a n", a=4), "qTall_ps", 1, "qTall")
            for k in range(1, 4):
                copy(qTall[:, 4 * k:4 * k + 4, :], PS[:, k, :].rearrange("p (a n) -> p a n", a=4),
                     "qTall_ps", k + 1, "qTall")
            act.activation(warm[:, 1:2], ones[:, 0:1], ACT.Exp)

            def key_hi(b, n):
                if n == 0:
                    for g in range(G):
                        act.wait_ge(*at("kp%d" % g, b * (16 * 3 * HG)))
                act.wait_ge(*at("ct_ps", b * QUADS + (n + 1)))
                act.activation(ctxT_hi[:, n * NQ * P:(n + 1) * NQ * P], PS[:, 4, :], ACT.Copy) \
                    .then_inc(mark("ct_hi"), 1)

            def exps(b, g, keys_follow):
                for n in range(KT // 2):
                    N0 = g * KT // 2 + n
                    act.wait_ge(*at("st_ps", b * (G * KT // 2) + (N0 + 1)))
                    act.wait_ge(*at("pv", b * (G * KT // 2) + max(N0 - 1, 0)))
                    act.activation(pexp[:, n % 2, :], PS[:, 2 * (n % 2):2 * (n % 2) + 2, :]
                                   .rearrange("p a n -> p (a n)"), ACT.Exp, scale=float(D) ** -0.5) \
                        .then_inc(mark("pexp"), 1)
                    if keys_follow and n < QUADS:
                        key_hi(b + 1, n)

            for n in range(QUADS):
                key_hi(0, n)
            with act.Fori(0, B - 1) as b:
                for g in range(G):
                    exps(b, g, g == 1)
            for g in range(G):
                exps(B - 1, g, False)
            copy(oT[:, :], PS[:, 0, :], "xo_T_ps", 1, "xo_T")

            copy(xT1[:, :], PS[:, 0, :], "ln4_T_ps", 1, "ln4_T")
            copy(qT1[:, :], PS[:, 3, :], "q1_T_ps", 1, "q1_T")

            copy(xnT[:, :], PS[:, 0, :], "ln5_T_ps", 1, "ln5_T")
            act.wait_ge(*at("r1_max"))
            act.activation(pr[:, :, :], lg[:, :, :], ACT.Exp).then_inc(mark("r1_exp"), 1)
            act.activation(warm[:, 2:3], ones[:, 0:1], ACT.Silu)
            with act.Fori(0, E // 2) as i:
                for p in range(2):
                    for c in range(FC):
                        n = p * FC + c
                        act.wait_ge(*at("e1_h_ps", i * 2 * FC + (n + 1)))
                        act.wait_ge(*at("e1_h", i * 2 * FC + max(n - 1, 0)))
                        act.activation(sil[:, c % 2, :], PS[:, 2 * (c % 2), :], ACT.Silu).then_inc(mark("e1_sil"), 1)

        @block.vector
        def _(dve):
            start(dve, "dve")
            ch = Chain(dve, sem("dve_chain"))

            def layer_norm_stats(src, name):
                for b in range(B):
                    ins = dve.bn_stats(stats[:, b, :], src[:, b, :])
                ch(ins)
                for b in range(B):
                    ins = dve.bn_aggr(mv[:, b, :], stats[:, b, :])
                ch(ins)
                dve.tensor_scalar(vpe[:, :], mv[:, :, 1], EPS, None, ALU.add).then_inc(mark(name + "_var"), 1)

            def layer_norm(src, dst, name):
                layer_norm_stats(src, name)
                dve.wait_ge(*at(name + "_rstd"))
                for b in range(B):
                    ins = dve.tensor_scalar(dst[:, b, :], src[:, b, :], mv[:, b, 0:1], rstd[:, b:b + 1],
                                            ALU.subtract, ALU.mult)
                ins.then_inc(mark(name), 1)
                dve.wait_ge(*at(name))

            dve.wait_ge(*at("x_in", 16))
            layer_norm(xs, xn, "ln0")
            layer_norm_stats(xn, "ln0b")
            dve.wait_ge(*at("ln0b_rstd"))
            dve.wait_ge(*at("rows_in", 16 * NB))
            for b in range(B):
                ins = dve.tensor_scalar(xn[:, b, :], xn[:, b, :], mv[:, b, 0:1], rstd[:, b:b + 1],
                                        ALU.subtract, ALU.mult)
            ch(ins)
            ch(dve.tensor_tensor(xn[:, :, :], xn[:, :, :], bc(rows[:, G_:G_ + 1, :], [P, B, D]), ALU.mult))
            dve.tensor_tensor(xn[:, :, :], xn[:, :, :], bc(rows[:, B_:B_ + 1, :], [P, B, D]), ALU.add) \
                .then_inc(mark("xq"), 1)
            dve.wait_ge(*at("wT", 2))
            dve.tensor_reduce(out=wbar[:, :], in_=wT[:, W_IN:W_IN + H, :], axis=AX.X, op=ALU.add) \
                .then_inc(mark("wbar"), 1)
            ch(dve.memset(kr[:, :, H:H + 1], 1.0))

            def norm_stats(b, G0, c):
                dve.wait_ge(*at("ctx%d" % c, b * 16 + 16))
                for j in range(NQ):
                    ins = dve.bn_stats(kst[:, j, :], cx[:, c * NQ + j, :])
                ch(ins)
                dve.memset(gate[:, 0:1], 0.0)
                for j in range(NQ):
                    ins = dve.bn_aggr(kmv[:, j, :], kst[:, j, :])
                ch(ins)
                dve.tensor_scalar(kvpe[:, :], kmv[:, :, 1], EPS, None, ALU.add).then_inc(mark("k_var"), 1)

            def norm_rows(b, G0, c):
                dve.wait_ge(*at("k_rstd", G0 + 1))
                dve.wait_ge(*at("a_ps", b * KT))
                for j in range(NQ):
                    ins = dve.tensor_scalar(X[:, c * NQ + j, :], cx[:, c * NQ + j, :], kmv[:, j, 0:1],
                                            krstd[:, j:j + 1], ALU.subtract, ALU.mult)
                ins.then_inc(mark("k_row"), 1)

            def sum_squares(b, c, j):
                t = c * NQ + j
                dve.wait_ge(*at("sq", b * KT + (t + 1)))
                dve.tensor_reduce(out=ss[:, j, :], in_=sq[:, t % 2, :].rearrange("p (h d) -> p h d", h=H),
                                  axis=AX.X, op=ALU.add).then_inc(mark("ssum"), 1)

            with dve.Fori(0, B) as b:
                ch.loop(b, QUADS * 7)
                norm_stats(b, b * QUADS, 0)
                norm_rows(b, b * QUADS, 0)
                for c in range(QUADS):
                    G0 = b * QUADS + c
                    sum_squares(b, c, 0)
                    sum_squares(b, c, 1)
                    dve.wait_ge(*at("mean_ps", G0 + 1))
                    dve.tensor_copy(msum[:, :, :], PS[:, 0, 0:NQ * H].rearrange("p (a h) -> p a h", a=NQ)) \
                        .then_inc(mark("msum"), 1)
                    if c + 1 < QUADS:
                        norm_stats(b, b * QUADS + (c + 1), c + 1)
                    sum_squares(b, c, 2)
                    if c + 1 < QUADS:
                        norm_rows(b, b * QUADS + (c + 1), c + 1)
                    sum_squares(b, c, 3)
                    dve.wait_ge(*at("ssum", b * KT + (c + 1) * NQ))
                    dve.wait_ge(*at("msum", G0 + 1))
                    dve.tensor_tensor(kt1[:, :, :], msum[:, :, :], msum[:, :, :], ALU.mult) \
                        .then_inc(mark("k_ss"), 1)
                    dve.wait_ge(*at("k_ss", G0 + 1))
                    ch(dve.scalar_tensor_tensor(kt2[:, :, :], kt1[:, :, :], -1.0 / D, ss[:, :, :],
                                                ALU.mult, ALU.add))
                    ch(dve.tensor_scalar(kt2[:, :, :], kt2[:, :, :], 1.0 / (D - 1), None, ALU.mult))
                    ch(dve.tensor_scalar(kt1[:, :, :], kt2[:, :, :], 1.0, None, ALU.add))
                    ch(dve.reciprocal(kt1[:, :, :], kt1[:, :, :]))
                    ch(dve.tensor_scalar(kt2[:, :, :], kt2[:, :, :], 1.0, 2.0, ALU.min, ALU.mult))
                    dve.wait_ge(*at("a_ps", b * KT + c * NQ))
                    dve.tensor_tensor(kr[:, :, 0:H], kt2[:, :, :], kt1[:, :, :], ALU.mult) \
                        .then_inc(mark("kr"), 1)
                    dve.wait_ge(*at("k_w", G0 + 1))
                    dve.wait_ge(*at("k_x", G0 + 1))
                    for j in range(NQ):
                        dve.tensor_tensor(Y[:, j, :].rearrange("p (h d) -> p h d", h=H),
                                          bc(X[:, c * NQ + j:c * NQ + j + 1, :], [P, H, D]),
                                          bc(kw[:, j, :].unsqueeze(2), [P, H, D]), ALU.mult) \
                            .then_inc(mark("y"), 1)
                dve.wait_ge(*at("a_ps", b * KT + KT))
                dve.tensor_copy(t_all[:, bass.ds(b, 1), :].rearrange("p a n -> p (a n)"), PS[:, 7, 0:H + 1]) \
                    .then_inc(mark("t_ev"), 1)
                ch.end_loop(B)
            dve.wait_ge(*at("t_ev", B))

            for b in range(B):
                hs = slice(b * H, b * H + H)
                fb = fq[:, b, :].rearrange("p (h d) -> p h d", h=H)
                dve.wait_ge(*at("fq", b + 1))
                dve.tensor_reduce(out=qsum[:, hs], in_=fb, axis=AX.X, op=ALU.add)
                ch(dve.tensor_tensor(sqb[:, :], fq[:, b, :], fq[:, b, :], ALU.mult))
                ch(dve.tensor_reduce(out=qss[:, hs], in_=sqb[:, :].rearrange("p (h d) -> p h d", h=H),
                                     axis=AX.X, op=ALU.add))
            ch(dve.tensor_scalar(q1[:, :], qsum[:, :], 1.0 / D, None, ALU.mult))
            dve.tensor_tensor(q2[:, :], q1[:, :], qsum[:, :], ALU.mult).then_inc(mark("q_ss"), 1)
            dve.wait_ge(*at("q_ss"))
            ch(dve.tensor_tensor(q2[:, :], qss[:, :], q2[:, :], ALU.subtract))
            ch(dve.tensor_scalar(q2[:, :], q2[:, :], 1.0 / (D - 1), None, ALU.mult))
            ch(dve.tensor_scalar(qratio[:, :], q2[:, :], 1.0, None, ALU.add))
            ch(dve.reciprocal(qratio[:, :], qratio[:, :]))
            ch(dve.tensor_scalar(q2[:, :], q2[:, :], 1.0, 2.0, ALU.min, ALU.mult))
            dve.tensor_tensor(qratio[:, :], qratio[:, :], q2[:, :], ALU.mult).then_inc(mark("qratio"), 1)
            dve.wait_ge(*at("small_ps"))
            ch(dve.tensor_copy(rwT[:, :], PS[:, 3, 0:E]))
            dve.tensor_copy(wp2T[:, :], PS[:, 3, E:E + 3]).then_inc(mark("small_cp"), 1)
            for b in range(B):
                hs = slice(b * H, b * H + H)
                if b >= 1:
                    dve.wait_ge(*at("cov_b", b))
                dve.tensor_tensor(sqb[:, :].rearrange("p (h d) -> p h d", h=H),
                                  fq[:, b, :].rearrange("p (h d) -> p h d", h=H),
                                  bc(q1[:, hs].unsqueeze(2), [P, H, D]), ALU.subtract).then_inc(mark("qc"), 1)
            dve.wait_ge(*at("q_inv"))
            for b in range(B):
                hs = slice(b * H, b * H + H)
                fb = fq[:, b, :].rearrange("p (h d) -> p h d", h=H)
                dve.tensor_tensor(fb, fb, bc(qinv[:, hs].unsqueeze(2), [P, H, D]), ALU.mult) \
                    .then_inc(mark("fq_unit"), 1)
            dve.wait_ge(*at("cov_b", B))
            ch(dve.tensor_tensor(sqb[:, :].rearrange("p (h d) -> p h d", h=H),
                                 PS[:, 6:8, :].rearrange("p a (h d) -> p (a h) d", d=D),
                                 bc(offdiag[:, :].unsqueeze(1), [P, H, D]), ALU.mult))
            ch(dve.tensor_tensor(sqb[:, :], sqb[:, :], sqb[:, :], ALU.mult))
            dve.tensor_reduce(out=covsum[:, :], in_=sqb[:, :].rearrange("p (h d) -> p h d", h=H),
                              axis=AX.X, op=ALU.add).then_inc(mark("covsum"), 1)
            dve.tensor_reduce(out=meanx[:, 0:1], in_=xnT[:, :], axis=AX.X, op=ALU.add)
            ch(dve.tensor_reduce(out=meanx[:, 1:2], in_=t_all[:, :, H], axis=AX.X, op=ALU.add))
            ch(dve.tensor_scalar(meanx[:, 0:1], meanx[:, 0:1], 1.0 / (B * S), None, ALU.mult))
            dve.tensor_scalar(meanx[:, 1:2], meanx[:, 1:2], 1.0 / (B * S2), None, ALU.mult) \
                .then_inc(mark("meanx"), 1)
            dve.wait_ge(*at("cov_tot"))
            dve.tensor_copy(sm8[:, 0:1], PS[0:8, 3, 300:301]).then_inc(mark("cov_ss"), 1)
            dve.wait_ge(*at("feats_ps"))
            dve.tensor_copy(feats[:, :], PS[:, 3, 0:2 * H]).then_inc(mark("feats"), 1)
            dve.wait_ge(*at("h1_ps"))
            ch(dve.tensor_tensor(h8[:, 0, :], PS[0:8, 3, 128:256], rows[0:8, WPB1, :], ALU.add))
            ch(dve.bn_stats(h8s[:, :], h8[:, 0, :]))
            ch(dve.bn_aggr(h8m[:, :], h8s[:, :]))
            dve.tensor_scalar(h8m[:, 1:2], h8m[:, 1:2], EPS, None, ALU.add).then_inc(mark("wp_var"), 1)
            dve.wait_ge(*at("wp_rstd"))
            ch(dve.tensor_scalar(h8[:, 1, :], h8[:, 0, :], h8m[:, 0:1], h8r[:, 0:1], ALU.subtract, ALU.mult))
            ch(dve.tensor_tensor(h8[:, 1, :], h8[:, 1, :], rows[0:8, WPG, :], ALU.mult))
            ch(dve.tensor_tensor(h8[:, 1, :], h8[:, 1, :], rows[0:8, WPB, :], ALU.add))
            dve.tensor_scalar(h8[:, 2, :], h8[:, 1, :], 0.0, None, ALU.max).then_inc(mark("h1"), 1)
            dve.wait_ge(*at("h1T_ps"))
            dve.tensor_copy(h1T[:, :], PS[:, 3, 256:256 + H]).then_inc(mark("h1T"), 1)
            dve.wait_ge(*at("wp_ps"))
            ch(dve.tensor_tensor(sm8[:, 4:7], PS[0:8, 3, 310:313], wpb2[0:8, :], ALU.add))
            ch(dve.tensor_reduce(out=sm8[:, 7:8], in_=sm8[:, 4:7], axis=AX.X, op=ALU.max))
            dve.tensor_scalar(sm8[:, 4:7], sm8[:, 4:7], sm8[:, 7:8], None, ALU.subtract) \
                .then_inc(mark("wp_logit"), 1)
            dve.wait_ge(*at("wp_exp"))
            ch(dve.tensor_reduce(out=sm8[:, 7:8], in_=sm8[:, 8:11], axis=AX.X, op=ALU.add))
            ch(dve.reciprocal(sm8[:, 7:8], sm8[:, 7:8]))
            ch(dve.tensor_scalar(sm8[:, 8:11], sm8[:, 8:11], sm8[:, 7:8], None, ALU.mult))
            dve.wait_ge(*at("decorr"))
            ch(dve.tensor_tensor(sm8[:, 11:12], sm8[:, 9:10], sm8[:, 3:4], ALU.mult))
            dve.tensor_tensor(sm8[:, 11:12], sm8[:, 11:12], sm8[:, 8:9], ALU.add).then_inc(mark("coef8"), 1)
            dve.wait_ge(*at("coef_ps"))
            ch(dve.tensor_copy(coef[:, :], PS[:, 3, 320:320 + 2 * H]))
            dve.tensor_tensor(wt_t[:, :, :], t_all[:, :, 0:H], bc(coef[:, H:2 * H].unsqueeze(1), [P, B, H]),
                              ALU.mult).then_inc(mark("coef"), 1)
            dve.wait_ge(*at("coef"))
            for h in range(H):
                dve.wait_ge(*at("u_ps", h + 1))
                if h >= 2:
                    dve.wait_ge(*at("out0_ps", h - 1))
                for b in range(B):
                    ins = dve.tensor_scalar(tmpU[:, h % 2, b * S:(b + 1) * S], PS[:, 7, b * S:(b + 1) * S],
                                            wt_t[:, b, h:h + 1], None, ALU.mult)
                ch(ins)
                dve.scalar_tensor_tensor(tmpU[:, h % 2, :], PS[:, 6, :], coef[:, h:h + 1], tmpU[:, h % 2, :],
                                         ALU.mult, ALU.add).then_inc(mark("u"), 1)
            dve.wait_ge(*at("out0_ps", H))
            ch(dve.tensor_tensor(xs[:, :, :], xs[:, :, :], bc(rows[:, BOUT:BOUT + 1, :], [P, B, D]), ALU.add))
            for b in range(B):
                ins = dve.tensor_tensor(xs[:, b, :], xs[:, b, :], PS[:, [0, 1, 4, 5][b], 0:D], ALU.add)
            ins.then_inc(mark("x1"), 1)
            dve.wait_ge(*at("x1"))

            for b in range(B):
                dve.wait_ge(*at("mask%d" % b, 16))
                dve.tensor_scalar(maskb[:, b, :], mask_i[:, b % 2, :], 0.0, MASKED, ALU.is_equal, ALU.mult) \
                    .then_inc(mark("maskb"), 1)

            ch(dve.tensor_scalar(gauss[:, :], gauss[:, :], 4.0 / S, None, ALU.mult))
            dve.tensor_tensor(gauss[:, :], gauss[:, :], gauss[:, :], ALU.mult).then_inc(mark("gauss_sq"), 1)
            layer_norm(xs, xn, "ln1")
            dve.wait_ge(*at("qk_ps"))
            dve.tensor_scalar(qT[:, :], PS[:, 1, :], bcol[:, 0:1], None, ALU.add)
            dve.tensor_scalar(kT[:, :], PS[:, 2, :], bcol[:, 1:2], None, ALU.add).then_inc(mark("qk"), 1)
            dve.wait_ge(*at("v_ps"))
            dve.tensor_tensor(vv[:, :, :], PS[:, 3, :].rearrange("p (b d) -> p b d", b=B),
                              bc(rows[:, BV:BV + 1, :], [P, B, D]), ALU.add).then_inc(mark("v0"), 1)
            dve.wait_ge(*at("sc_ps"))
            dve.wait_ge(*at("gauss"))
            ch(dve.scalar_tensor_tensor(sc[:, :, :], PS[:, 4, :].rearrange("p (b d) -> p b d", b=B),
                                        float(D) ** -0.5, bc(gauss[:, :].unsqueeze(1), [P, B, S]),
                                        ALU.mult, ALU.mult))
            ch(dve.tensor_reduce(out=s4[:, :], in_=sc[:, :, :], axis=AX.X, op=ALU.max))
            dve.tensor_tensor(sc[:, :, :], sc[:, :, :], bc(s4[:, :].unsqueeze(2), [P, B, S]), ALU.subtract) \
                .then_inc(mark("sc_max"), 1)
            dve.wait_ge(*at("sc_exp"))
            ch(dve.tensor_reduce(out=s4[:, :], in_=sc[:, :, :], axis=AX.X, op=ALU.add))
            ch(dve.reciprocal(r4[:, :], s4[:, :]))
            dve.tensor_tensor(sc[:, :, :], sc[:, :, :], bc(r4[:, :].unsqueeze(2), [P, B, S]), ALU.mult) \
                .then_inc(mark("probs"), 1)

            def add_rows(bank, bias, done):
                dve.wait_ge(*at(done))
                ch(dve.tensor_tensor(xs[:, :, :], xs[:, :, :], bc(rows[:, bias:bias + 1, :], [P, B, D]), ALU.add))
                ch(dve.tensor_tensor(xs[:, :, :], xs[:, :, :], PS[:, bank, :].rearrange("p (b d) -> p b d", b=B),
                                     ALU.add))

            add_rows(2, BO, "o0_ps")

            def best(src, dst):
                ch(dve.tensor_reduce(out=s4[:, :], in_=src, axis=AX.X, op=ALU.max))
                ch(dve.tensor_tensor(dst, src, bc(s4[:, :].unsqueeze(2), [P, B, E]), ALU.is_equal))
                ch(dve.tensor_tensor(dst, dst, bc(lastfirst[:, :].unsqueeze(1), [P, B, E]), ALU.mult))
                ch(dve.tensor_reduce(out=s4[:, :], in_=dst, axis=AX.X, op=ALU.max))
                ch(dve.tensor_tensor(dst, dst, bc(s4[:, :].unsqueeze(2), [P, B, E]), ALU.is_equal))

            def router_softmax(name, bias):
                dve.wait_ge(*at(name + "_ps"))
                src = PS[:, 1, 0:B * E].rearrange("p (b e) -> p b e", b=B)
                if bias is None:
                    ch(dve.tensor_copy(lg[:, :, :], src))
                else:
                    ch(dve.tensor_tensor(lg[:, :, :], src, bc(bias.unsqueeze(1), [P, B, E]), ALU.add))
                ch(dve.tensor_reduce(out=s4[:, :], in_=lg[:, :, :], axis=AX.X, op=ALU.max))
                dve.tensor_tensor(lg[:, :, :], lg[:, :, :], bc(s4[:, :].unsqueeze(2), [P, B, E]), ALU.subtract) \
                    .then_inc(mark(name + "_max"), 1)
                dve.wait_ge(*at(name + "_exp"))
                ch(dve.tensor_reduce(out=s4[:, :], in_=pr[:, :, :], axis=AX.X, op=ALU.add))
                ch(dve.reciprocal(r4[:, :], s4[:, :]))
                ch(dve.tensor_tensor(pr[:, :, :], pr[:, :, :], bc(r4[:, :].unsqueeze(2), [P, B, E]), ALU.mult))

            layer_norm(xs, xn, "ln2")
            router_softmax("r0", None)
            best(pr[:, :, :], oh[:, :, :])
            ch(dve.scalar_tensor_tensor(lg[:, :, :], oh[:, :, :], -4.0, pr[:, :, :], ALU.mult, ALU.add))
            best(lg[:, :, :], oh2[:, :, :])
            ch(dve.tensor_tensor(oh[:, :, :], oh[:, :, :], oh2[:, :, :], ALU.add))
            ch(dve.tensor_tensor(wgt[:, :, :], oh[:, :, :].rearrange("p b e -> p e b"),
                                 pr[:, :, :].rearrange("p b e -> p e b"), ALU.mult))

            def combine(i, p, layer):
                dve.wait_ge(*at("e%d_y%d" % (layer, p), i + 1))
                ch(dve.tensor_tensor(ytmp[:, :].rearrange("p (b d) -> p b d", b=B),
                                     PS[:, 6 + p, :].rearrange("p (b d) -> p b d", b=B),
                                     bc(wgt[:, bass.ds(i * 2 + p, 1), :].rearrange("p a b -> p (a b)").unsqueeze(2),
                                        [P, B, D]), ALU.mult))
                dve.tensor_tensor(acc[:, :], acc[:, :], ytmp[:, :], ALU.add) \
                    .then_inc(mark("e%d_add%d" % (layer, p)), 1)
                dve.wait_ge(*at("e%d_add%d" % (layer, p), i + 1))

            dve.memset(acc[:, :], 0.0).then_inc(mark("acc0"), 1)
            dve.wait_ge(*at("acc0"))
            with dve.Fori(0, E // 2) as i:
                ch.loop(i, 2)
                for p in range(2):
                    combine(i, p, 0)
                ch.end_loop(E // 2)
            dve.tensor_tensor(xs[:, :, :], xs[:, :, :], acc[:, :].rearrange("p (b d) -> p b d", b=B), ALU.add) \
                .then_inc(mark("x3"), 1)
            dve.wait_ge(*at("x3"))

            layer_norm(xs, xn, "ln3")
            qr_hi = q_one[:, :].bitcast(F32R)
            ch(dve.tensor_copy(qr_hi, xn[:, :, :].rearrange("p b d -> p (b d)")))
            ch(dve.memset(qpack[:, :, :], 0.0))
            ch(dve.memset(nm[:, :], 0.0))
            qv = qpack[:, :, :].rearrange("p (b g) (j r) -> p b (g j) r", g=G, j=HG)
            hi_v = q_one[:, :].rearrange("p (b h d) -> p b h d", b=B, d=HD)
            xn_v = xn[:, :, :].rearrange("p b (h d) -> p b h d", d=HD)
            for b in range(B):
                dve.tensor_copy(qv[:, b, :, 2:2 + HD], hi_v[:, b])
                dve.tensor_copy(qv[:, b, :, 2 + 2 * HD:2 + 3 * HD], hi_v[:, b])
                ins = dve.tensor_tensor(qv[:, b, :, 2 + HD:2 + 2 * HD], xn_v[:, b], hi_v[:, b], ALU.subtract)
            ins.then_inc(mark("qpack"), 1)

            bm = bc(groupmask[:, :].unsqueeze(2), [P, HG, S])

            def q_blocks(n_dyn, par):
                dve.tensor_tensor(qp1[:, par, :].rearrange("p (j q) -> p j q", j=HG),
                                  bc(qTall[:, bass.ds(n_dyn, 1), :], [P, HG, S]), bm, ALU.mult) \
                    .then_inc(mark("qp1"), 1)

            def chunk_max(mask, C0, c):
                dve.wait_ge(*at("smx_ps", C0 + (c + 1)))
                dve.wait_ge(*at("smx", C0 + c))
                k0 = c % 2 * (S2 // 2)
                dve.memset(gate[:, 1:2], 0.0)
                dve.tensor_tensor_reduce(out=junk[:, :], in0=PS[:, 4:6, :].rearrange("p a n -> p (a n)"),
                                         in1=mask[:, k0:k0 + S2 // 2],
                                         scale=1.0, scalar=LOWEST, op0=ALU.add, op1=ALU.max,
                                         accum_out=mx[:, c:c + 1]).then_inc(mark("smx"), 1)

            def q_shift(n_dyn, U1, par):
                dve.wait_ge(*at("smx", U1 * 2 * HG))
                nv = nm[:, :].rearrange("p (j r) -> p j r", j=HG)
                ch(dve.tensor_reduce(out=nmax[:, :], in_=mx[:, 0:2 * HG].rearrange("p (j a) -> p j a", a=2),
                                     axis=AX.X, op=ALU.max, negate=True))
                ch(dve.tensor_copy(nv[:, :, 0].bitcast(F32R), nmax[:, :]))
                dve.tensor_tensor(nv[:, :, 1], nmax[:, :], nv[:, :, 0], ALU.subtract).then_inc(mark("nm"), 1)
                dve.wait_ge(*at("nmT_ps", U1))
                ch(dve.tensor_tensor(qs2[:, :], PS[:, 4, 0:P],
                                     qTall[:, bass.ds(n_dyn, 1), :].rearrange("p a n -> p (a n)"), ALU.add))
                dve.tensor_tensor(qp2[:, par, :].rearrange("p (j q) -> p j q", j=HG),
                                  bc(qs2[:, :].unsqueeze(1), [P, HG, S]), bm, ALU.mult).then_inc(mark("qp2"), 1)

            def finish_unit(b_dyn, U0, g):
                dve.wait_ge(*at("pv", b_dyn * (G * KT // 2) + (g + 1) * KT // 2))
                po = PS[:, 6 + g % 2, 0:HG * VC].rearrange("p (j c) -> p j c", c=VC)
                ch(dve.reciprocal(rec4[:, :], po[:, :, HD]))
                dve.tensor_tensor(orow[:, bass.ds(b_dyn, 1), g * HG * HD:(g + 1) * HG * HD]
                                  .rearrange("p a (j d) -> p (a j) d", d=HD), po[:, :, 0:HD],
                                  bc(rec4[:, :].unsqueeze(2), [P, HG, HD]), ALU.mult).then_inc(mark("orow%d" % g), 1)
                dve.wait_ge(*at("orow%d" % g, b_dyn + 1))

            def key_lo(b, n):
                dve.wait_ge(*at("ct_hi", b * QUADS + (n + 1)))
                dve.tensor_tensor(ctxT_lo[:, n * NQ * P:(n + 1) * NQ * P], PS[:, 4, :],
                                  ctxT_hi[:, n * NQ * P:(n + 1) * NQ * P].bitcast(F32), ALU.subtract) \
                    .then_inc(mark("ct_lo"), 1)

            for n in range(QUADS):
                key_lo(0, n)
            dve.wait_ge(*at("qTall", 4))
            q_blocks(0, 0)
            for c in range(2 * HG):
                chunk_max(maskb[:, 0, :], 0, c)
            q_shift(0, 1, 0)

            def batch(b, last):
                for g in range(G):
                    if not (last and g == G - 1):
                        n = b * G + (g + 1)
                        q_blocks(n, (g + 1) % 2)
                        if g == 0:
                            dve.wait_ge(*at("mnow", b + 1))
                        if g == G - 1:
                            dve.wait_ge(*at("mnext", b + 1))
                        for c in range(2 * HG):
                            if c == 2 and g >= 1:
                                finish_unit(b, b * G, g - 1)
                            chunk_max(mnow if g < G - 1 else mnext, n * 2 * HG, c)
                            if not last and g == 1 and c < QUADS:
                                key_lo(b + 1, c)
                        dve.wait_ge(*at("st_ps", b * (G * KT // 2) + g * KT // 2))
                        q_shift(n, n + 1, (g + 1) % 2)
                    else:
                        finish_unit(b, b * G, g - 1)
                finish_unit(b, b * G, G - 1)

            with dve.Fori(0, B - 1) as b:
                ch.loop(b, G * 4)
                batch(b, False)
                ch.end_loop(B - 1)
            batch(B - 1, True)
            add_rows(1, BFC, "fc_ps")

            layer_norm(xs, xn, "ln4")
            for name, bank, dst, wrow in (("rms_q", 1, q1r, QW), ("rms_v", 2, v1r, VW)):
                src = PS[:, bank, :]
                dve.wait_ge(*at(name + "_ps"))
                ch(dve.tensor_copy(dst[:, :, :].rearrange("p b d -> p (b d)"), src))
                dv = dst[:, :, :].rearrange("p b (h d) -> p (b h) d", d=HD)
                ch(dve.tensor_tensor(t1r[:, :, :], dst[:, :, :], dst[:, :, :], ALU.mult))
                ch(dve.tensor_reduce(out=q_ms[:, :], in_=t1r[:, :, :].rearrange("p b (h d) -> p (b h) d", d=HD),
                                     axis=AX.X, op=ALU.add))
                dve.tensor_scalar(q_ms[:, :], q_ms[:, :], 1.0 / HD, RMS_EPS, ALU.mult, ALU.add) \
                    .then_inc(mark(name + "_ms"), 1)
                dve.wait_ge(*at(name + "_inv"))
                ch(dve.tensor_tensor(dv, dv, bc(q_rms[:, :].unsqueeze(2), [P, B * NH, HD]), ALU.mult))
                dve.tensor_tensor(dst[:, :, :], dst[:, :, :], bc(rows[:, wrow:wrow + 1, :], [P, B, D]),
                                  ALU.mult).then_inc(mark(name), 1)
            dve.wait_ge(*at("q1_T"))
            for b in range(B):
                if b >= 1:
                    dve.wait_ge(*at("s1_ps", b))
                dve.tensor_tensor(qbd[:, :, :], bc(qT1[:, b * S:(b + 1) * S].unsqueeze(1), [P, NH, S]),
                                  bc(headmask[:, :].unsqueeze(2), [P, NH, S]), ALU.mult).then_inc(mark("qbd"), 1)
                dve.wait_ge(*at("s1_ps", b + 1))
                if b >= 2:
                    dve.wait_ge(*at("o1_ps", b - 1))
                dve.tensor_tensor(sT1[:, b % 2, :].rearrange("p (h q) -> p h q", q=S),
                                  PS[:, 4:8, :].rearrange("p a (h q) -> p (a h) q", q=S),
                                  bc(causal[:, :].unsqueeze(1), [P, NH, S]), ALU.mult).then_inc(mark("s1"), 1)
            dve.wait_ge(*at("o1_ps", B))
            ch(dve.tensor_tensor(xs[:, :, :], xs[:, :, :], PS[:, 0, :].rearrange("p (b d) -> p b d", b=B), ALU.add))

            layer_norm(xs, xn, "ln5")
            router_softmax("r1", rb1[:, :])
            best(pr[:, :, :], oh[:, :, :])
            ch(dve.tensor_tensor(wgt[:, :, :], oh[:, :, :].rearrange("p b e -> p e b"),
                                 pr[:, :, :].rearrange("p b e -> p e b"), ALU.mult))
            dve.memset(acc[:, :], 0.0).then_inc(mark("acc1"), 1)
            dve.wait_ge(*at("acc1"))
            with dve.Fori(0, E // 2) as i:
                ch.loop(i, 2)
                for p in range(2):
                    for c in range(FC):
                        n = p * FC + c
                        dve.wait_ge(*at("e1_sil", i * 2 * FC + (n + 1)))
                        if c == 0:
                            dve.wait_ge(*at("e1_y%d" % p, i))
                        dve.tensor_tensor(hT[:, p, c * B * S:(c + 1) * B * S], sil[:, c % 2, :],
                                          PS[:, 2 * (c % 2) + 1, :], ALU.mult).then_inc(mark("e1_h"), 1)
                    combine(i, p, 1)
                ch.end_loop(E // 2)
            dve.tensor_tensor(xs[:, :, :], xs[:, :, :], acc[:, :].rearrange("p (b d) -> p b d", b=B), ALU.add) \
                .then_inc(mark("x6"), 1)

        @block.tensor
        def _(pe):
            start(pe, "pe")
            def mm(dst, lhsT, rhs, start=True, stop=True):
                return pe.matmul(dst, lhsT, rhs, start=start, stop=stop, skip_group_check=True)

            def turn(dst, src, n=P):
                return pe.transpose(dst, src, ident[0:n, 0:n])

            def turn_rows(src, bank, wait, done):
                pe.wait_ge(*at(wait))
                for b in range(B):
                    ins = turn(PS[:, bank, b * P:(b + 1) * P], src[:, b, :])
                ins.then_inc(mark(done), 1)

            pe.wait_ge(*at("consts"))
            pe.wait_ge(*at("w_in", 16))
            for k in range(2):
                for n in range(4):
                    ins = turn(PS[:, k, n * P:(n + 1) * P], w[:, 4 * k + n, :])
                ins.then_inc(mark("wT_ps"), 1)
            pe.wait_ge(*at("wT", 2))
            pe.wait_ge(*at("wbar"))

            def turn_x(G0, c):
                pe.wait_ge(*at("k_x", G0 + 1))
                pe.wait_ge(*at("msum", G0))
                for j in range(NQ):
                    ins = turn(PS[:, 0, j * P:(j + 1) * P], X[:, c * NQ + j, :])
                ins.then_inc(mark("xt_ps"), 1)

            def sums(b, c, j):
                t = c * NQ + j
                pe.wait_ge(*at("y", b * KT + (t + 1)))
                if t == 0:
                    pe.wait_ge(*at("a_ev", b))
                    pe.wait_ge(*at("t_ev", b))
                xr = X[:, t, :]
                mm(PS[:, 7, 0:H + 1], xr, kr[:, j, :], t == 0, t == KT - 1)
                mm(PS[:, 5, :], xr, Y[:, j, 0:512], t == 0, t == KT - 1)
                mm(PS[:, 6, :], xr, Y[:, j, 512:1024], t == 0, t == KT - 1).then_inc(mark("a_ps"), 1)

            w_in_T = wT[:, W_IN:W_IN + H, :].rearrange("p h d -> p (h d)")
            with pe.Fori(0, B) as b:
                turn_x(b * QUADS, 0)
                for c in range(QUADS):
                    G0 = b * QUADS + c
                    for j in range(NQ):
                        t = c * NQ + j
                        if j == 0:
                            pe.wait_ge(*at("xt", G0 + 1))
                        pe.wait_ge(*at("sq", b * KT + max(t - 1, 0)))
                        xt_j = XT[:, c % 2, j * P:(j + 1) * P]
                        f0 = 1 + 2 * (t % 2)
                        mm(PS[:, f0, :], xt_j, w_in_T[:, 0:512])
                        mm(PS[:, f0 + 1, :], xt_j, w_in_T[:, 512:1024]).then_inc(mark("f_ps"), 1)
                        if c >= 1:
                            sums(b, c - 1, j)
                        if j == 1:
                            for n in range(NQ):
                                ins = mm(PS[:, 0, n * H:(n + 1) * H], XT[:, c % 2, n * P:(n + 1) * P], wbar[:, :])
                            ins.then_inc(mark("mean_ps"), 1)
                        if j == 2 and c + 1 < QUADS:
                            turn_x(b * QUADS + (c + 1), c + 1)
                for j in range(NQ):
                    sums(b, QUADS - 1, j)

            pe.wait_ge(*at("w_all", 16 * 16))
            for k in range(2, 7):
                if k >= 4:
                    pe.wait_ge(*at("wT", k - 1))
                for n in range(4):
                    if 4 * k + n < NW:
                        ins = turn(PS[:, k % 2, n * P:(n + 1) * P], w[:, 4 * k + n, :])
                ins.then_inc(mark("wT_ps"), 1)
            pe.wait_ge(*at("a_ev", B))
            pe.wait_ge(*at("t_ev", B))
            turn_rows(xn, 2, "xq", "xq_T_ps")
            turn(PS[:, 3, 0:E], small[0:E, 0, :], E)
            turn(PS[:, 3, E:E + 3], small[0:3, 1, :], 3).then_inc(mark("small_ps"), 1)
            pe.wait_ge(*at("xq_T"))
            for b in range(B):
                if b >= 2:
                    pe.wait_ge(*at("fq", b - 1))
                for n in range(2):
                    ins = mm(PS[:, 4 + 2 * (b % 2) + n, :], xnT[:, b * S:(b + 1) * S],
                             w_in_T[:, n * 512:(n + 1) * 512])
                ins.then_inc(mark("fq_ps"), 1)

            pe.wait_ge(*at("wT", 7))
            pe.wait_ge(*at("small_cp"))
            for b in range(B):
                pe.wait_ge(*at("qc", b + 1))
                for h in range(H):
                    qc = sqb[:, h * D:(h + 1) * D]
                    ins = mm(PS[:, 6 + h // 4, (h % 4) * D:(h % 4 + 1) * D], qc, qc,
                             b == 0 and h % 4 == 0, b == B - 1)
                ins.then_inc(mark("cov_b"), 1)
            pe.wait_ge(*at("fq_unit", B))
            for h in range(H):
                if h >= 2:
                    pe.wait_ge(*at("fqT", h - 1))
                for b in range(B):
                    ins = turn(PS[:, h % 2, b * S:(b + 1) * S], fq[:, b, h * D:(h + 1) * D])
                ins.then_inc(mark("fqT_ps"), 1)
            for h in range(H):
                ins = mm(PS[:, 4 + h // 4, (h % 4) * D:(h % 4 + 1) * D], w[:, W_IN + h, :], wT[:, W_OUT + h, :])
            ins.then_inc(mark("comb_ps"), 1)
            pe.wait_ge(*at("covsum"))
            mm(PS[0:8, 3, 300:301], covsum[:, :], ones[:, 0:1]).then_inc(mark("cov_tot"), 1)
            pe.wait_ge(*at("meanx"))
            pe.wait_ge(*at("cov_ss"))
            for a in range(2):
                for h in range(H):
                    ins = mm(PS[:, 3, a * H + h:a * H + h + 1], wT[:, W_IN + h, :], meanx[:, a:a + 1])
            ins.then_inc(mark("feats_ps"), 1)
            pe.wait_ge(*at("feats"))
            mm(PS[0:8, 3, 128:256], feats[:, 0:H], wT[:, WP1, :], True, False)
            mm(PS[0:8, 3, 128:256], feats[:, H:2 * H], wT[:, WP1 + 1, :], False, True).then_inc(mark("h1_ps"), 1)
            pe.wait_ge(*at("h1"))
            turn(PS[:, 3, 256:256 + H], h8[:, 2, :], 8).then_inc(mark("h1T_ps"), 1)
            pe.wait_ge(*at("h1T"))
            mm(PS[0:8, 3, 310:313], h1T[:, :], wp2T[:, :]).then_inc(mark("wp_ps"), 1)
            pe.wait_ge(*at("coef8"))
            mm(PS[:, 3, 320:320 + H], sm8[:, 11:12].to_broadcast([8, P]), ident[0:8, 0:8])
            mm(PS[:, 3, 320 + H:320 + 2 * H], sm8[:, 10:11].to_broadcast([8, P]), ident[0:8, 0:8]) \
                .then_inc(mark("coef_ps"), 1)
            pe.wait_ge(*at("coef"))
            pe.wait_ge(*at("comb", 2))

            def z_of(h):
                if h >= 2:
                    pe.wait_ge(*at("zt", h - 1))
                pe.wait_ge(*at("fqT", h + 1 if h > 0 else H))
                mm(PS[:, 2 + h % 2, :], w[:, W_IN + h, :], fqT[:, h, :]).then_inc(mark("zt_ps"), 1)

            def out_of(h):
                pe.wait_ge(*at("u", h + 1))
                for b, bank in enumerate((0, 1, 4, 5)):
                    ins = mm(PS[:, bank, 0:D], tmpU[:, h % 2, b * S:(b + 1) * S], comb[:, h, :], h == 0, h == H - 1)
                ins.then_inc(mark("out0_ps"), 1)

            z_of(0)
            for h in range(H):
                if h + 1 < H:
                    z_of(h + 1)
                pe.wait_ge(*at("zt", h + 1))
                if h >= 1:
                    pe.wait_ge(*at("u", h))
                for b in range(B):
                    mm(PS[:, 6, b * S:(b + 1) * S], a_all[:, b, h * D:(h + 1) * D], zt[:, h % 2, b * S:(b + 1) * S])
                    ins = mm(PS[:, 7, b * S:(b + 1) * S],
                             qratio[:, b * H + h:b * H + h + 1].to_broadcast([P, P]), ident[:, :])
                ins.then_inc(mark("u_ps"), 1)
                if h >= 1:
                    out_of(h - 1)
            out_of(H - 1)
            pe.wait_ge(*at("x1"))

            for n in range(B * KT // 8):
                if n % 2 == 0:
                    pe.wait_ge(*at("maskb", n // 2 + 1))
                if n >= 2:
                    pe.wait_ge(*at("maskT", n - 1))
                pb = PS[:, 6 + n % 2, :].bitcast(BF16)
                for a in range(8):
                    k0 = (n % 2 * 8 + a) * P
                    ins = pe.transpose(pb[:, a * P:(a + 1) * P], maskb[:, n // 2, k0:k0 + P], identb[:, :])
                ins.then_inc(mark("maskT_ps"), 1)
            pe.wait_ge(*at("maskT", B * KT // 8))

            turn_rows(xn, 0, "ln1", "ln1_T_ps")
            pe.wait_ge(*at("ln1_T"))
            mm(PS[:, 1, :], wT[:, WQ, :], xnT[:, :])
            mm(PS[:, 2, :], wT[:, WK, :], xnT[:, :]).then_inc(mark("qk_ps"), 1)
            for b in range(B):
                ins = mm(PS[:, 3, b * D:(b + 1) * D], xnT[:, b * S:(b + 1) * S], wT[:, WV, :])
            ins.then_inc(mark("v_ps"), 1)
            pe.wait_ge(*at("qk"))
            for b in range(B):
                ins = mm(PS[:, 4, b * S:(b + 1) * S], qT[:, b * S:(b + 1) * S], kT[:, b * S:(b + 1) * S])
            ins.then_inc(mark("sc_ps"), 1)
            turn_rows(sc, 0, "probs", "pT_ps")
            pe.wait_ge(*at("pT"))
            pe.wait_ge(*at("v0"))
            for b in range(B):
                ins = mm(PS[:, 1, b * S:(b + 1) * S], vv[:, b, :], pT[:, b * S:(b + 1) * S])
            ins.then_inc(mark("oT_ps"), 1)
            pe.wait_ge(*at("oT"))
            for b in range(B):
                ins = mm(PS[:, 2, b * D:(b + 1) * D], oT[:, b * S:(b + 1) * S], wT[:, WO, :])
            ins.then_inc(mark("o0_ps"), 1)

            def route(name, weights):
                for b in range(B):
                    ins = mm(PS[:, 1, b * E:(b + 1) * E], xnT[:, b * S:(b + 1) * S], weights)
                ins.then_inc(mark(name + "_ps"), 1)

            def expert_rows(par, done):
                for b in range(B):
                    for c in range(FC):
                        ins = mm(PS[:, 6 + par, b * D:(b + 1) * D],
                                 hT[:, par, c * B * S + b * S:c * B * S + (b + 1) * S],
                                 w2T[:, par, c * D:(c + 1) * D], c == 0, c == FC - 1)
                ins.then_inc(mark(done), 1)

            turn_rows(xn, 0, "ln2", "ln2_T_ps")
            pe.wait_ge(*at("ln2_T"))
            route("r0", rwT[:, :])
            pe.wait_ge(*at("acc0"))
            with pe.Fori(0, E // 2) as i:
                for p in range(2):
                    pe.wait_ge(*at("w1_0_%d" % p, i * 16 + 16))
                    pe.wait_ge(*at("e0_T%d" % (1 - p), i * 2 + 2 * p))
                    for c in range(FC):
                        ins = turn(PS[:, 0, c * P:(c + 1) * P], raw1[:, p, c * P:(c + 1) * P])
                    ins.then_inc(mark("e0_T_ps"), 1)
                    pe.wait_ge(*at("w2_0_%d" % p, i * 16 + 16))
                    for c in range(FC):
                        ins = turn(PS[:, 1, c * P:(c + 1) * P], raw2[:, p, c * P:(c + 1) * P])
                    ins.then_inc(mark("e0_T_ps"), 1)
                    pe.wait_ge(*at("e0_T%d" % p, i * 2 + 2))
                    pe.wait_ge(*at("e0_h", i * 2 * FC + p * FC))
                    for c in range(FC):
                        mm(PS[:, 2 + c, :], w1T[:, p, c * P:(c + 1) * P], xnT[:, :]).then_inc(mark("e0_h_ps"), 1)
                    pe.wait_ge(*at("e0_h", i * 2 * FC + (p + 1) * FC))
                    pe.wait_ge(*at("e0_add%d" % p, i))
                    expert_rows(p, "e0_y%d" % p)

            pe.wait_ge(*at("x3"))

            def turn_keys(b, n):
                pe.wait_ge(*at("cx2", b * (16 * QUADS) + 16 * QUADS))
                pe.wait_ge(*at("ct_lo", b * QUADS + n))
                for a in range(NQ):
                    ins = turn(PS[:, 4, a * P:(a + 1) * P], cx2[:, n * NQ + a, :])
                ins.then_inc(mark("ct_ps"), 1)

            pe.wait_ge(*at("qpack"))
            for k in range(4):
                for a in range(4):
                    ins = turn(PS[:, k, a * P:(a + 1) * P], qpack[:, 4 * k + a, :])
                ins.then_inc(mark("qTall_ps"), 1)
            for n in range(QUADS):
                turn_keys(0, n)
            pe.wait_ge(*at("ct_lo", QUADS))
            pe.wait_ge(*at("qTall", 4))

            def scores_for_max(C0, par, g, c):
                pe.wait_ge(*at("smx", C0 + c))
                j = c // 2
                for a in range(2):
                    k0 = (c % 2) * 1024 + a * 512
                    ins = mm(PS[:, 4 + a, :], qp1[:, par, j * S:(j + 1) * S], kp[:, g, k0:k0 + 512])
                ins.then_inc(mark("smx_ps"), 1)

            def turn_shift(U1):
                pe.wait_ge(*at("nm", U1))
                turn(PS[:, 4, 0:P], nm[:, :]).then_inc(mark("nmT_ps"), 1)

            def scores(b, g, n):
                N0 = b * (G * KT // 2)
                m = g * KT // 2 + n
                if n == 0:
                    pe.wait_ge(*at("qp2", b * G + (g + 1)))
                pe.wait_ge(*at("pexp", N0 + max(m - 1, 0)))
                for a in range(2):
                    kt = 2 * n + a
                    bank = 2 * (n % 2) + a
                    ins = mm(PS[:, bank, :], kp[:, g, kt * P:(kt + 1) * P], qp2[:, g % 2, :], True, False)
                    if kt == KT - 1:
                        ins.then_inc(mark("st_unit%d" % g), 1)
                    ins = mm(PS[:, bank, :].rearrange("p (j q) -> p j q", j=HG), identb[:, :],
                             maskT[:, bass.ds(b * KT + kt, 1), :].to_broadcast([P, HG, S]), False, True)
                ins.then_inc(mark("st_ps"), 1)

            def weigh(b, g, n):
                m = g * KT // 2 + n
                pe.wait_ge(*at("pexp", b * (G * KT // 2) + (m + 1)))
                if n == 0:
                    pe.wait_ge(*at("vaug", b * G + (g + 1)))
                    pe.wait_ge(*at("orow%d" % ((g + 2) % G), b + (1 if g >= 2 else 0)))
                for a in range(2):
                    kt = 2 * n + a
                    for j in range(HG):
                        ins = mm(PS[:, 6 + g % 2, j * VC:(j + 1) * VC],
                                 pexp[:, n % 2, a * HG * S + j * S:a * HG * S + (j + 1) * S],
                                 vaug[:, g, kt, j, :], kt == 0 and j == 0, kt == KT - 1)
                ins.then_inc(mark("pv"), 1)

            def attend(b, last):
                for g in range(G):
                    n = b * G + (g + 1)
                    follow = not (last and g == G - 1)
                    keys = g == 1 and not last
                    plan = [1, 1, 1, 1, 2, 2, 0, 0] if keys else [2, 2, 2, 1, 1, 0, 0, 0]
                    c = 0
                    for t in range(KT // 2):
                        scores(b, g, t)
                        if follow:
                            if t == 0:
                                g1 = (g + 1) % G
                                pe.wait_ge(*at("kp%d" % g1, (b + (1 if g == G - 1 else 0)) * (16 * 3 * HG)
                                           + 16 * 3 * HG))
                                pe.wait_ge(*at("qp1", n + 1))
                                pe.wait_ge(*at("qp2", n))
                            for a in range(plan[t]):
                                if keys and c >= 1:
                                    pe.wait_ge(*at("ct_lo", (b + 1) * QUADS + min(c, QUADS)))
                                scores_for_max(n * 2 * HG, (g + 1) % 2, (g + 1) % G, c)
                                c += 1
                                if keys and t < QUADS:
                                    pe.wait_ge(*at("smx", n * 2 * HG + c))
                                    turn_keys(b + 1, t)
                        if t > 0:
                            weigh(b, g, t - 1)
                        elif g > 0:
                            weigh(b, g - 1, KT // 2 - 1)
                        if follow and t == KT // 2 - 2:
                            turn_shift(n + 1)
                weigh(b, G - 1, KT // 2 - 1)

            pe.wait_ge(*at("kp0", 16 * 3 * HG))
            pe.wait_ge(*at("qp1"))
            for c in range(2 * HG):
                scores_for_max(0, 0, 0, c)
            turn_shift(1)
            with pe.Fori(0, B - 1) as b:
                attend(b, False)
            attend(B - 1, True)
            for g in range(G):
                pe.wait_ge(*at("orow%d" % g, B))
            for b in range(B):
                ins = turn(PS[:, 0, b * S:(b + 1) * S], orow[:, b, :])
            ins.then_inc(mark("xo_T_ps"), 1)
            pe.wait_ge(*at("xo_T"))
            for b in range(B):
                ins = mm(PS[:, 1, b * D:(b + 1) * D], oT[:, b * S:(b + 1) * S], wT[:, WFC, :])
            ins.then_inc(mark("fc_ps"), 1)

            turn_rows(xn, 0, "ln4", "ln4_T_ps")
            pe.wait_ge(*at("ln4_T"))
            for bank, n, name in ((1, WQ1, "rms_q_ps"), (2, WV1, "rms_v_ps")):
                for b in range(B):
                    ins = mm(PS[:, bank, b * D:(b + 1) * D], xT1[:, b * S:(b + 1) * S], wT[:, n, :])
                ins.then_inc(mark(name), 1)
            turn_rows(q1r, 3, "rms_q", "q1_T_ps")
            pe.wait_ge(*at("q1_T"))
            pe.wait_ge(*at("rms_v"))
            for b in range(B):
                pe.wait_ge(*at("qbd", b + 1))
                if b >= 1:
                    pe.wait_ge(*at("s1", b))
                for k in range(4):
                    ins = mm(PS[:, 4 + k, :], xT1[:, b * S:(b + 1) * S],
                             qbd[:, 4 * k:4 * k + 4, :].rearrange("p h q -> p (h q)"))
                ins.then_inc(mark("s1_ps"), 1)
                pe.wait_ge(*at("s1", b + 1))
                for h in range(NH):
                    ins = mm(PS[:, 0, b * D + h * HD:b * D + (h + 1) * HD], sT1[:, b % 2, h * S:(h + 1) * S],
                             v1r[:, b, h * HD:(h + 1) * HD])
                ins.then_inc(mark("o1_ps"), 1)

            turn_rows(xn, 0, "ln5", "ln5_T_ps")
            pe.wait_ge(*at("ln5_T"))
            route("r1", rw1[:, :])
            pe.wait_ge(*at("acc1"))
            with pe.Fori(0, E // 2) as i:
                for p in range(2):
                    pe.wait_ge(*at("w1_1_%d" % p, i * 16 + 16))
                    pe.wait_ge(*at("w2_1_%d" % p, i * 16 + 16))
                    for c in range(FC):
                        n = p * FC + c
                        pe.wait_ge(*at("e1_h", i * 2 * FC + max(n - 1, 0)))
                        mm(PS[:, 2 * (c % 2), :], wide1[:, p, c * P:(c + 1) * P], xnT[:, :])
                        mm(PS[:, 2 * (c % 2) + 1, :], wide1[:, p, (FC + c) * P:(FC + c + 1) * P], xnT[:, :]) \
                            .then_inc(mark("e1_h_ps"), 1)
                    pe.wait_ge(*at("e1_h", i * 2 * FC + (p + 1) * FC))
                    pe.wait_ge(*at("e1_add%d" % p, i))
                    expert_rows(p, "e1_y%d" % p)


_INS = ["x", "ctx_1024", "mask_Bx1xSxS2_ik1", "L0_xattn_ln_g", "L0_xattn_ln_b", "L0_xattn_w_in",
        "L0_xattn_wp_w1", "L0_xattn_wp_b1", "L0_xattn_wp_ln_g", "L0_xattn_wp_ln_b", "L0_xattn_wp_w2",
        "L0_xattn_wp_b2", "L0_xattn_w_out", "L0_xattn_b_out", "L0_attn_Wq", "L0_attn_bq", "L0_attn_Wk",
        "L0_attn_bk", "L0_attn_Wv", "L0_attn_bv", "L0_attn_Wo", "L0_attn_bo", "L0_ffn_router_w",
        "L0_ffn_w1", "L0_ffn_w2", "L1_xattn_W_fc", "L1_xattn_b_fc", "L1_attn_Wq", "L1_attn_Wv",
        "L1_attn_q_norm_w", "L1_attn_v_norm_w", "L1_ffn_router_w", "L1_ffn_router_b", "L1_ffn_w1",
        "L1_ffn_w2"]


def kernel(**inputs):
    import numpy as _np
    import concourse.bacc as _bacc
    from concourse import mybir as _mybir
    from concourse.bass_utils import run_bass_kernel_spmd as _run

    nc = _bacc.Bacc("TRN2", target_bir_lowering=False, num_devices=1)
    arrays, tensors = {}, {}
    for name in _INS:
        a = _np.ascontiguousarray(inputs[name])
        arrays[f"in_{name}"] = a
        tensors[name] = nc.dram_tensor(f"in_{name}", a.shape, _mybir.dt.from_np(a.dtype),
                                       kind="ExternalInput").ap()
    out = nc.dram_tensor("out_x", inputs["x"].shape, _mybir.dt.float32, kind="ExternalOutput").ap()
    perceiver_two_layers(nc, tensors, out)
    r = _run(nc, [arrays], core_ids=[0])
    return r.results[0]["out_x"]
```

```python
from contextlib import ExitStack

import concourse.bass as bass
from concourse import mybir

ALU = mybir.AluOpType
ACT = mybir.ActivationFunctionType
AX = mybir.AxisListType
F32 = mybir.dt.float32
F32R = mybir.dt.float32r
BF16 = mybir.dt.bfloat16
I32 = mybir.dt.int32

P = 128
EPS = 1e-5
RMS_EPS = 1e-8
MASKED = -1e20
LOWEST = -3.0e38


ONCE = {
    "pool": ["consts", "ln0_rstd", "ln0b_rstd", "kp_ones", "q_inv", "wp_rstd", "ln1_rstd", "ln2_rstd", "ln3_rstd",
             "ln4_rstd", "rms_q_inv", "rms_v_inv", "ln5_rstd"],
    "act": ["xq_T", "cov_norm", "decorr", "wp_exp", "gauss", "ln1_T", "sc_exp", "pT", "oT", "ln2_T",
            "r0_exp", "xo_T", "ln4_T", "q1_T", "ln5_T", "r1_exp"],
    "dve": ["ln0_var", "ln0", "ln0b_var", "xq", "wbar", "q_ss", "qratio", "small_cp", "covsum", "meanx",
            "cov_ss", "feats", "wp_var", "h1", "h1T", "wp_logit", "coef8", "coef", "x1", "gauss_sq",
            "ln1_var", "ln1", "qk", "v0", "sc_max", "probs", "ln2_var", "ln2", "r0_max", "acc0", "x3",
            "ln3_var", "ln3", "qpack", "ln4_var", "ln4", "rms_q_ms", "rms_q", "rms_v_ms", "rms_v",
            "ln5_var", "ln5", "r1_max", "acc1", "x6"],
    "pe": ["xq_T_ps", "small_ps", "comb_ps", "cov_tot", "feats_ps", "h1_ps", "h1T_ps", "wp_ps", "coef_ps",
           "ln1_T_ps", "qk_ps", "v_ps", "sc_ps", "pT_ps", "oT_ps", "o0_ps", "ln2_T_ps", "r0_ps", "xo_T_ps",
           "fc_ps", "ln4_T_ps", "rms_q_ps", "rms_v_ps", "q1_T_ps", "ln5_T_ps", "r1_ps"],
}


START_AT = {
    "pool": {"vaug": 1},
    "act": {"a_ev": 1, "e0_T0": 1, "e0_T1": 1, "e0_h": 1},
    "dve": {"t_ev": 1, "e0_add0": 1, "e0_add1": 1, "e1_add0": 1, "e1_add1": 1, "e1_h": 1, "ct_lo": 1, "smx": 1,
            "orow": 1},
    "pe": {"a_ps": 4, "e0_y0": 1, "e0_y1": 1, "e1_y0": 1, "e1_y1": 1, "ct_ps": 1,
           "st_unit0": 1, "st_unit1": 1, "st_unit2": 1, "st_unit3": 1},
}


class Chain:

    def __init__(self, eng, sem):
        self.eng, self.sem, self.base, self.n = eng, sem, 0, 0

    def __call__(self, ins):
        self.n += 1
        ins.then_inc(self.sem, 1)
        self.eng.wait_ge(self.sem, self.base + self.n)

    def loop(self, i, per):
        self.start = self.base + self.n
        self.base, self.n, self.per = i * per + self.start, 0, per

    def end_loop(self, count):
        assert self.n == self.per, self.n
        self.base, self.n = self.start + count * self.per, 0


def perceiver_two_layers(nc, T, out):
    x_d, ctx_d, mask_d = T["x"], T["ctx_1024"], T["mask_Bx1xSxS2_ik1"]
    B, S, D = x_d.shape
    S2 = ctx_d.shape[1]
    assert S == P and D == P
    H = T["L0_xattn_w_in"].shape[0] // D
    KT = S2 // P
    NQ = 4
    QUADS = KT // NQ
    NH = T["L1_attn_q_norm_w"].shape[0]
    HD = D // NH
    G = 4
    HG = NH // G
    VC = HD + 1
    E = T["L0_ffn_router_w"].shape[0]
    FC = T["L0_ffn_w1"].shape[1] // P
    assert QUADS == 4 and G == 4 and HG == 4 and FC == 4 and H == 8 and B == 4

    ctx_stack = ExitStack()
    with ctx_stack as stack:
        def sb(name, shape, dt=F32):
            return stack.enter_context(nc.sbuf_tensor("sb_" + name, shape, dt))

        sems = {}

        def sem(name):
            if name not in sems:
                sems[name] = stack.enter_context(nc.semaphore("s_" + name))
            return sems[name]

        once = {}
        for who, names in ONCE.items():
            for n, name in enumerate(names):
                once[name] = (who, n + 1)
        start_at = {name: n for signals in START_AT.values() for name, n in signals.items()}

        def start(eng, who):
            for name, n in START_AT[who].items():
                eng.sem_inc(sem(name), n)

        given = {who: 0 for who in ONCE}

        def at(name, value=1):
            if name in once:
                who, n = once[name]
                return sem(who + "_once"), n
            return sem(name), value + start_at.get(name, 0)

        def mark(name):
            if name not in once:
                return sem(name)
            who, n = once[name]
            given[who] += 1
            assert given[who] == n, (name, n, given[who])
            return sem(who + "_once")

        PS = stack.enter_context(nc.psum_tensor("banks", [P, 8, 512], F32))

        ident = sb("ident", [P, P])
        identb = sb("identb", [P, P], BF16)
        offdiag = sb("offdiag", [P, P])
        ones = sb("ones", [P, P])
        neghalf = sb("neghalf", [P, B * NH])
        groupmask = sb("groupmask", [P, HG])
        headmask = sb("headmask", [P, NH])
        causal = sb("causal", [P, P])
        lastfirst = sb("lastfirst", [P, E])
        gauss = sb("gauss", [P, S])

        W_IN, W_OUT, WQ, WK, WV, WO, WFC, WQ1, WV1, WP1, NW = 0, H, 2 * H, 2 * H + 1, 2 * H + 2, 2 * H + 3, \
            2 * H + 4, 2 * H + 5, 2 * H + 6, 2 * H + 7, 2 * H + 9
        w = sb("w", [P, NW, P])
        wT = sb("wT", [P, NW, P])
        small = sb("small", [32, 2, P])
        rwT = sb("rwT", [P, E])
        wp2T = sb("wp2T", [P, 3])
        rw1 = sb("rw1", [P, E])
        wbar = sb("wbar", [P, H])
        G_, B_, BOUT, BV, BO, BFC, QW, VW, WPB1, WPG, WPB, NB = range(12)
        rows = sb("rows", [P, NB, P])
        wpb2 = sb("wpb2", [P, 3])
        rb1 = sb("rb1", [P, E])
        bcol = sb("bcol", [P, 2])

        xs = sb("xs", [P, B, D])
        xn = sb("xn", [P, B, D])
        xnT = sb("xnT", [P, B * S])
        stats = sb("stats", [P, B, 6])
        mv = sb("mv", [P, B, 2])
        vpe = sb("vpe", [P, B])
        rstd = sb("rstd", [P, B])

        vaug = sb("vaug", [P, G, KT, 2 * HG * VC], F32R)
        ctxT_hi = sb("ctxT_hi", [P, S2], F32R)
        ctxT_lo = sb("ctxT_lo", [P, S2], F32R)
        kp = sb("kp", [P, G, S2], F32R)
        a_all = sb("a_all", [P, B, H * D])
        maskb = a_all[:, :, :].rearrange("p b n -> p (b n)").bitcast(BF16) \
            .rearrange("p (b n) -> p b n", b=B)
        mnow = sb("mnow", [P, S2], BF16)
        mnext = sb("mnext", [P, S2], BF16)
        maskT = sb("maskT", [P, B * KT, S], BF16)

        ARENA = 7936
        arena = sb("arena", [P, ARENA])
        used = [0]

        def view(shape, dims=None):
            n = 1
            for s in shape:
                n *= s
            a = arena[:, used[0]:used[0] + n]
            used[0] += n
            assert used[0] <= ARENA, used[0]
            if len(shape) == 2:
                a = a.rearrange("p (a b) -> p a b", b=shape[1])
            if len(shape) == 3:
                a = a.rearrange("p (a b c) -> p a b c", b=shape[1], c=shape[2])
            return a

        t_all = sb("t_all", [P, B, H + 1])

        mask_i = arena[:, 3072:3072 + 2 * S2].bitcast(I32).rearrange("p (a n) -> p a n", a=2)
        used[0] = 0
        cx = ctxT_hi[:, :].bitcast(F32).rearrange("p (t d) -> p t d", d=D)
        X = view([KT, D])
        XT = view([2, NQ * P])
        maskT_f = maskT[:, :, :].rearrange("p a n -> p (a n)").bitcast(F32)
        sq = maskT_f[:, 0:2 * H * D].rearrange("p (a n) -> p a n", a=2)
        Y = view([NQ, H * D])
        kst = sb("kst", [P, NQ, 6])
        kmv = sb("kmv", [P, NQ, 2])
        kvpe = sb("kvpe", [P, NQ])
        krstd = sb("krstd", [P, NQ])
        ss = sb("ss", [P, NQ, H])
        kw = sb("kw", [P, NQ, H])
        msum = sb("msum", [P, NQ, H])
        kt1 = sb("kt1", [P, NQ, H])
        kt2 = sb("kt2", [P, NQ, H])
        kr = sb("kr", [P, 2, NQ, H + 1])
        used[0] = 0
        fq = view([B, H * D])
        fqT = maskT_f.rearrange("p (h n) -> p h n", h=H)
        sqb = view([H * D])
        zt = sqb.rearrange("p (a n) -> p a n", a=2)
        tmpU = mnext[:, :].bitcast(F32).rearrange("p (a n) -> p a n", a=2)
        qsum = sb("qsum", [P, B * H])
        qss = sb("qss", [P, B * H])
        qinv = sb("qinv", [P, B * H])
        qratio = sb("qratio", [P, B * H])
        q1 = sb("q1", [P, B * H])
        q2 = sb("q2", [P, B * H])
        covsum = sb("covsum", [P, H])
        meanx = sb("meanx", [P, 2])
        feats = sb("feats", [P, 2 * H])
        h8 = sb("h8", [8, 3, P])
        h8s = sb("h8s", [8, 6])
        h8m = sb("h8m", [8, 2])
        h8r = sb("h8r", [8, 2])
        h1T = sb("h1T", [P, H])
        sm8 = sb("sm8", [8, 16])
        coef = sb("coef", [P, 2 * H])
        wt_t = sb("wt_t", [P, B, H])
        comb = mnow[:, :].bitcast(F32).rearrange("p (h d) -> p h d", d=D)
        used[0] = 0
        qT = view([B * S])
        kT = view([B * S])
        vv = view([B, D])
        sc = view([B, S])
        pT = view([B * S])
        oT = view([B * S])
        used[0] = 0
        q1r = view([B, D])
        v1r = view([B, D])
        t1r = view([B, D])
        xT1 = view([B * S])
        qT1 = view([B * S])
        qbd = view([NH, S])
        sT1 = maskT_f.rearrange("p (a n) -> p a n", a=2)
        used[0] = 0
        w_f = w[:, 0:2 * H, :].rearrange("p a n -> p (a n)")
        raw1 = w_f[:, 0:2 * FC * P].rearrange("p (a n) -> p a n", a=2)
        raw2 = w_f[:, 2 * FC * P:4 * FC * P].rearrange("p (a n) -> p a n", a=2)
        w1T = view([2, FC * P])
        w2T = view([2, FC * P])
        hT = view([2, FC * B * S])
        acc = view([B * D])
        ytmp = xn[:, :, :].rearrange("p b d -> p (b d)")
        sil = view([2, B * S])
        wide1 = w_f.rearrange("p (a n) -> p a n", a=2)
        warm = sb("warm", [P, 3])
        gate = sb("gate", [P, 4])
        HC = S2 // 512
        mx = sb("mx", [P, HC * HG])
        s4 = sb("s4", [P, B])
        r4 = sb("r4", [P, B])
        lg = sb("lg", [P, B, E])
        pr = sb("pr", [P, B, E])
        oh = sb("oh", [P, B, E])
        oh2 = sb("oh2", [P, B, E])
        wgt = sb("wgt", [P, E, B])
        used[0] = 0
        pexp = w_f.rearrange("p (a n) -> p a n", a=2)
        junk = view([512])
        o_t = view([HG * S])
        p_hi = sb("p_hi", [P, 2, 2 * HG * S], F32R)
        p_lo = sb("p_lo", [P, 2, 2 * HG * S], F32R)
        qpack = view([G * B, P])
        qTall = view([G * B, S])
        nm = view([P])
        qs2 = view([P])
        cx2 = view([KT, D])
        orow = view([B, D])
        q_one = orow.rearrange("p b d -> p (b d)")
        rec4 = sb("rec4", [P, HG])
        osum = sb("osum", [P, HG, VC])
        nmax = sb("nmax", [P, HG])
        q_ms = sb("q_ms", [P, B * NH])
        q_rms = sb("q_rms", [P, B * NH])
        qp1 = sb("qp1", [P, 2, HG * S], F32R)
        qp2 = sb("qp2", [P, 2, HG * S], F32R)

        block = stack.enter_context(nc.Block())

        def bc(ap, shape):
            return ap.to_broadcast(shape)

        def phase_a(eng, step, chain=None, links=0):
            step(0, 0, False, True, True)
            with eng.Fori(0, B - 1) as b:
                if chain:
                    chain.loop(b, links)
                for c in range(1, QUADS + 1):
                    step(b, c, True, True, True)
                if chain:
                    chain.end_loop(B - 1)
            for c in range(1, QUADS + 1):
                step(B - 1, c, True, c < QUADS, c < QUADS - 1)

        def phase_c(eng, unit, chain=None, links=0):
            unit(0, 0)
            with eng.Fori(0, B - 1) as b:
                if chain:
                    chain.loop(b, links)
                for g in range(1, G + 1):
                    unit(b, g)
                if chain:
                    chain.end_loop(B - 1)
            for g in range(1, G + 1):
                unit(B - 1, g)

        def static(b):
            return isinstance(b, int)

        CHUNKS = [3, 3, 3, 2, 2, 2, 1, 0]
        KEYS_AT = 2

        LNS = ["ln0", "ln0b", "ln1", "ln2", "ln3", "ln4", "ln5"]
        ROUTED = ["r0", "r1"]

        def row_of(name):
            return T[name].rearrange("(a n) -> a n", a=1)

        @block.sync
        def _(sp):
            sp.dma_start(xs[:, :, :], x_d.rearrange("b s d -> s b d")).then_inc(mark("x_in"), 16)
            sp.dma_start(w[:, W_IN:W_IN + H, :], T["L0_xattn_w_in"].rearrange("(h d) n -> d h n", h=H)) \
                .then_inc(mark("w_in"), 16)
            def load_ctx(b, c):
                sp.dma_start(cx[:, c * NQ:(c + 1) * NQ, :],
                             ctx_d[bass.ds(b, 1), c * NQ * P:(c + 1) * NQ * P, :]
                             .rearrange("a (t p) d -> p (a t) d", p=P)).then_inc(mark("ctx%d" % c), 16)

            for c in range(QUADS):
                load_ctx(0, c)
            with sp.Fori(1, B) as b:
                for c in range(QUADS):
                    sp.wait_ge(*at("k_row", (b - 1) * QUADS + (c + 1)))
                    load_ctx(b, c)
            sp.wait_ge(*at("x1"))
            for b in range(B):
                if b >= 2:
                    sp.wait_ge(*at("maskb", b - 1))
                sp.dma_start(mask_i[:, b % 2, :], mask_d[b, 0, :, :]).then_inc(mark("mask%d" % b), 16)
            sp.wait_ge(*at("r0_max"))
            with sp.Fori(0, E // 2) as i:
                for p in range(2):
                    sp.wait_ge(*at("e0_T%d" % p, i * 2))
                    sp.dma_start(raw1[:, p, :].rearrange("p (c d) -> p c d", c=FC),
                                 T["L0_ffn_w1"][bass.ds(i * 2 + p, 1), :, :]
                                 .rearrange("a (c p) d -> p (a c) d", p=P)).then_inc(mark("w1_0_%d" % p), 16)
                    sp.dma_start(raw2[:, p, :], T["L0_ffn_w2"][bass.ds(i * 2 + p, 1), :, :]
                                 .rearrange("a d n -> d (a n)")).then_inc(mark("w2_0_%d" % p), 16)
            sp.wait_ge(*at("x3"))
            sp.wait_ge(*at("kp_ones"))
            with sp.Fori(1, B + 1) as b1:
                b = b1 - 1
                sp.wait_ge(*at("ct_ps", b * QUADS))
                sp.wait_ge(*at("vaug", b * G))
                for c in range(QUADS):
                    sp.dma_start(cx2[:, c * NQ:(c + 1) * NQ, :],
                                 ctx_d[bass.ds(b, 1), c * NQ * P:(c + 1) * NQ * P, :]
                                 .rearrange("a (t p) d -> p (a t) d", p=P)).then_inc(mark("cx2"), 16)
                sp.wait_ge(*at("ct_lo", b1 * QUADS))
                for g in range(G):
                    sp.wait_ge(*at("st_unit%d" % g, b1 - 1))
                    for j in range(HG):
                        for t, src in enumerate((ctxT_hi, ctxT_hi, ctxT_lo)):
                            r = 32 * j + 2 + HD * t
                            k0 = (HG * g + j) * HD
                            sp.dma_start(kp[r:r + HD, g, :].bitcast(F32), src[k0:k0 + HD, :].bitcast(F32)) \
                                .then_inc(mark("kp%d" % g), 16)
            sp.wait_ge(*at("r1_max"))
            with sp.Fori(0, E // 2) as i:
                for p in range(2):
                    sp.wait_ge(*at("e1_y%d" % p, i))
                    sp.dma_start(wide1[:, p, :], T["L1_ffn_w1"][bass.ds(i * 2 + p, 1), :, :]
                                 .rearrange("a d n -> d (a n)")).then_inc(mark("w1_1_%d" % p), 16)
                    sp.dma_start(w2T[:, p, :].rearrange("p (c d) -> p c d", c=FC),
                                 T["L1_ffn_w2"][bass.ds(i * 2 + p, 1), :, :]
                                 .rearrange("a (c p) d -> p (a c) d", p=P)).then_inc(mark("w2_1_%d" % p), 16)
            sp.wait_ge(*at("x6"))
            sp.dma_start(out.rearrange("b s d -> s b d"), xs[:, :, :]).then_inc(mark("out"), 16)
            sp.wait_ge(*at("out", 16))

        @block.gpsimd
        def _(pool):
            start(pool, "pool")
            ch = Chain(pool, sem("pool_chain"))
            ch(pool.memset(ident[:, :], 0.0))
            pool.memset(offdiag[:, :], 1.0)
            pool.memset(neghalf[:, :], -0.5)
            pool.memset(ones[:, :], 1.0)
            pool.memset(headmask[:, :], 1.0)
            pool.memset(groupmask[:, :], 0.0)
            ch(pool.memset(causal[:, :], 1.0))
            ch(pool.affine_select(out=ident[:, :], in_=ident[:, :], compare_op=ALU.not_equal, fill=1.0,
                                  base=0, pattern=[[-1, P]], channel_multiplier=1))
            pool.affine_select(out=offdiag[:, :], in_=offdiag[:, :], compare_op=ALU.not_equal, fill=0.0,
                               base=0, pattern=[[-1, P]], channel_multiplier=1)
            pool.affine_select(out=causal[:, :], in_=causal[:, :], compare_op=ALU.is_ge, fill=0.0,
                               base=0, pattern=[[1, P]], channel_multiplier=-1)
            ch(pool.affine_select(out=headmask[:, :], in_=headmask[:, :], compare_op=ALU.is_ge, fill=0.0,
                                  base=0, pattern=[[-HD, NH]], channel_multiplier=1))
            ch(pool.affine_select(out=headmask[:, :], in_=headmask[:, :], compare_op=ALU.is_ge, fill=0.0,
                                  base=HD - 1, pattern=[[HD, NH]], channel_multiplier=-1))
            for j in range(HG):
                ch(pool.memset(groupmask[32 * j:32 * j + 32, j:j + 1], 1.0))
            pool.iota(lastfirst[:, :], pattern=[[-1, E]], base=E, channel_multiplier=0,
                      allow_small_or_imprecise_dtypes=True)
            ch(pool.iota(gauss[:, :], pattern=[[1, S]], base=-(S // 2), channel_multiplier=0,
                         allow_small_or_imprecise_dtypes=True))
            pool.tensor_copy(identb[:, :], ident[:, :]).then_inc(mark("consts"), 1)
            pool.memset(vaug[:, :, :, 0:HG * VC].bitcast(F32), 1.0)
            ch(pool.memset(vaug[:, :, :, HG * VC:2 * HG * VC].bitcast(F32), 0.0))

            def rstd_of(name):
                pool.wait_ge(*at(name + "_var"))
                pool.tensor_tensor(rstd[:, :], vpe[:, :], neghalf[:, 0:B], ALU.pow) \
                    .then_inc(mark(name + "_rstd"), 1)

            rstd_of("ln0")
            rstd_of("ln0b")
            pool.wait_ge(*at("rows_in", 16 * NB))

            with pool.Fori(0, B) as b:
                ch.loop(b, QUADS)
                for c in range(QUADS):
                    pool.wait_ge(*at("k_row", b * QUADS + (c + 1)))
                    xq = X[:, c * NQ:(c + 1) * NQ, :]
                    ch(pool.tensor_tensor(xq, xq, bc(rows[:, G_:G_ + 1, :], [P, NQ, D]), ALU.mult))
                    pool.tensor_tensor(xq, xq, bc(rows[:, B_:B_ + 1, :], [P, NQ, D]), ALU.add) \
                        .then_inc(mark("k_x"), 1)
                ch.end_loop(B)
            ch(pool.memset(kp[:, :, :].bitcast(F32), 0.0))
            for j in range(HG - 1):
                ch(pool.memset(kp[32 * j:32 * j + 2, :, :].bitcast(F32), 1.0))
            pool.memset(kp[96:98, :, :].bitcast(F32), 1.0).then_inc(mark("kp_ones"), 1)
            pool.wait_ge(*at("kp_ones"))
            pool.wait_ge(*at("q_ss"))
            pool.tensor_tensor(qinv[:, :], qss[:, :], neghalf[:, 0:B * H], ALU.pow).then_inc(mark("q_inv"), 1)
            pool.wait_ge(*at("wp_var"))
            pool.tensor_tensor(h8r[:, 0:1], h8m[:, 1:2], neghalf[0:8, 0:1], ALU.pow).then_inc(mark("wp_rstd"), 1)
            for name in ("ln1", "ln2", "ln3"):
                rstd_of(name)

            def parts(g):
                src = cx2[:, :, g * HG * HD:(g + 1) * HG * HD].rearrange("p t (j d) -> p t j d", j=HG)
                hi, lo = (vaug[:, g, :, a * HG * VC:(a + 1) * HG * VC]
                          .rearrange("p t (j c) -> p t j c", j=HG)[:, :, :, 0:HD] for a in range(2))
                return src, hi, lo

            def values_hi(g):
                src, hi, lo = parts(g)
                ch(pool.tensor_tensor(hi, src, bc(ones[:, 0:1].unsqueeze(2).unsqueeze(3), [P, KT, HG, HD]),
                                      ALU.mult))

            def values_lo(g):
                src, hi, lo = parts(g)
                pool.tensor_tensor(lo, src, hi.bitcast(F32), ALU.subtract).then_inc(mark("vaug"), 1)

            def unit(b, g):
                cur = not (static(b) and b == B - 1 and g == G)
                if not cur:
                    return
                N0 = (b * G + g) * (KT // 2)
                for t in range(KT // 2):
                    half = slice(HG * S, 2 * HG * S)
                    pool.wait_ge(*at("phi", N0 + t + 1))
                    pool.tensor_tensor(p_lo[:, t % 2, half], pexp[:, t % 2, half],
                                       p_hi[:, t % 2, half].bitcast(F32), ALU.subtract) \
                        .then_inc(mark("plo_pool"), 1)
                    if not static(b) and t == 5:
                        if g == 1:
                            pool.wait_ge(*at("cx2", (b + 1) * (16 * QUADS) + 16 * QUADS))
                        pool.wait_ge(*at("orow", b * G + g))
                        values_hi(g - 1)
                    if not static(b) and t == 6:
                        values_lo(g - 1)

            pool.wait_ge(*at("cx2", 16 * QUADS))
            for g in range(G):
                values_hi(g)
                values_lo(g)
            phase_c(pool, unit, ch, G)
            rstd_of("ln4")
            for name in ("rms_q", "rms_v"):
                pool.wait_ge(*at(name + "_ms"))
                pool.tensor_tensor(q_rms[:, :], q_ms[:, :], neghalf[:, 0:B * NH], ALU.pow) \
                    .then_inc(mark(name + "_inv"), 1)
            rstd_of("ln5")

        @block.scalar
        def _(act):
            start(act, "act")
            act.dma_start(w[:, W_OUT:W_OUT + H, :], T["L0_xattn_w_out"].rearrange("n (h d) -> n h d", h=H)) \
                .then_inc(mark("w_all"), 16)
            for n, name in ((WQ, "L0_attn_Wq"), (WK, "L0_attn_Wk"), (WV, "L0_attn_Wv"), (WO, "L0_attn_Wo"),
                            (WFC, "L1_xattn_W_fc"), (WQ1, "L1_attn_Wq"), (WV1, "L1_attn_Wv")):
                act.dma_start(w[:, n, :], T[name]).then_inc(mark("w_all"), 16)
            act.dma_start(w[:, WP1:WP1 + 2, :], T["L0_xattn_wp_w1"].rearrange("n (a d) -> n a d", a=2)) \
                .then_inc(mark("w_all"), 16)
            act.dma_start(small[0:E, 0, :], T["L0_ffn_router_w"]).then_inc(mark("w_all"), 16)
            act.dma_start(small[0:3, 1, :], T["L0_xattn_wp_w2"]).then_inc(mark("w_all"), 16)
            act.dma_start(rw1[:, :], T["L1_ffn_router_w"]).then_inc(mark("w_all"), 16)
            for n, name in ((G_, "L0_xattn_ln_g"), (B_, "L0_xattn_ln_b"), (BOUT, "L0_xattn_b_out"),
                            (BV, "L0_attn_bv"), (BO, "L0_attn_bo"), (BFC, "L1_xattn_b_fc"),
                            (WPB1, "L0_xattn_wp_b1"), (WPG, "L0_xattn_wp_ln_g"), (WPB, "L0_xattn_wp_ln_b")):
                act.dma_start(rows[:, n, :], row_of(name).to_broadcast([P, P])).then_inc(mark("rows_in"), 16)
            for n, name in ((QW, "L1_attn_q_norm_w"), (VW, "L1_attn_v_norm_w")):
                act.dma_start(rows[:, n, :], T[name].rearrange("(a h) d -> a (h d)", a=1).to_broadcast([P, P])) \
                    .then_inc(mark("rows_in"), 16)
            act.dma_start(wpb2[:, :], row_of("L0_xattn_wp_b2").to_broadcast([P, 3])).then_inc(mark("w_all"), 16)
            act.dma_start(rb1[:, :], row_of("L1_ffn_router_b").to_broadcast([P, E])).then_inc(mark("w_all"), 16)
            with nc.allow_non_contiguous_dma(reason="two bias vectors, one element a partition"):
                for n, name in enumerate(("L0_attn_bq", "L0_attn_bk")):
                    act.dma_start(bcol[:, n:n + 1], T[name].rearrange("(n a) -> n a", a=1)) \
                        .then_inc(mark("w_all"), 16)

            def copy(dst, src, wait, value, done):
                act.wait_ge(*at(wait, value))
                act.activation(dst, src, ACT.Copy).then_inc(mark(done), 1)

            for k in range(2):
                copy(wT[:, 4 * k:4 * k + 4, :], PS[:, k, :].rearrange("p (a n) -> p a n", a=4),
                     "wT_ps", k + 1, "wT")
            def rows_sd(G1):
                act.wait_ge(*at("k_var", G1 + 1))
                act.activation(krstd[:, :], kvpe[:, :], ACT.Sqrt).then_inc(mark("k_sd"), 1)

            def xt(G1, c1):
                act.wait_ge(*at("xt_ps", G1 + 1))
                act.activation(XT[:, c1 % 2, :], PS[:, 0, :], ACT.Copy).then_inc(mark("xt"), 1)

            def squares(b, c, j):
                t = c * NQ + j
                act.wait_ge(*at("f_ps", b * KT + (t + 1)))
                if not (isinstance(b, int) and t < 2):
                    act.wait_ge(*at("ssum", b * KT + (t - 1)))
                act.activation(sq[:, j % 2, :], PS[:, 1 + 2 * (j % 2):3 + 2 * (j % 2), :]
                               .rearrange("p a n -> p (a n)"), ACT.Square).then_inc(mark("sq"), 1)

            def step(b, c, prev, cur, nxt):
                G0 = b * QUADS + c
                if cur:
                    squares(b, c, 0)
                    squares(b, c, 1)
                if nxt:
                    rows_sd(G0 + 1)
                if cur:
                    squares(b, c, 2)
                    squares(b, c, 3)
                if nxt:
                    xt(G0 + 1, c + 1)
                if cur:
                    act.wait_ge(*at("k_ss", G0 + 1))
                    act.activation(kw[:, :, :], ss[:, :, :], ACT.Sqrt).then_inc(mark("k_norm"), 1)
                if c == QUADS:
                    act.wait_ge(*at("a_ps", b * KT + KT))
                    act.activation(a_all[:, bass.ds(b, 1), :].rearrange("p a n -> p (a n)"),
                                   PS[:, 5:7, :].rearrange("p a n -> p (a n)"), ACT.Copy).then_inc(mark("a_ev"), 1)

            rows_sd(0)
            xt(0, 0)
            phase_a(act, step)

            for k in range(2, 7):
                m = min(4, NW - 4 * k)
                copy(wT[:, 4 * k:4 * k + m, :], PS[:, k % 2, 0:m * P].rearrange("p (a n) -> p a n", a=m),
                     "wT_ps", k + 1, "wT")
            copy(xnT[:, :], PS[:, 2, :], "xq_T_ps", 1, "xq_T")
            for b in range(B):
                copy(fq[:, b, :], PS[:, 4 + 2 * (b % 2):6 + 2 * (b % 2), :].rearrange("p a n -> p (a n)"),
                     "fq_ps", b + 1, "fq")
            for h in range(H):
                copy(fqT[:, h, :], PS[:, h % 2, :], "fqT_ps", h + 1, "fqT")
            copy(comb[:, 0:4, :], PS[:, 4, :].rearrange("p (a n) -> p a n", a=4), "comb_ps", 1, "comb")
            copy(comb[:, 4:8, :], PS[:, 5, :].rearrange("p (a n) -> p a n", a=4), "comb_ps", 1, "comb")
            act.wait_ge(*at("cov_ss"))
            act.activation(sm8[:, 2:3], sm8[:, 0:1], ACT.Sqrt).then_inc(mark("cov_norm"), 1)
            act.wait_ge(*at("cov_norm"))
            act.activation(sm8[:, 3:4], sm8[:, 2:3], ACT.Exp, scale=-5.0 / (D * D) / (B * S)) \
                .then_inc(mark("decorr"), 1)
            act.wait_ge(*at("wp_logit"))
            act.activation(sm8[:, 8:11], sm8[:, 4:7], ACT.Exp).then_inc(mark("wp_exp"), 1)
            for h in range(H):
                copy(zt[:, h % 2, :], PS[:, 2 + h % 2, :], "zt_ps", h + 1, "zt")

            for n in range(B * KT // 8):
                copy(maskT[:, 8 * n:8 * n + 8, :],
                     PS[:, 6 + n % 2, :].bitcast(BF16).rearrange("p (a n) -> p a n", a=8),
                     "maskT_ps", n + 1, "maskT")

            act.wait_ge(*at("gauss_sq"))
            act.activation(gauss[:, :], gauss[:, :], ACT.Exp, scale=-0.5).then_inc(mark("gauss"), 1)
            copy(xnT[:, :], PS[:, 0, :], "ln1_T_ps", 1, "ln1_T")
            act.wait_ge(*at("sc_max"))
            act.activation(sc[:, :, :], sc[:, :, :], ACT.Exp).then_inc(mark("sc_exp"), 1)
            copy(pT[:, :], PS[:, 0, :], "pT_ps", 1, "pT")
            copy(oT[:, :], PS[:, 1, :], "oT_ps", 1, "oT")

            copy(xnT[:, :], PS[:, 0, :], "ln2_T_ps", 1, "ln2_T")
            act.wait_ge(*at("r0_max"))
            act.activation(pr[:, :, :], lg[:, :, :], ACT.Exp).then_inc(mark("r0_exp"), 1)

            act.activation(warm[:, 0:1], ones[:, 0:1], ACT.Gelu)
            with act.Fori(0, E // 2) as i:
                for p in range(2):
                    act.wait_ge(*at("e0_y%d" % p, i))
                    act.wait_ge(*at("e0_T_ps", i * 4 + (2 * p + 1)))
                    act.activation(w1T[:, p, :], PS[:, 0, :], ACT.Copy).then_inc(mark("e0_T%d" % p), 1)
                    act.wait_ge(*at("e0_T_ps", i * 4 + (2 * p + 2)))
                    act.activation(w2T[:, p, :], PS[:, 1, :], ACT.Copy).then_inc(mark("e0_T%d" % p), 1)
                    for c in range(FC):
                        act.wait_ge(*at("e0_h_ps", i * 2 * FC + (p * FC + c + 1)))
                        act.activation(hT[:, p, c * B * S:(c + 1) * B * S], PS[:, 2 + c, :], ACT.Gelu) \
                            .then_inc(mark("e0_h"), 1)

            copy(qTall[:, 0:4, :], PS[:, 0, :].rearrange("p (a n) -> p a n", a=4), "qTall_ps", 1, "qTall")
            for k in range(1, 4):
                copy(qTall[:, 4 * k:4 * k + 4, :], PS[:, k, :].rearrange("p (a n) -> p a n", a=4),
                     "qTall_ps", k + 1, "qTall")
            act.activation(warm[:, 1:2], ones[:, 0:1], ACT.Exp)

            def key_hi(b, n):
                if n == 0:
                    for g in range(G):
                        act.wait_ge(*at("kp%d" % g, b * (16 * 3 * HG)))
                act.wait_ge(*at("ct_ps", b * QUADS + (n + 1)))
                act.activation(ctxT_hi[:, n * NQ * P:(n + 1) * NQ * P], PS[:, 4, :], ACT.Copy) \
                    .then_inc(mark("ct_hi"), 1)

            def unit(b, g):
                U = b * G + g
                cur = not (static(b) and b == B - 1 and g == G)
                prev = not (static(b) and g == 0)
                for t in range(KT // 2):
                    N = U * (KT // 2) + t
                    if cur:
                        act.wait_ge(*at("st_ps", N + 1))
                        if not (static(N) and N < 2):
                            act.wait_ge(*at("plo_dve", N - 1))
                            act.wait_ge(*at("plo_pool", N - 1))
                        act.activation(pexp[:, t % 2, :], PS[:, 2 * (t % 2):2 * (t % 2) + 2, :]
                                       .rearrange("p a n -> p (a n)"), ACT.Exp, scale=float(D) ** -0.5) \
                            .then_inc(mark("pexp"), 1)
                        act.wait_ge(*at("pexp", N + 1))
                        if not (static(N) and N < 2):
                            act.wait_ge(*at("pv", N - 1))
                        act.activation(p_hi[:, t % 2, :], pexp[:, t % 2, :], ACT.Copy).then_inc(mark("phi"), 1)
                    if not static(b) and g == 1 and KEYS_AT <= t < KEYS_AT + QUADS:
                        key_hi(b + 1, t - KEYS_AT)
                    if prev and t == 2:
                        act.wait_ge(*at("pv", U * (KT // 2)))
                        act.activation(o_t[0:2 * HG * VC, :], PS[0:2 * HG * VC, 6 + (g - 1) % 2, :], ACT.Copy) \
                            .then_inc(mark("o_t"), 1)

            for n in range(QUADS):
                key_hi(0, n)
            phase_c(act, unit)
            copy(oT[:, :], PS[:, 0, :], "xo_T_ps", 1, "xo_T")

            copy(xT1[:, :], PS[:, 0, :], "ln4_T_ps", 1, "ln4_T")
            copy(qT1[:, :], PS[:, 3, :], "q1_T_ps", 1, "q1_T")

            copy(xnT[:, :], PS[:, 0, :], "ln5_T_ps", 1, "ln5_T")
            act.wait_ge(*at("r1_max"))
            act.activation(pr[:, :, :], lg[:, :, :], ACT.Exp).then_inc(mark("r1_exp"), 1)
            act.activation(warm[:, 2:3], ones[:, 0:1], ACT.Silu)
            with act.Fori(0, E // 2) as i:
                for p in range(2):
                    for c in range(FC):
                        n = p * FC + c
                        act.wait_ge(*at("e1_h_ps", i * 2 * FC + (n + 1)))
                        act.wait_ge(*at("e1_h", i * 2 * FC + max(n - 1, 0)))
                        act.activation(sil[:, c % 2, :], PS[:, 2 * (c % 2), :], ACT.Silu).then_inc(mark("e1_sil"), 1)

        @block.vector
        def _(dve):
            start(dve, "dve")
            ch = Chain(dve, sem("dve_chain"))

            def layer_norm_stats(src, name):
                for b in range(B):
                    ins = dve.bn_stats(stats[:, b, :], src[:, b, :])
                ch(ins)
                for b in range(B):
                    ins = dve.bn_aggr(mv[:, b, :], stats[:, b, :])
                ch(ins)
                dve.tensor_scalar(vpe[:, :], mv[:, :, 1], EPS, None, ALU.add).then_inc(mark(name + "_var"), 1)

            def layer_norm(src, dst, name):
                layer_norm_stats(src, name)
                dve.wait_ge(*at(name + "_rstd"))
                for b in range(B):
                    ins = dve.tensor_scalar(dst[:, b, :], src[:, b, :], mv[:, b, 0:1], rstd[:, b:b + 1],
                                            ALU.subtract, ALU.mult)
                ins.then_inc(mark(name), 1)
                dve.wait_ge(*at(name))

            dve.wait_ge(*at("x_in", 16))
            layer_norm(xs, xn, "ln0")
            layer_norm_stats(xn, "ln0b")
            dve.wait_ge(*at("ln0b_rstd"))
            dve.wait_ge(*at("rows_in", 16 * NB))
            for b in range(B):
                ins = dve.tensor_scalar(xn[:, b, :], xn[:, b, :], mv[:, b, 0:1], rstd[:, b:b + 1],
                                        ALU.subtract, ALU.mult)
            ch(ins)
            ch(dve.tensor_tensor(xn[:, :, :], xn[:, :, :], bc(rows[:, G_:G_ + 1, :], [P, B, D]), ALU.mult))
            dve.tensor_tensor(xn[:, :, :], xn[:, :, :], bc(rows[:, B_:B_ + 1, :], [P, B, D]), ALU.add) \
                .then_inc(mark("xq"), 1)
            dve.wait_ge(*at("wT", 2))
            dve.tensor_reduce(out=wbar[:, :], in_=wT[:, W_IN:W_IN + H, :], axis=AX.X, op=ALU.add) \
                .then_inc(mark("wbar"), 1)
            ch(dve.memset(kr[:, :, :, H:H + 1], 1.0))

            def norm_stats(b, c):
                dve.wait_ge(*at("ctx%d" % (c % QUADS), (b + c // QUADS) * 16 + 16))
                for j in range(NQ):
                    ins = dve.bn_stats(kst[:, j, :], cx[:, c % QUADS * NQ + j, :])
                ch(ins)
                dve.memset(gate[:, 0:1], 0.0)
                for j in range(NQ):
                    ins = dve.bn_aggr(kmv[:, j, :], kst[:, j, :])
                ch(ins)
                dve.tensor_scalar(kvpe[:, :], kmv[:, :, 1], EPS, None, ALU.add).then_inc(mark("k_var"), 1)

            def norm_rows(b, c):
                dve.wait_ge(*at("k_sd", b * QUADS + (c + 1)))
                ch(dve.reciprocal(krstd[:, :], krstd[:, :]))
                for j in range(NQ):
                    t = c % QUADS * NQ + j
                    ins = dve.tensor_scalar(X[:, t, :], cx[:, t, :], kmv[:, j, 0:1], krstd[:, j:j + 1],
                                            ALU.subtract, ALU.mult)
                ins.then_inc(mark("k_row"), 1)

            def sum_squares(b, c, j):
                dve.wait_ge(*at("sq", b * KT + (c * NQ + j + 1)))
                dve.tensor_reduce(out=ss[:, j, :], in_=sq[:, j % 2, :].rearrange("p (h d) -> p h d", h=H),
                                  axis=AX.X, op=ALU.add).then_inc(mark("ssum"), 1)

            def ratios(b, c):
                G0 = b * QUADS + c
                dve.wait_ge(*at("ssum", b * KT + (c + 1) * NQ))
                dve.wait_ge(*at("msum", G0 + 1))
                dve.tensor_tensor(kt1[:, :, :], msum[:, :, :], msum[:, :, :], ALU.mult).then_inc(mark("k_ss"), 1)
                dve.wait_ge(*at("k_ss", G0 + 1))
                ch(dve.scalar_tensor_tensor(kt2[:, :, :], kt1[:, :, :], -1.0 / D, ss[:, :, :], ALU.mult, ALU.add))
                ch(dve.tensor_scalar(kt2[:, :, :], kt2[:, :, :], 1.0 / (D - 1), None, ALU.mult))
                ch(dve.tensor_scalar(kt1[:, :, :], kt2[:, :, :], 1.0, None, ALU.add))
                ch(dve.reciprocal(kt1[:, :, :], kt1[:, :, :]))
                ch(dve.tensor_scalar(kt2[:, :, :], kt2[:, :, :], 1.0, 2.0, ALU.min, ALU.mult))
                dve.tensor_tensor(kr[:, c % 2, :, 0:H], kt2[:, :, :], kt1[:, :, :], ALU.mult) \
                    .then_inc(mark("kr"), 1)

            def scaled(b, c, j):
                if not (isinstance(b, int) and c == 0):
                    dve.wait_ge(*at("a_ps", b * KT + ((c - 1) * NQ + j + 1)))
                dve.tensor_tensor(Y[:, j, :].rearrange("p (h d) -> p h d", h=H),
                                  bc(X[:, c * NQ + j:c * NQ + j + 1, :], [P, H, D]),
                                  bc(kw[:, j, :].unsqueeze(2), [P, H, D]), ALU.mult).then_inc(mark("y"), 1)

            def step(b, c, prev, cur, nxt):
                G0 = b * QUADS + c
                if cur:
                    dve.wait_ge(*at("mean_ps", G0 + 1))
                    dve.tensor_copy(msum[:, :, :], PS[:, 0, 0:NQ * H].rearrange("p (a h) -> p a h", a=NQ)) \
                        .then_inc(mark("msum"), 1)
                if prev:
                    dve.wait_ge(*at("k_norm", G0))
                    ch(dve.reciprocal(kw[:, :, :], kw[:, :, :]))
                    dve.wait_ge(*at("k_x", G0))
                    scaled(b, c - 1, 0)
                    scaled(b, c - 1, 1)
                if nxt:
                    norm_stats(b, c + 1)
                if cur:
                    sum_squares(b, c, 0)
                if prev:
                    scaled(b, c - 1, 2)
                if cur:
                    sum_squares(b, c, 1)
                if nxt:
                    norm_rows(b, c + 1)
                if prev:
                    scaled(b, c - 1, 3)
                if cur:
                    sum_squares(b, c, 2)
                    sum_squares(b, c, 3)
                    ratios(b, c)
                if c == QUADS:
                    dve.wait_ge(*at("a_ps", b * KT + KT))
                    dve.tensor_copy(t_all[:, bass.ds(b, 1), :].rearrange("p a n -> p (a n)"), PS[:, 7, 0:H + 1]) \
                        .then_inc(mark("t_ev"), 1)

            norm_stats(0, 0)
            norm_rows(0, 0)
            phase_a(dve, step, ch, QUADS * 9)
            dve.wait_ge(*at("t_ev", B))

            for b in range(B):
                hs = slice(b * H, b * H + H)
                fb = fq[:, b, :].rearrange("p (h d) -> p h d", h=H)
                dve.wait_ge(*at("fq", b + 1))
                dve.tensor_reduce(out=qsum[:, hs], in_=fb, axis=AX.X, op=ALU.add)
                ch(dve.tensor_tensor(sqb[:, :], fq[:, b, :], fq[:, b, :], ALU.mult))
                ch(dve.tensor_reduce(out=qss[:, hs], in_=sqb[:, :].rearrange("p (h d) -> p h d", h=H),
                                     axis=AX.X, op=ALU.add))
            ch(dve.tensor_scalar(q1[:, :], qsum[:, :], 1.0 / D, None, ALU.mult))
            dve.tensor_tensor(q2[:, :], q1[:, :], qsum[:, :], ALU.mult).then_inc(mark("q_ss"), 1)
            dve.wait_ge(*at("q_ss"))
            ch(dve.tensor_tensor(q2[:, :], qss[:, :], q2[:, :], ALU.subtract))
            ch(dve.tensor_scalar(q2[:, :], q2[:, :], 1.0 / (D - 1), None, ALU.mult))
            ch(dve.tensor_scalar(qratio[:, :], q2[:, :], 1.0, None, ALU.add))
            ch(dve.reciprocal(qratio[:, :], qratio[:, :]))
            ch(dve.tensor_scalar(q2[:, :], q2[:, :], 1.0, 2.0, ALU.min, ALU.mult))
            dve.tensor_tensor(qratio[:, :], qratio[:, :], q2[:, :], ALU.mult).then_inc(mark("qratio"), 1)
            dve.wait_ge(*at("small_ps"))
            ch(dve.tensor_copy(rwT[:, :], PS[:, 3, 0:E]))
            dve.tensor_copy(wp2T[:, :], PS[:, 3, E:E + 3]).then_inc(mark("small_cp"), 1)
            for b in range(B):
                hs = slice(b * H, b * H + H)
                if b >= 1:
                    dve.wait_ge(*at("cov_b", b))
                dve.tensor_tensor(sqb[:, :].rearrange("p (h d) -> p h d", h=H),
                                  fq[:, b, :].rearrange("p (h d) -> p h d", h=H),
                                  bc(q1[:, hs].unsqueeze(2), [P, H, D]), ALU.subtract).then_inc(mark("qc"), 1)
            dve.wait_ge(*at("q_inv"))
            for b in range(B):
                hs = slice(b * H, b * H + H)
                fb = fq[:, b, :].rearrange("p (h d) -> p h d", h=H)
                dve.tensor_tensor(fb, fb, bc(qinv[:, hs].unsqueeze(2), [P, H, D]), ALU.mult) \
                    .then_inc(mark("fq_unit"), 1)
            dve.wait_ge(*at("cov_b", B))
            ch(dve.tensor_tensor(sqb[:, :].rearrange("p (h d) -> p h d", h=H),
                                 PS[:, 6:8, :].rearrange("p a (h d) -> p (a h) d", d=D),
                                 bc(offdiag[:, :].unsqueeze(1), [P, H, D]), ALU.mult))
            ch(dve.tensor_tensor(sqb[:, :], sqb[:, :], sqb[:, :], ALU.mult))
            dve.tensor_reduce(out=covsum[:, :], in_=sqb[:, :].rearrange("p (h d) -> p h d", h=H),
                              axis=AX.X, op=ALU.add).then_inc(mark("covsum"), 1)
            dve.tensor_reduce(out=meanx[:, 0:1], in_=xnT[:, :], axis=AX.X, op=ALU.add)
            ch(dve.tensor_reduce(out=meanx[:, 1:2], in_=t_all[:, :, H], axis=AX.X, op=ALU.add))
            ch(dve.tensor_scalar(meanx[:, 0:1], meanx[:, 0:1], 1.0 / (B * S), None, ALU.mult))
            dve.tensor_scalar(meanx[:, 1:2], meanx[:, 1:2], 1.0 / (B * S2), None, ALU.mult) \
                .then_inc(mark("meanx"), 1)
            dve.wait_ge(*at("cov_tot"))
            dve.tensor_copy(sm8[:, 0:1], PS[0:8, 3, 300:301]).then_inc(mark("cov_ss"), 1)
            dve.wait_ge(*at("feats_ps"))
            dve.tensor_copy(feats[:, :], PS[:, 3, 0:2 * H]).then_inc(mark("feats"), 1)
            dve.wait_ge(*at("h1_ps"))
            ch(dve.tensor_tensor(h8[:, 0, :], PS[0:8, 3, 128:256], rows[0:8, WPB1, :], ALU.add))
            ch(dve.bn_stats(h8s[:, :], h8[:, 0, :]))
            ch(dve.bn_aggr(h8m[:, :], h8s[:, :]))
            dve.tensor_scalar(h8m[:, 1:2], h8m[:, 1:2], EPS, None, ALU.add).then_inc(mark("wp_var"), 1)
            dve.wait_ge(*at("wp_rstd"))
            ch(dve.tensor_scalar(h8[:, 1, :], h8[:, 0, :], h8m[:, 0:1], h8r[:, 0:1], ALU.subtract, ALU.mult))
            ch(dve.tensor_tensor(h8[:, 1, :], h8[:, 1, :], rows[0:8, WPG, :], ALU.mult))
            ch(dve.tensor_tensor(h8[:, 1, :], h8[:, 1, :], rows[0:8, WPB, :], ALU.add))
            dve.tensor_scalar(h8[:, 2, :], h8[:, 1, :], 0.0, None, ALU.max).then_inc(mark("h1"), 1)
            dve.wait_ge(*at("h1T_ps"))
            dve.tensor_copy(h1T[:, :], PS[:, 3, 256:256 + H]).then_inc(mark("h1T"), 1)
            dve.wait_ge(*at("wp_ps"))
            ch(dve.tensor_tensor(sm8[:, 4:7], PS[0:8, 3, 310:313], wpb2[0:8, :], ALU.add))
            ch(dve.tensor_reduce(out=sm8[:, 7:8], in_=sm8[:, 4:7], axis=AX.X, op=ALU.max))
            dve.tensor_scalar(sm8[:, 4:7], sm8[:, 4:7], sm8[:, 7:8], None, ALU.subtract) \
                .then_inc(mark("wp_logit"), 1)
            dve.wait_ge(*at("wp_exp"))
            ch(dve.tensor_reduce(out=sm8[:, 7:8], in_=sm8[:, 8:11], axis=AX.X, op=ALU.add))
            ch(dve.reciprocal(sm8[:, 7:8], sm8[:, 7:8]))
            ch(dve.tensor_scalar(sm8[:, 8:11], sm8[:, 8:11], sm8[:, 7:8], None, ALU.mult))
            dve.wait_ge(*at("decorr"))
            ch(dve.tensor_tensor(sm8[:, 11:12], sm8[:, 9:10], sm8[:, 3:4], ALU.mult))
            dve.tensor_tensor(sm8[:, 11:12], sm8[:, 11:12], sm8[:, 8:9], ALU.add).then_inc(mark("coef8"), 1)
            dve.wait_ge(*at("coef_ps"))
            ch(dve.tensor_copy(coef[:, :], PS[:, 3, 320:320 + 2 * H]))
            dve.tensor_tensor(wt_t[:, :, :], t_all[:, :, 0:H], bc(coef[:, H:2 * H].unsqueeze(1), [P, B, H]),
                              ALU.mult).then_inc(mark("coef"), 1)
            dve.wait_ge(*at("coef"))
            for h in range(H):
                dve.wait_ge(*at("u_ps", h + 1))
                if h >= 2:
                    dve.wait_ge(*at("out0_ps", h - 1))
                for b in range(B):
                    ins = dve.tensor_scalar(tmpU[:, h % 2, b * S:(b + 1) * S], PS[:, 7, b * S:(b + 1) * S],
                                            wt_t[:, b, h:h + 1], None, ALU.mult)
                ch(ins)
                dve.scalar_tensor_tensor(tmpU[:, h % 2, :], PS[:, 6, :], coef[:, h:h + 1], tmpU[:, h % 2, :],
                                         ALU.mult, ALU.add).then_inc(mark("u"), 1)
            dve.wait_ge(*at("out0_ps", H))
            ch(dve.tensor_tensor(xs[:, :, :], xs[:, :, :], bc(rows[:, BOUT:BOUT + 1, :], [P, B, D]), ALU.add))
            for b in range(B):
                ins = dve.tensor_tensor(xs[:, b, :], xs[:, b, :], PS[:, [0, 1, 4, 5][b], 0:D], ALU.add)
            ins.then_inc(mark("x1"), 1)
            dve.wait_ge(*at("x1"))

            for b in range(B):
                dve.wait_ge(*at("mask%d" % b, 16))
                dve.tensor_scalar(maskb[:, b, :], mask_i[:, b % 2, :], 0.0, MASKED, ALU.is_equal, ALU.mult) \
                    .then_inc(mark("maskb"), 1)

            ch(dve.tensor_scalar(gauss[:, :], gauss[:, :], 4.0 / S, None, ALU.mult))
            dve.tensor_tensor(gauss[:, :], gauss[:, :], gauss[:, :], ALU.mult).then_inc(mark("gauss_sq"), 1)
            layer_norm(xs, xn, "ln1")
            dve.wait_ge(*at("qk_ps"))
            dve.tensor_scalar(qT[:, :], PS[:, 1, :], bcol[:, 0:1], None, ALU.add)
            dve.tensor_scalar(kT[:, :], PS[:, 2, :], bcol[:, 1:2], None, ALU.add).then_inc(mark("qk"), 1)
            dve.wait_ge(*at("v_ps"))
            dve.tensor_tensor(vv[:, :, :], PS[:, 3, :].rearrange("p (b d) -> p b d", b=B),
                              bc(rows[:, BV:BV + 1, :], [P, B, D]), ALU.add).then_inc(mark("v0"), 1)
            dve.wait_ge(*at("sc_ps"))
            dve.wait_ge(*at("gauss"))
            ch(dve.scalar_tensor_tensor(sc[:, :, :], PS[:, 4, :].rearrange("p (b d) -> p b d", b=B),
                                        float(D) ** -0.5, bc(gauss[:, :].unsqueeze(1), [P, B, S]),
                                        ALU.mult, ALU.mult))
            ch(dve.tensor_reduce(out=s4[:, :], in_=sc[:, :, :], axis=AX.X, op=ALU.max))
            dve.tensor_tensor(sc[:, :, :], sc[:, :, :], bc(s4[:, :].unsqueeze(2), [P, B, S]), ALU.subtract) \
                .then_inc(mark("sc_max"), 1)
            dve.wait_ge(*at("sc_exp"))
            ch(dve.tensor_reduce(out=s4[:, :], in_=sc[:, :, :], axis=AX.X, op=ALU.add))
            ch(dve.reciprocal(r4[:, :], s4[:, :]))
            dve.tensor_tensor(sc[:, :, :], sc[:, :, :], bc(r4[:, :].unsqueeze(2), [P, B, S]), ALU.mult) \
                .then_inc(mark("probs"), 1)

            def add_rows(bank, bias, done):
                dve.wait_ge(*at(done))
                ch(dve.tensor_tensor(xs[:, :, :], xs[:, :, :], bc(rows[:, bias:bias + 1, :], [P, B, D]), ALU.add))
                ch(dve.tensor_tensor(xs[:, :, :], xs[:, :, :], PS[:, bank, :].rearrange("p (b d) -> p b d", b=B),
                                     ALU.add))

            add_rows(2, BO, "o0_ps")

            def best(src, dst):
                ch(dve.tensor_reduce(out=s4[:, :], in_=src, axis=AX.X, op=ALU.max))
                ch(dve.tensor_tensor(dst, src, bc(s4[:, :].unsqueeze(2), [P, B, E]), ALU.is_equal))
                ch(dve.tensor_tensor(dst, dst, bc(lastfirst[:, :].unsqueeze(1), [P, B, E]), ALU.mult))
                ch(dve.tensor_reduce(out=s4[:, :], in_=dst, axis=AX.X, op=ALU.max))
                ch(dve.tensor_tensor(dst, dst, bc(s4[:, :].unsqueeze(2), [P, B, E]), ALU.is_equal))

            def router_softmax(name, bias):
                dve.wait_ge(*at(name + "_ps"))
                src = PS[:, 1, 0:B * E].rearrange("p (b e) -> p b e", b=B)
                if bias is None:
                    ch(dve.tensor_copy(lg[:, :, :], src))
                else:
                    ch(dve.tensor_tensor(lg[:, :, :], src, bc(bias.unsqueeze(1), [P, B, E]), ALU.add))
                ch(dve.tensor_reduce(out=s4[:, :], in_=lg[:, :, :], axis=AX.X, op=ALU.max))
                dve.tensor_tensor(lg[:, :, :], lg[:, :, :], bc(s4[:, :].unsqueeze(2), [P, B, E]), ALU.subtract) \
                    .then_inc(mark(name + "_max"), 1)
                dve.wait_ge(*at(name + "_exp"))
                ch(dve.tensor_reduce(out=s4[:, :], in_=pr[:, :, :], axis=AX.X, op=ALU.add))
                ch(dve.reciprocal(r4[:, :], s4[:, :]))
                ch(dve.tensor_tensor(pr[:, :, :], pr[:, :, :], bc(r4[:, :].unsqueeze(2), [P, B, E]), ALU.mult))

            layer_norm(xs, xn, "ln2")
            router_softmax("r0", None)
            best(pr[:, :, :], oh[:, :, :])
            ch(dve.scalar_tensor_tensor(lg[:, :, :], oh[:, :, :], -4.0, pr[:, :, :], ALU.mult, ALU.add))
            best(lg[:, :, :], oh2[:, :, :])
            ch(dve.tensor_tensor(oh[:, :, :], oh[:, :, :], oh2[:, :, :], ALU.add))
            ch(dve.tensor_tensor(wgt[:, :, :], oh[:, :, :].rearrange("p b e -> p e b"),
                                 pr[:, :, :].rearrange("p b e -> p e b"), ALU.mult))

            def combine(i, p, layer):
                dve.wait_ge(*at("e%d_y%d" % (layer, p), i + 1))
                ch(dve.tensor_tensor(ytmp[:, :].rearrange("p (b d) -> p b d", b=B),
                                     PS[:, 6 + p, :].rearrange("p (b d) -> p b d", b=B),
                                     bc(wgt[:, bass.ds(i * 2 + p, 1), :].rearrange("p a b -> p (a b)").unsqueeze(2),
                                        [P, B, D]), ALU.mult))
                dve.tensor_tensor(acc[:, :], acc[:, :], ytmp[:, :], ALU.add) \
                    .then_inc(mark("e%d_add%d" % (layer, p)), 1)
                dve.wait_ge(*at("e%d_add%d" % (layer, p), i + 1))

            dve.memset(acc[:, :], 0.0).then_inc(mark("acc0"), 1)
            dve.wait_ge(*at("acc0"))
            with dve.Fori(0, E // 2) as i:
                ch.loop(i, 2)
                for p in range(2):
                    combine(i, p, 0)
                ch.end_loop(E // 2)
            dve.tensor_tensor(xs[:, :, :], xs[:, :, :], acc[:, :].rearrange("p (b d) -> p b d", b=B), ALU.add) \
                .then_inc(mark("x3"), 1)
            dve.wait_ge(*at("x3"))

            layer_norm(xs, xn, "ln3")
            qr_hi = q_one[:, :].bitcast(F32R)
            ch(dve.tensor_copy(qr_hi, xn[:, :, :].rearrange("p b d -> p (b d)")))
            ch(dve.memset(qpack[:, :, :], 0.0))
            ch(dve.memset(nm[:, :], 0.0))
            qv = qpack[:, :, :].rearrange("p (b g) (j r) -> p b (g j) r", g=G, j=HG)
            hi_v = q_one[:, :].rearrange("p (b h d) -> p b h d", b=B, d=HD)
            xn_v = xn[:, :, :].rearrange("p b (h d) -> p b h d", d=HD)
            for b in range(B):
                dve.tensor_copy(qv[:, b, :, 2:2 + HD], hi_v[:, b])
                dve.tensor_copy(qv[:, b, :, 2 + 2 * HD:2 + 3 * HD], hi_v[:, b])
                ins = dve.tensor_tensor(qv[:, b, :, 2 + HD:2 + 2 * HD], xn_v[:, b], hi_v[:, b], ALU.subtract)
            ins.then_inc(mark("qpack"), 1)

            bm = bc(groupmask[:, :].unsqueeze(2), [P, HG, S])

            def q_blocks(n_dyn, par):
                dve.tensor_tensor(qp1[:, par, :].rearrange("p (j q) -> p j q", j=HG),
                                  bc(qTall[:, bass.ds(n_dyn, 1), :], [P, HG, S]), bm, ALU.mult) \
                    .then_inc(mark("qp1"), 1)

            def chunk_max(mask, C0, c):
                dve.wait_ge(*at("smx_ps", C0 + (c + 1)))
                dve.wait_ge(*at("smx", C0 + c))
                k0 = c % HC * 512
                dve.memset(gate[:, 1:2], 0.0)
                dve.tensor_tensor_reduce(out=junk[:, :], in0=PS[:, 4 + c % 2, :], in1=mask[:, k0:k0 + 512],
                                         scale=1.0, scalar=LOWEST, op0=ALU.add, op1=ALU.max,
                                         accum_out=mx[:, c:c + 1]).then_inc(mark("smx"), 1)

            def q_max(U1):
                dve.wait_ge(*at("smx", U1 * HC * HG))
                nv = nm[:, :].rearrange("p (j r) -> p j r", j=HG)
                ch(dve.tensor_reduce(out=nmax[:, :], in_=mx[:, :].rearrange("p (j a) -> p j a", a=HC),
                                     axis=AX.X, op=ALU.max, negate=True))
                ch(dve.tensor_copy(nv[:, :, 0].bitcast(F32R), nmax[:, :]))
                dve.tensor_tensor(nv[:, :, 1], nmax[:, :], nv[:, :, 0], ALU.subtract).then_inc(mark("nm"), 1)

            def q_shift(n_dyn, U1, par):
                dve.wait_ge(*at("nmT_ps", U1))
                ch(dve.tensor_tensor(qs2[:, :], PS[:, 4, 0:P],
                                     qTall[:, bass.ds(n_dyn, 1), :].rearrange("p a n -> p (a n)"), ALU.add))
                dve.tensor_tensor(qp2[:, par, :].rearrange("p (j q) -> p j q", j=HG),
                                  bc(qs2[:, :].unsqueeze(1), [P, HG, S]), bm, ALU.mult).then_inc(mark("qp2"), 1)

            def finish_unit(b, g):
                dve.wait_ge(*at("o_t_ps", b * G + g + 1))
                R = 2 * HG * VC + VC
                hi, lo = (PS[:, 6 + g % 2, a * HG * VC:a * HG * VC + (HG - 1) * R + VC + (R - VC)]
                          .rearrange("p (j r) -> p j r", r=R)[:, :, 0:VC] for a in range(2))
                ch(dve.tensor_copy(osum[:, :, :], hi))
                ch(dve.tensor_tensor(osum[:, :, :], lo, osum[:, :, :], ALU.add))
                ch(dve.reciprocal(rec4[:, :], osum[:, :, HD]))
                dve.tensor_tensor(orow[:, bass.ds(b, 1), g * HG * HD:(g + 1) * HG * HD]
                                  .rearrange("p a (j d) -> p (a j) d", d=HD), osum[:, :, 0:HD],
                                  bc(rec4[:, :].unsqueeze(2), [P, HG, HD]), ALU.mult).then_inc(mark("orow"), 1)
                dve.wait_ge(*at("orow", b * G + g + 1))

            def key_lo(b, n):
                dve.wait_ge(*at("ct_hi", b * QUADS + (n + 1)))
                dve.tensor_tensor(ctxT_lo[:, n * NQ * P:(n + 1) * NQ * P], PS[:, 4, :],
                                  ctxT_hi[:, n * NQ * P:(n + 1) * NQ * P].bitcast(F32), ALU.subtract) \
                    .then_inc(mark("ct_lo"), 1)

            for n in range(QUADS):
                key_lo(0, n)
            dve.wait_ge(*at("qTall", 4))
            q_blocks(0, 0)
            for c in range(HC * HG):
                chunk_max(maskb[:, 0, :], 0, c)
            q_max(1)
            q_shift(0, 1, 0)
            ch(dve.tensor_copy(mnow[:, :], maskb[:, 0, :]))

            def unit(b, g):
                U = b * G + g
                cur = not (static(b) and b == B - 1 and g == G)
                prev = not (static(b) and g == 0)
                follow = cur and not (static(b) and b == B - 1 and g == G - 1)
                c = 0
                if follow:
                    q_blocks(U + 1, (g + 1) % 2)
                for t in range(KT // 2):
                    if follow:
                        for _ in range(CHUNKS[t]):
                            chunk_max(mnow if (g + 1) % G else mnext, (U + 1) * HC * HG, c)
                            c += 1
                    if not static(b) and g == 1 and KEYS_AT <= t < KEYS_AT + QUADS:
                        key_lo(b + 1, t - KEYS_AT)
                    if follow and t == 6:
                        q_max(U + 2)
                    if follow and t == 7:
                        q_shift(U + 1, U + 2, (g + 1) % 2)
                    if cur:
                        dve.wait_ge(*at("phi", U * (KT // 2) + t + 1))
                        dve.tensor_tensor(p_lo[:, t % 2, 0:HG * S], pexp[:, t % 2, 0:HG * S],
                                          p_hi[:, t % 2, 0:HG * S].bitcast(F32), ALU.subtract) \
                            .then_inc(mark("plo_dve"), 1)
                    if prev and t == 4:
                        finish_unit(b, g - 1)
                    if not static(b) and t == 3 and g in (1, 3):
                        ch(dve.tensor_copy((mnext if g == 1 else mnow)[:, :],
                                           maskb[:, bass.ds(b + 1, 1), :].rearrange("p a n -> p (a n)")))

            phase_c(dve, unit, ch, G * 6 + 2)
            add_rows(1, BFC, "fc_ps")

            layer_norm(xs, xn, "ln4")
            for name, bank, dst, wrow in (("rms_q", 1, q1r, QW), ("rms_v", 2, v1r, VW)):
                src = PS[:, bank, :]
                dve.wait_ge(*at(name + "_ps"))
                ch(dve.tensor_copy(dst[:, :, :].rearrange("p b d -> p (b d)"), src))
                dv = dst[:, :, :].rearrange("p b (h d) -> p (b h) d", d=HD)
                ch(dve.tensor_tensor(t1r[:, :, :], dst[:, :, :], dst[:, :, :], ALU.mult))
                ch(dve.tensor_reduce(out=q_ms[:, :], in_=t1r[:, :, :].rearrange("p b (h d) -> p (b h) d", d=HD),
                                     axis=AX.X, op=ALU.add))
                dve.tensor_scalar(q_ms[:, :], q_ms[:, :], 1.0 / HD, RMS_EPS, ALU.mult, ALU.add) \
                    .then_inc(mark(name + "_ms"), 1)
                dve.wait_ge(*at(name + "_inv"))
                ch(dve.tensor_tensor(dv, dv, bc(q_rms[:, :].unsqueeze(2), [P, B * NH, HD]), ALU.mult))
                dve.tensor_tensor(dst[:, :, :], dst[:, :, :], bc(rows[:, wrow:wrow + 1, :], [P, B, D]),
                                  ALU.mult).then_inc(mark(name), 1)
            dve.wait_ge(*at("q1_T"))
            for b in range(B):
                if b >= 1:
                    dve.wait_ge(*at("s1_ps", b))
                dve.tensor_tensor(qbd[:, :, :], bc(qT1[:, b * S:(b + 1) * S].unsqueeze(1), [P, NH, S]),
                                  bc(headmask[:, :].unsqueeze(2), [P, NH, S]), ALU.mult).then_inc(mark("qbd"), 1)
                dve.wait_ge(*at("s1_ps", b + 1))
                if b >= 2:
                    dve.wait_ge(*at("o1_ps", b - 1))
                dve.tensor_tensor(sT1[:, b % 2, :].rearrange("p (h q) -> p h q", q=S),
                                  PS[:, 4:8, :].rearrange("p a (h q) -> p (a h) q", q=S),
                                  bc(causal[:, :].unsqueeze(1), [P, NH, S]), ALU.mult).then_inc(mark("s1"), 1)
            dve.wait_ge(*at("o1_ps", B))
            ch(dve.tensor_tensor(xs[:, :, :], xs[:, :, :], PS[:, 0, :].rearrange("p (b d) -> p b d", b=B), ALU.add))

            layer_norm(xs, xn, "ln5")
            router_softmax("r1", rb1[:, :])
            best(pr[:, :, :], oh[:, :, :])
            ch(dve.tensor_tensor(wgt[:, :, :], oh[:, :, :].rearrange("p b e -> p e b"),
                                 pr[:, :, :].rearrange("p b e -> p e b"), ALU.mult))
            dve.memset(acc[:, :], 0.0).then_inc(mark("acc1"), 1)
            dve.wait_ge(*at("acc1"))
            with dve.Fori(0, E // 2) as i:
                ch.loop(i, 2)
                for p in range(2):
                    for c in range(FC):
                        n = p * FC + c
                        dve.wait_ge(*at("e1_sil", i * 2 * FC + (n + 1)))
                        if c == 0:
                            dve.wait_ge(*at("e1_y%d" % p, i))
                        dve.tensor_tensor(hT[:, p, c * B * S:(c + 1) * B * S], sil[:, c % 2, :],
                                          PS[:, 2 * (c % 2) + 1, :], ALU.mult).then_inc(mark("e1_h"), 1)
                    combine(i, p, 1)
                ch.end_loop(E // 2)
            dve.tensor_tensor(xs[:, :, :], xs[:, :, :], acc[:, :].rearrange("p (b d) -> p b d", b=B), ALU.add) \
                .then_inc(mark("x6"), 1)

        @block.tensor
        def _(pe):
            start(pe, "pe")
            def mm(dst, lhsT, rhs, start=True, stop=True):
                return pe.matmul(dst, lhsT, rhs, start=start, stop=stop, skip_group_check=True)

            def turn(dst, src, n=P):
                return pe.transpose(dst, src, ident[0:n, 0:n])

            def turn_rows(src, bank, wait, done):
                pe.wait_ge(*at(wait))
                for b in range(B):
                    ins = turn(PS[:, bank, b * P:(b + 1) * P], src[:, b, :])
                ins.then_inc(mark(done), 1)

            pe.wait_ge(*at("consts"))
            pe.wait_ge(*at("w_in", 16))
            for k in range(2):
                for n in range(4):
                    ins = turn(PS[:, k, n * P:(n + 1) * P], w[:, 4 * k + n, :])
                ins.then_inc(mark("wT_ps"), 1)
            pe.wait_ge(*at("wT", 2))
            pe.wait_ge(*at("wbar"))

            w_in_T = wT[:, W_IN:W_IN + H, :].rearrange("p h d -> p (h d)")

            def turn_x(G1, c1):
                pe.wait_ge(*at("k_x", G1 + 1))
                if not isinstance(G1, int) or G1 > 0:
                    pe.wait_ge(*at("msum", G1))
                for j in range(NQ):
                    ins = turn(PS[:, 0, j * P:(j + 1) * P], X[:, c1 % QUADS * NQ + j, :])
                ins.then_inc(mark("xt_ps"), 1)

            def sums(b, c, j):
                t = c * NQ + j
                pe.wait_ge(*at("y", b * KT + (t + 1)))
                if t == 0:
                    pe.wait_ge(*at("a_ev", b))
                    pe.wait_ge(*at("t_ev", b))
                xr = X[:, t, :]
                mm(PS[:, 7, 0:H + 1], xr, kr[:, c % 2, j, :], t == 0, t == KT - 1)
                mm(PS[:, 5, :], xr, Y[:, j, 0:512], t == 0, t == KT - 1)
                mm(PS[:, 6, :], xr, Y[:, j, 512:1024], t == 0, t == KT - 1).then_inc(mark("a_ps"), 1)

            def project(b, c, j):
                t = c * NQ + j
                if not (isinstance(b, int) and t < 2):
                    pe.wait_ge(*at("sq", b * KT + (t - 1)))
                xt_j = XT[:, c % 2, j * P:(j + 1) * P]
                f0 = 1 + 2 * (j % 2)
                mm(PS[:, f0, :], xt_j, w_in_T[:, 0:512])
                mm(PS[:, f0 + 1, :], xt_j, w_in_T[:, 512:1024]).then_inc(mark("f_ps"), 1)

            def step(b, c, prev, cur, nxt):
                G0 = b * QUADS + c
                if cur:
                    pe.wait_ge(*at("xt", G0 + 1))
                    for n in range(NQ):
                        ins = mm(PS[:, 0, n * H:(n + 1) * H], XT[:, c % 2, n * P:(n + 1) * P], wbar[:, :])
                    ins.then_inc(mark("mean_ps"), 1)
                    project(b, c, 0)
                    project(b, c, 1)
                if prev:
                    sums(b, c - 1, 0)
                if cur:
                    project(b, c, 2)
                if prev:
                    sums(b, c - 1, 1)
                if cur:
                    project(b, c, 3)
                if nxt:
                    turn_x(G0 + 1, c + 1)
                if prev:
                    sums(b, c - 1, 2)
                    sums(b, c - 1, 3)

            turn_x(0, 0)
            phase_a(pe, step)

            pe.wait_ge(*at("w_all", 16 * 16))
            for k in range(2, 7):
                if k >= 4:
                    pe.wait_ge(*at("wT", k - 1))
                for n in range(4):
                    if 4 * k + n < NW:
                        ins = turn(PS[:, k % 2, n * P:(n + 1) * P], w[:, 4 * k + n, :])
                ins.then_inc(mark("wT_ps"), 1)
            pe.wait_ge(*at("a_ev", B))
            pe.wait_ge(*at("t_ev", B))
            turn_rows(xn, 2, "xq", "xq_T_ps")
            turn(PS[:, 3, 0:E], small[0:E, 0, :], E)
            turn(PS[:, 3, E:E + 3], small[0:3, 1, :], 3).then_inc(mark("small_ps"), 1)
            pe.wait_ge(*at("xq_T"))
            for b in range(B):
                if b >= 2:
                    pe.wait_ge(*at("fq", b - 1))
                for n in range(2):
                    ins = mm(PS[:, 4 + 2 * (b % 2) + n, :], xnT[:, b * S:(b + 1) * S],
                             w_in_T[:, n * 512:(n + 1) * 512])
                ins.then_inc(mark("fq_ps"), 1)

            pe.wait_ge(*at("wT", 7))
            pe.wait_ge(*at("small_cp"))
            for b in range(B):
                pe.wait_ge(*at("qc", b + 1))
                for h in range(H):
                    qc = sqb[:, h * D:(h + 1) * D]
                    ins = mm(PS[:, 6 + h // 4, (h % 4) * D:(h % 4 + 1) * D], qc, qc,
                             b == 0 and h % 4 == 0, b == B - 1)
                ins.then_inc(mark("cov_b"), 1)
            pe.wait_ge(*at("fq_unit", B))
            for h in range(H):
                if h >= 2:
                    pe.wait_ge(*at("fqT", h - 1))
                for b in range(B):
                    ins = turn(PS[:, h % 2, b * S:(b + 1) * S], fq[:, b, h * D:(h + 1) * D])
                ins.then_inc(mark("fqT_ps"), 1)
            for h in range(H):
                ins = mm(PS[:, 4 + h // 4, (h % 4) * D:(h % 4 + 1) * D], w[:, W_IN + h, :], wT[:, W_OUT + h, :])
            ins.then_inc(mark("comb_ps"), 1)
            pe.wait_ge(*at("covsum"))
            mm(PS[0:8, 3, 300:301], covsum[:, :], ones[:, 0:1]).then_inc(mark("cov_tot"), 1)
            pe.wait_ge(*at("meanx"))
            pe.wait_ge(*at("cov_ss"))
            for a in range(2):
                for h in range(H):
                    ins = mm(PS[:, 3, a * H + h:a * H + h + 1], wT[:, W_IN + h, :], meanx[:, a:a + 1])
            ins.then_inc(mark("feats_ps"), 1)
            pe.wait_ge(*at("feats"))
            mm(PS[0:8, 3, 128:256], feats[:, 0:H], wT[:, WP1, :], True, False)
            mm(PS[0:8, 3, 128:256], feats[:, H:2 * H], wT[:, WP1 + 1, :], False, True).then_inc(mark("h1_ps"), 1)
            pe.wait_ge(*at("h1"))
            turn(PS[:, 3, 256:256 + H], h8[:, 2, :], 8).then_inc(mark("h1T_ps"), 1)
            pe.wait_ge(*at("h1T"))
            mm(PS[0:8, 3, 310:313], h1T[:, :], wp2T[:, :]).then_inc(mark("wp_ps"), 1)
            pe.wait_ge(*at("coef8"))
            mm(PS[:, 3, 320:320 + H], sm8[:, 11:12].to_broadcast([8, P]), ident[0:8, 0:8])
            mm(PS[:, 3, 320 + H:320 + 2 * H], sm8[:, 10:11].to_broadcast([8, P]), ident[0:8, 0:8]) \
                .then_inc(mark("coef_ps"), 1)
            pe.wait_ge(*at("coef"))
            pe.wait_ge(*at("comb", 2))

            def z_of(h):
                if h >= 2:
                    pe.wait_ge(*at("zt", h - 1))
                pe.wait_ge(*at("fqT", h + 1 if h > 0 else H))
                mm(PS[:, 2 + h % 2, :], w[:, W_IN + h, :], fqT[:, h, :]).then_inc(mark("zt_ps"), 1)

            def out_of(h):
                pe.wait_ge(*at("u", h + 1))
                for b, bank in enumerate((0, 1, 4, 5)):
                    ins = mm(PS[:, bank, 0:D], tmpU[:, h % 2, b * S:(b + 1) * S], comb[:, h, :], h == 0, h == H - 1)
                ins.then_inc(mark("out0_ps"), 1)

            z_of(0)
            for h in range(H):
                if h + 1 < H:
                    z_of(h + 1)
                pe.wait_ge(*at("zt", h + 1))
                if h >= 1:
                    pe.wait_ge(*at("u", h))
                for b in range(B):
                    mm(PS[:, 6, b * S:(b + 1) * S], a_all[:, b, h * D:(h + 1) * D], zt[:, h % 2, b * S:(b + 1) * S])
                    ins = mm(PS[:, 7, b * S:(b + 1) * S],
                             qratio[:, b * H + h:b * H + h + 1].to_broadcast([P, P]), ident[:, :])
                ins.then_inc(mark("u_ps"), 1)
                if h >= 1:
                    out_of(h - 1)
            out_of(H - 1)
            pe.wait_ge(*at("x1"))

            for n in range(B * KT // 8):
                if n % 2 == 0:
                    pe.wait_ge(*at("maskb", n // 2 + 1))
                if n >= 2:
                    pe.wait_ge(*at("maskT", n - 1))
                pb = PS[:, 6 + n % 2, :].bitcast(BF16)
                for a in range(8):
                    k0 = (n % 2 * 8 + a) * P
                    ins = pe.transpose(pb[:, a * P:(a + 1) * P], maskb[:, n // 2, k0:k0 + P], identb[:, :])
                ins.then_inc(mark("maskT_ps"), 1)
            pe.wait_ge(*at("maskT", B * KT // 8))

            turn_rows(xn, 0, "ln1", "ln1_T_ps")
            pe.wait_ge(*at("ln1_T"))
            mm(PS[:, 1, :], wT[:, WQ, :], xnT[:, :])
            mm(PS[:, 2, :], wT[:, WK, :], xnT[:, :]).then_inc(mark("qk_ps"), 1)
            for b in range(B):
                ins = mm(PS[:, 3, b * D:(b + 1) * D], xnT[:, b * S:(b + 1) * S], wT[:, WV, :])
            ins.then_inc(mark("v_ps"), 1)
            pe.wait_ge(*at("qk"))
            for b in range(B):
                ins = mm(PS[:, 4, b * S:(b + 1) * S], qT[:, b * S:(b + 1) * S], kT[:, b * S:(b + 1) * S])
            ins.then_inc(mark("sc_ps"), 1)
            turn_rows(sc, 0, "probs", "pT_ps")
            pe.wait_ge(*at("pT"))
            pe.wait_ge(*at("v0"))
            for b in range(B):
                ins = mm(PS[:, 1, b * S:(b + 1) * S], vv[:, b, :], pT[:, b * S:(b + 1) * S])
            ins.then_inc(mark("oT_ps"), 1)
            pe.wait_ge(*at("oT"))
            for b in range(B):
                ins = mm(PS[:, 2, b * D:(b + 1) * D], oT[:, b * S:(b + 1) * S], wT[:, WO, :])
            ins.then_inc(mark("o0_ps"), 1)

            def route(name, weights):
                for b in range(B):
                    ins = mm(PS[:, 1, b * E:(b + 1) * E], xnT[:, b * S:(b + 1) * S], weights)
                ins.then_inc(mark(name + "_ps"), 1)

            def expert_rows(par, done):
                for b in range(B):
                    for c in range(FC):
                        ins = mm(PS[:, 6 + par, b * D:(b + 1) * D],
                                 hT[:, par, c * B * S + b * S:c * B * S + (b + 1) * S],
                                 w2T[:, par, c * D:(c + 1) * D], c == 0, c == FC - 1)
                ins.then_inc(mark(done), 1)

            turn_rows(xn, 0, "ln2", "ln2_T_ps")
            pe.wait_ge(*at("ln2_T"))
            route("r0", rwT[:, :])
            pe.wait_ge(*at("acc0"))
            with pe.Fori(0, E // 2) as i:
                for p in range(2):
                    pe.wait_ge(*at("w1_0_%d" % p, i * 16 + 16))
                    pe.wait_ge(*at("e0_T%d" % (1 - p), i * 2 + 2 * p))
                    for c in range(FC):
                        ins = turn(PS[:, 0, c * P:(c + 1) * P], raw1[:, p, c * P:(c + 1) * P])
                    ins.then_inc(mark("e0_T_ps"), 1)
                    pe.wait_ge(*at("w2_0_%d" % p, i * 16 + 16))
                    for c in range(FC):
                        ins = turn(PS[:, 1, c * P:(c + 1) * P], raw2[:, p, c * P:(c + 1) * P])
                    ins.then_inc(mark("e0_T_ps"), 1)
                    pe.wait_ge(*at("e0_T%d" % p, i * 2 + 2))
                    pe.wait_ge(*at("e0_h", i * 2 * FC + p * FC))
                    for c in range(FC):
                        mm(PS[:, 2 + c, :], w1T[:, p, c * P:(c + 1) * P], xnT[:, :]).then_inc(mark("e0_h_ps"), 1)
                    pe.wait_ge(*at("e0_h", i * 2 * FC + (p + 1) * FC))
                    pe.wait_ge(*at("e0_add%d" % p, i))
                    expert_rows(p, "e0_y%d" % p)

            pe.wait_ge(*at("x3"))

            def turn_keys(b, n):
                pe.wait_ge(*at("cx2", b * (16 * QUADS) + 16 * QUADS))
                pe.wait_ge(*at("ct_lo", b * QUADS + n))
                for a in range(NQ):
                    ins = turn(PS[:, 4, a * P:(a + 1) * P], cx2[:, n * NQ + a, :])
                ins.then_inc(mark("ct_ps"), 1)

            pe.wait_ge(*at("qpack"))
            for k in range(4):
                for a in range(4):
                    ins = turn(PS[:, k, a * P:(a + 1) * P], qpack[:, 4 * k + a, :])
                ins.then_inc(mark("qTall_ps"), 1)
            for n in range(QUADS):
                turn_keys(0, n)
            pe.wait_ge(*at("ct_lo", QUADS))
            pe.wait_ge(*at("qTall", 4))

            def scores_for_max(C0, par, g, c):
                if not (static(C0) and C0 + c < 2):
                    pe.wait_ge(*at("smx", C0 + c - 1))
                j, k0 = c // HC, c % HC * 512
                mm(PS[:, 4 + c % 2, :], qp1[:, par, j * S:(j + 1) * S], kp[:, g, k0:k0 + 512]) \
                    .then_inc(mark("smx_ps"), 1)

            def scores(b, g, t, beside):
                U = b * G + g
                N = U * (KT // 2) + t
                if t == 0:
                    pe.wait_ge(*at("qp2", U + 1))
                if not (static(N) and N < 2):
                    pe.wait_ge(*at("pexp", N - 1))
                for a in range(2):
                    kt = 2 * t + a
                    bank = 2 * (t % 2) + a
                    ins = mm(PS[:, bank, :], kp[:, g % G, kt * P:(kt + 1) * P], qp2[:, g % 2, :], True, False)
                    if kt == KT - 1:
                        ins.then_inc(mark("st_unit%d" % (g % G)), 1)
                    ins = mm(PS[:, bank, :].rearrange("p (j q) -> p j q", j=HG), identb[:, :],
                             maskT[:, bass.ds((b + g // G) * KT + kt, 1), :].to_broadcast([P, HG, S]), False, True)
                    if a == 0:
                        beside()
                ins.then_inc(mark("st_ps"), 1)

            def weigh(b, g, t, beside):
                U = b * G + g
                N = U * (KT // 2) + t
                if t == 0:
                    pe.wait_ge(*at("vaug", U + 1))
                    if not (static(U) and U < 2):
                        pe.wait_ge(*at("orow", U - 1))
                dst = PS[0:2 * HG * VC, 6 + g % 2, :]
                pe.wait_ge(*at("phi", N + 1))
                for a in range(2):
                    mm(dst, vaug[:, g % G, 2 * t + a, :], p_hi[:, t % 2, a * HG * S:(a + 1) * HG * S],
                       t == 0 and a == 0, False)
                beside()
                for a, made in enumerate(("plo_dve", "plo_pool")):
                    pe.wait_ge(*at(made, N + 1))
                    ins = mm(dst, vaug[:, g % G, 2 * t + a, :], p_lo[:, t % 2, a * HG * S:(a + 1) * HG * S],
                             False, t == KT // 2 - 1 and a == 1)
                ins.then_inc(mark("pv"), 1)

            def unit(b, g):
                U = b * G + g
                cur = not (static(b) and b == B - 1 and g == G)
                prev = not (static(b) and g == 0)
                follow = cur and not (static(b) and b == B - 1 and g == G - 1)
                keys = not static(b) and g == 1
                g1 = (g + 1) % G
                done = [0]

                def chunk(t):
                    c = done[0]
                    if not follow or c >= sum(CHUNKS[:t + 1]):
                        return
                    if c == 0:
                        pe.wait_ge(*at("kp%d" % g1, (b + (g + 1) // G) * (16 * 3 * HG) + 16 * 3 * HG))
                        pe.wait_ge(*at("qp1", U + 2))
                        pe.wait_ge(*at("qp2", U + 1))
                    if keys and KEYS_AT < t <= KEYS_AT + QUADS and c == sum(CHUNKS[:t]):
                        pe.wait_ge(*at("ct_lo", (b + 1) * QUADS + t - KEYS_AT))
                    scores_for_max((U + 1) * HC * HG, (g + 1) % 2, g1, c)
                    done[0] += 1

                for t in range(KT // 2):
                    def beside():
                        chunk(t)

                    if prev and t == 0:
                        weigh(b, g - 1, KT // 2 - 2, lambda: None)
                    if cur:
                        scores(b, g, t, beside)
                        beside()
                    if t >= 2:
                        if cur:
                            weigh(b, g, t - 2, beside)
                    elif prev and t == 1:
                        weigh(b, g - 1, KT // 2 - 1, beside)
                    beside()
                    if follow and t == 7:
                        pe.wait_ge(*at("nm", U + 2))
                        turn(PS[:, 4, 0:P], nm[:, :]).then_inc(mark("nmT_ps"), 1)
                    if prev and t == 3:
                        pe.wait_ge(*at("o_t", U))
                        for j in range(HG):
                            ins = turn(PS[:, 6 + (g - 1) % 2, j * 2 * HG * VC:(j + 1) * 2 * HG * VC],
                                       o_t[0:2 * HG * VC, j * S:(j + 1) * S], 2 * HG * VC)
                        ins.then_inc(mark("o_t_ps"), 1)
                    if keys and KEYS_AT <= t < KEYS_AT + QUADS:
                        pe.wait_ge(*at("smx", (U + 1) * HC * HG + done[0]))
                        turn_keys(b + 1, t - KEYS_AT)
                assert not follow or done[0] == HC * HG

            pe.wait_ge(*at("kp0", 16 * 3 * HG))
            pe.wait_ge(*at("qp1"))
            for c in range(HC * HG):
                scores_for_max(0, 0, 0, c)
            pe.wait_ge(*at("nm"))
            turn(PS[:, 4, 0:P], nm[:, :]).then_inc(mark("nmT_ps"), 1)
            phase_c(pe, unit)
            pe.wait_ge(*at("orow", B * G))
            for b in range(B):
                ins = turn(PS[:, 0, b * S:(b + 1) * S], orow[:, b, :])
            ins.then_inc(mark("xo_T_ps"), 1)
            pe.wait_ge(*at("xo_T"))
            for b in range(B):
                ins = mm(PS[:, 1, b * D:(b + 1) * D], oT[:, b * S:(b + 1) * S], wT[:, WFC, :])
            ins.then_inc(mark("fc_ps"), 1)

            turn_rows(xn, 0, "ln4", "ln4_T_ps")
            pe.wait_ge(*at("ln4_T"))
            for bank, n, name in ((1, WQ1, "rms_q_ps"), (2, WV1, "rms_v_ps")):
                for b in range(B):
                    ins = mm(PS[:, bank, b * D:(b + 1) * D], xT1[:, b * S:(b + 1) * S], wT[:, n, :])
                ins.then_inc(mark(name), 1)
            turn_rows(q1r, 3, "rms_q", "q1_T_ps")
            pe.wait_ge(*at("q1_T"))
            pe.wait_ge(*at("rms_v"))
            for b in range(B):
                pe.wait_ge(*at("qbd", b + 1))
                if b >= 1:
                    pe.wait_ge(*at("s1", b))
                for k in range(4):
                    ins = mm(PS[:, 4 + k, :], xT1[:, b * S:(b + 1) * S],
                             qbd[:, 4 * k:4 * k + 4, :].rearrange("p h q -> p (h q)"))
                ins.then_inc(mark("s1_ps"), 1)
                pe.wait_ge(*at("s1", b + 1))
                for h in range(NH):
                    ins = mm(PS[:, 0, b * D + h * HD:b * D + (h + 1) * HD], sT1[:, b % 2, h * S:(h + 1) * S],
                             v1r[:, b, h * HD:(h + 1) * HD])
                ins.then_inc(mark("o1_ps"), 1)

            turn_rows(xn, 0, "ln5", "ln5_T_ps")
            pe.wait_ge(*at("ln5_T"))
            route("r1", rw1[:, :])
            pe.wait_ge(*at("acc1"))
            with pe.Fori(0, E // 2) as i:
                for p in range(2):
                    pe.wait_ge(*at("w1_1_%d" % p, i * 16 + 16))
                    pe.wait_ge(*at("w2_1_%d" % p, i * 16 + 16))
                    for c in range(FC):
                        n = p * FC + c
                        pe.wait_ge(*at("e1_h", i * 2 * FC + max(n - 1, 0)))
                        mm(PS[:, 2 * (c % 2), :], wide1[:, p, c * P:(c + 1) * P], xnT[:, :])
                        mm(PS[:, 2 * (c % 2) + 1, :], wide1[:, p, (FC + c) * P:(FC + c + 1) * P], xnT[:, :]) \
                            .then_inc(mark("e1_h_ps"), 1)
                    pe.wait_ge(*at("e1_h", i * 2 * FC + (p + 1) * FC))
                    pe.wait_ge(*at("e1_add%d" % p, i))
                    expert_rows(p, "e1_y%d" % p)


_INS = ["x", "ctx_1024", "mask_Bx1xSxS2_ik1", "L0_xattn_ln_g", "L0_xattn_ln_b", "L0_xattn_w_in",
        "L0_xattn_wp_w1", "L0_xattn_wp_b1", "L0_xattn_wp_ln_g", "L0_xattn_wp_ln_b", "L0_xattn_wp_w2",
        "L0_xattn_wp_b2", "L0_xattn_w_out", "L0_xattn_b_out", "L0_attn_Wq", "L0_attn_bq", "L0_attn_Wk",
        "L0_attn_bk", "L0_attn_Wv", "L0_attn_bv", "L0_attn_Wo", "L0_attn_bo", "L0_ffn_router_w",
        "L0_ffn_w1", "L0_ffn_w2", "L1_xattn_W_fc", "L1_xattn_b_fc", "L1_attn_Wq", "L1_attn_Wv",
        "L1_attn_q_norm_w", "L1_attn_v_norm_w", "L1_ffn_router_w", "L1_ffn_router_b", "L1_ffn_w1",
        "L1_ffn_w2"]


def kernel(**inputs):
    import numpy as _np
    import concourse.bacc as _bacc
    from concourse import mybir as _mybir
    from concourse.bass_utils import run_bass_kernel_spmd as _run

    nc = _bacc.Bacc("TRN2", target_bir_lowering=False, num_devices=1)
    arrays, tensors = {}, {}
    for name in _INS:
        a = _np.ascontiguousarray(inputs[name])
        arrays[f"in_{name}"] = a
        tensors[name] = nc.dram_tensor(f"in_{name}", a.shape, _mybir.dt.from_np(a.dtype),
                                       kind="ExternalInput").ap()
    out = nc.dram_tensor("out_x", inputs["x"].shape, _mybir.dt.float32, kind="ExternalOutput").ap()
    perceiver_two_layers(nc, tensors, out)
    r = _run(nc, [arrays], core_ids=[0])
    return r.results[0]["out_x"]
```

```python
from contextlib import ExitStack

import concourse.bass as bass
from concourse import mybir

ALU = mybir.AluOpType
ACT = mybir.ActivationFunctionType
AX = mybir.AxisListType
F32 = mybir.dt.float32
F32R = mybir.dt.float32r
BF16 = mybir.dt.bfloat16
I32 = mybir.dt.int32

P = 128
EPS = 1e-5
RMS_EPS = 1e-8
MASKED = -1e20
LOWEST = -3.0e38


ONCE = {
    "pool": [
        "consts", "ln0_rstd", "ln0b_rstd", "wp_rstd", "ln1_rstd", "kp_ones", "ln2_rstd", "qpack_0",
        "ln3_rstd", "ln4_rstd", "ln5_rstd",
    ],
    "act": [
        "w_hi", "xq_T", "q_norm", "cov_norm", "decorr", "wp_exp", "gauss", "ln1_T", "sc_exp", "pT", "oT",
        "ln2_T", "x2_hi", "r0_exp", "xo_T", "ln4_T", "rms_sd", "q1_T", "ln5_T", "x5_hi", "r1_exp",
    ],
    "dve": [
        "wbar", "wbar_lo", "ln0_var", "ln0", "ln0b_var", "xq", "q_mean", "small_cp", "q_ss", "qratio",
        "covsum", "meanx", "cov_ss", "feats", "wp_var", "h1", "h1T", "wp_logit", "coef8", "coef",
        "gauss_sq", "x1", "ln1_var", "ln1", "qk", "v0", "sc_max", "probs", "ln2_var", "ln2", "x2_lo",
        "r0_max", "x3", "ln3_var", "ln3", "ln4_var", "ln4", "rms_ms", "rms_q", "rms_v", "qbd0", "ln5_var",
        "ln5", "x5_lo", "r1_max", "x6",
    ],
    "pe": [
        "xq_T_ps", "small_ps", "qsum_ps", "comb_ps", "cov_tot", "feats_ps", "h1_ps", "h1T_ps", "wp_ps",
        "coef_ps", "ln1_T_ps", "qk_ps", "v_ps", "sc_ps", "pT_ps", "oT_ps", "o0_ps", "ln2_T_ps", "r0_ps",
        "xo_T_ps", "fc_ps", "ln4_T_ps", "rms_q_ps", "rms_v_ps", "q1_T_ps", "ln5_T_ps", "r1_ps",
    ],
}


START_AT = {
    "pool": {"vaug": 1},
    "act": {"a_ev": 1, "e0_T0": 1, "e0_T1": 1, "e0_h": 1},
    "dve": {"t_ev": 1, "e0_add0": 1, "e0_add1": 1, "e1_add0": 1, "e1_add1": 1, "e1_h": 1, "ct_lo": 1, "smx": 1,
            "orow": 1},
    "pe": {"a_ps": 4, "e0_y0": 1, "e0_y1": 1, "e1_y0": 1, "e1_y1": 1, "ct_ps": 1,
           "st_unit0": 1, "st_unit1": 1, "st_unit2": 1, "st_unit3": 1},
}


class Chain:

    def __init__(self, eng, sem):
        self.eng, self.sem, self.base, self.n = eng, sem, 0, 0

    def __call__(self, ins):
        self.n += 1
        ins.then_inc(self.sem, 1)
        self.eng.wait_ge(self.sem, self.base + self.n)

    def loop(self, i, per):
        self.start = self.base + self.n
        self.base, self.n, self.per = i * per + self.start, 0, per

    def end_loop(self, count):
        assert self.n == self.per, self.n
        self.base, self.n = self.start + count * self.per, 0


def perceiver_two_layers(nc, T, out):
    x_d, ctx_d, mask_d = T["x"], T["ctx_1024"], T["mask_Bx1xSxS2_ik1"]
    B, S, D = x_d.shape
    S2 = ctx_d.shape[1]
    assert S == P and D == P
    H = T["L0_xattn_w_in"].shape[0] // D
    KT = S2 // P
    NQ = 4
    QUADS = KT // NQ
    NH = T["L1_attn_q_norm_w"].shape[0]
    HD = D // NH
    G = 4
    HG = NH // G
    VC = HD + 1
    E = T["L0_ffn_router_w"].shape[0]
    FC = T["L0_ffn_w1"].shape[1] // P
    assert QUADS == 4 and G == 4 and HG == 4 and FC == 4 and H == 8 and B == 4

    ctx_stack = ExitStack()
    with ctx_stack as stack:
        def sb(name, shape, dt=F32):
            return stack.enter_context(nc.sbuf_tensor("sb_" + name, shape, dt))

        sems = {}

        def sem(name):
            if name not in sems:
                sems[name] = stack.enter_context(nc.semaphore("s_" + name))
            return sems[name]

        once = {}
        for who, names in ONCE.items():
            for n, name in enumerate(names):
                once[name] = (who, n + 1)
        start_at = {name: n for signals in START_AT.values() for name, n in signals.items()}

        def start(eng, who):
            for name, n in START_AT[who].items():
                eng.sem_inc(sem(name), n)

        given = {who: 0 for who in ONCE}

        def at(name, value=1):
            if name in once:
                who, n = once[name]
                return sem(who + "_once"), n
            return sem(name), value + start_at.get(name, 0)

        def mark(name):
            if name not in once:
                return sem(name)
            who, n = once[name]
            given[who] += 1
            assert given[who] == n, (name, n, given[who])
            return sem(who + "_once")

        PS = stack.enter_context(nc.psum_tensor("banks", [P, 8, 512], F32))

        ident = sb("ident", [P, P])
        identb = sb("identb", [P, P], BF16)
        offdiag = sb("offdiag", [P, P])
        ones = sb("ones", [P, P])
        neghalf = sb("neghalf", [P, B * NH])
        groupmask = sb("groupmask", [P, HG])
        headmask = sb("headmask", [P, NH])
        causal = sb("causal", [P, P])
        lastfirst = sb("lastfirst", [P, E])
        gauss = sb("gauss", [P, S])

        W_IN, W_OUT, WQ, WK, WV, WO, WFC, WQ1, WV1, WP1, NW = 0, H, 2 * H, 2 * H + 1, 2 * H + 2, 2 * H + 3, \
            2 * H + 4, 2 * H + 5, 2 * H + 6, 2 * H + 7, 2 * H + 9
        w = sb("w", [P, NW, P])
        wT = sb("wT", [P, NW, P])
        small = sb("small", [32, 2, P])
        rwT = sb("rwT", [P, E])
        wp2T = sb("wp2T", [P, 3])
        rw1 = sb("rw1", [P, E])
        wbar = sb("wbar", [P, H])
        G_, B_, BOUT, BV, BO, BFC, QW, VW, WPB1, WPG, WPB, NB = range(12)
        rows = sb("rows", [P, NB, P])
        wpb2 = sb("wpb2", [P, 3])
        rb1 = sb("rb1", [P, E])
        bcol = sb("bcol", [P, 2])

        xs = sb("xs", [P, B, D])
        xn = sb("xn", [P, B, D])
        xnT = sb("xnT", [P, B * S])
        stats = sb("stats", [P, B, 6])
        mv = sb("mv", [P, B, 2])
        vpe = sb("vpe", [P, B])
        rstd = sb("rstd", [P, B])

        vaug = sb("vaug", [P, G, KT, 2 * HG * VC], F32R)
        ctxT_hi = sb("ctxT_hi", [P, S2], F32R)
        ctxT_lo = sb("ctxT_lo", [P, S2], F32R)
        kp = sb("kp", [P, G, S2], F32R)
        a_all = sb("a_all", [P, B, H * D])
        maskb = a_all[:, :, :].rearrange("p b n -> p (b n)").bitcast(BF16) \
            .rearrange("p (b n) -> p b n", b=B)
        mnow = sb("mnow", [P, S2], BF16)
        mnext = sb("mnext", [P, S2], BF16)
        maskT = sb("maskT", [P, B * KT, S], BF16)

        ARENA = 7936
        arena = sb("arena", [P, ARENA])
        used = [0]

        def view(shape, dims=None):
            n = 1
            for s in shape:
                n *= s
            a = arena[:, used[0]:used[0] + n]
            used[0] += n
            assert used[0] <= ARENA, used[0]
            if len(shape) == 2:
                a = a.rearrange("p (a b) -> p a b", b=shape[1])
            if len(shape) == 3:
                a = a.rearrange("p (a b c) -> p a b c", b=shape[1], c=shape[2])
            return a

        t_all = sb("t_all", [P, B, H + 1])

        mask_i = [ctxT_lo[:, :].bitcast(I32), ctxT_hi[:, :].bitcast(I32)]
        used[0] = 0
        cx = ctxT_hi[:, :].bitcast(F32).rearrange("p (t d) -> p t d", d=D)
        X = view([KT, D])
        kp_f = kp[:, :, :].rearrange("p g n -> p (g n)")
        XT_hi = kp_f[:, 0:2 * NQ * P].rearrange("p (a n) -> p a n", a=2)
        XT_lo = kp_f[:, 2 * NQ * P:4 * NQ * P].rearrange("p (a n) -> p a n", a=2)
        w_hi = kp_f[:, 4 * NQ * P:4 * NQ * P + H * D]
        w_lo = kp_f[:, 4 * NQ * P + H * D:4 * NQ * P + 2 * H * D]
        wbar_hi = kp_f[:, 4 * NQ * P + 2 * H * D:4 * NQ * P + 2 * H * D + H]
        wbar_lo = kp_f[:, 4 * NQ * P + 2 * H * D + H:4 * NQ * P + 2 * H * D + 2 * H]
        wbar_parts = kp_f[:, 4 * NQ * P + 2 * H * D:4 * NQ * P + 2 * H * D + 2 * H]
        maskT_f = maskT[:, :, :].rearrange("p a n -> p (a n)").bitcast(F32)
        sq = maskT_f[:, 0:2 * H * D].rearrange("p (a n) -> p a n", a=2)
        Y = view([NQ, H * D])
        kst = sb("kst", [P, NQ, 6])
        kmv = sb("kmv", [P, NQ, 2])
        kvpe = sb("kvpe", [P, NQ])
        krstd = sb("krstd", [P, NQ])
        ss = sb("ss", [P, NQ, H])
        kw = sb("kw", [P, NQ, H])
        msum = sb("msum", [P, 2, NQ, H])
        kt1 = sb("kt1", [P, NQ, H])
        kt2 = sb("kt2", [P, NQ, H])
        kr = sb("kr", [P, 2, NQ, H + 1])
        used[0] = 0
        fq = view([B, H * D])
        fqT = maskT_f.rearrange("p (h n) -> p h n", h=H)
        qc = view([2, H * D])
        sqb = qc[:, 0, :]
        q_sq = [mnow[:, :].bitcast(F32), mnext[:, :].bitcast(F32)]
        tmpU = mnext[:, :].bitcast(F32).rearrange("p (a n) -> p a n", a=2)
        qsum = sb("qsum", [P, B * H])
        qss = sb("qss", [P, B * H])
        qinv = sb("qinv", [P, B * H])
        qratio = sb("qratio", [P, B * H])
        q1 = sb("q1", [P, B * H])
        q2 = sb("q2", [P, B * H])
        covsum = sb("covsum", [P, H])
        meanx = sb("meanx", [P, 2])
        feats = sb("feats", [P, 2 * H])
        h8 = sb("h8", [8, 3, P])
        h8s = sb("h8s", [8, 6])
        h8m = sb("h8m", [8, 2])
        h8r = sb("h8r", [8, 2])
        h1T = sb("h1T", [P, H])
        sm8 = sb("sm8", [8, 16])
        coef = sb("coef", [P, 2 * H])
        wt_t = sb("wt_t", [P, B, H])
        comb = mnow[:, :].bitcast(F32).rearrange("p (h d) -> p h d", d=D)
        used[0] = 0
        qT = view([B * S])
        kT = view([B * S])
        vv = view([B, D])
        sc = view([B, S])
        pT = view([B * S])
        oT = view([B * S])
        used[0] = 0
        q1r = view([B, D])
        v1r = view([B, D])
        t1r = view([B, D])
        xT1 = view([B * S])
        qT1 = view([B * S])
        qbd = view([2, NH * S])
        own = view([HG * S])
        o1s = view([S])
        pairmask = view([HG])
        q_ms = view([2 * B * NH])
        q_rms = view([2 * B * NH])
        sT1 = maskT_f.rearrange("p (a n) -> p a n", a=2)
        used[0] = 0
        w_f = w[:, 0:2 * H, :].rearrange("p a n -> p (a n)")
        raw1 = w_f[:, 0:2 * FC * P].rearrange("p (a n) -> p a n", a=2)
        raw2 = w_f[:, 2 * FC * P:4 * FC * P].rearrange("p (a n) -> p a n", a=2)
        w2T = mnext[:, :].bitcast(F32).rearrange("p (a n) -> p a n", a=2)
        hT = view([2, FC * B * S])
        acc = view([B * D])
        ytmp = xn[:, :, :].rearrange("p b d -> p (b d)")
        sil = view([2, B * S])
        w2_all = a_all[:, :, :].rearrange("p b (e n) -> p (b e) n", n=FC * D)
        wide1 = w_f.rearrange("p (a n) -> p a n", a=2)
        WF = 2 * FC * P
        wide_hi = kp_f[:, 0:2 * WF].rearrange("p (a n) -> p a n", a=2)
        wide_lo = kp_f[:, 2 * WF:4 * WF].rearrange("p (a n) -> p a n", a=2)
        x5_hi = kp_f[:, 4 * WF:4 * WF + B * S]
        x5_lo = kp_f[:, 4 * WF + B * S:4 * WF + 2 * B * S]
        warm = sb("warm", [P, 3])
        gate = sb("gate", [P, 4])
        HC = S2 // 512
        mx = sb("mx", [P, HC * HG])
        s4 = sb("s4", [P, B])
        r4 = sb("r4", [P, B])
        lg = sb("lg", [P, B, E])
        pr = sb("pr", [P, B, E])
        oh = sb("oh", [P, B, E])
        oh2 = sb("oh2", [P, B, E])
        wgt = sb("wgt", [P, E, B])
        used[0] = 0
        pexp = w_f.rearrange("p (a n) -> p a n", a=2)
        junk = [view([512]), xn[:, :, :].rearrange("p b d -> p (b d)")]
        o_t = view([HG * S])
        p_hi = sb("p_hi", [P, 2, 2 * HG * S], F32R)
        p_lo = sb("p_lo", [P, 2, 2 * HG * S], F32R)
        w1T_hi, w1T_lo = (p_hi[:, a, :].rearrange("p (a n) -> p a n", a=2) for a in range(2))
        x2_hi, x2_lo = (p_lo[:, 0, a * B * S:(a + 1) * B * S] for a in range(2))
        qpack = view([G * B, P])
        qTall = view([G * B, S])
        nm = view([P])
        qs2 = view([P])
        orow = view([B, D])
        cx2 = view([KT, D])
        q_one = orow.rearrange("p b d -> p (b d)")
        rec4 = sb("rec4", [P, HG])
        osum = sb("osum", [P, HG, VC])
        nmax = sb("nmax", [P, HG])
        qp1 = sb("qp1", [P, 2, HG * S], F32R)
        qp2 = sb("qp2", [P, 2, HG * S], F32R)

        block = stack.enter_context(nc.Block())

        def bc(ap, shape):
            return ap.to_broadcast(shape)

        def phase_a(eng, step, chain=None, links=0):
            step(0, 0, False, True, True)
            with eng.Fori(0, B - 1) as b:
                if chain:
                    chain.loop(b, links)
                for c in range(1, QUADS + 1):
                    step(b, c, True, True, True)
                if chain:
                    chain.end_loop(B - 1)
            for c in range(1, QUADS + 1):
                step(B - 1, c, True, c < QUADS, c < QUADS - 1)

        def phase_c(eng, unit, chain=None, links=0):
            unit(0, 0)
            with eng.Fori(0, B - 1) as b:
                if chain:
                    chain.loop(b, links)
                for g in range(1, G + 1):
                    unit(b, g)
                if chain:
                    chain.end_loop(B - 1)
            for g in range(1, G + 1):
                unit(B - 1, g)

        def experts(eng, step, chain=None):
            step(0, 0)
            with eng.Fori(0, E // 2 - 1) as i:
                if chain:
                    chain.loop(i, 2)
                step(i, 1)
                step(i, 2)
                if chain:
                    chain.end_loop(E // 2 - 1)
            step(E // 2 - 1, 1)
            step(E // 2 - 1, 2)

        def stage(i, p):
            return not (static(i) and i * 2 + p == E), not (static(i) and i * 2 + p == 0)

        Z_BANKS = (2, 4, 5)
        U_BANKS = ((6, 7), (2, 3))

        def static(b):
            return isinstance(b, int)

        def quad_after(b, c):
            return not (static(b) and b * QUADS + c + 2 >= B * QUADS)

        def key_bank(b, n):
            return 6 + n % 2 if static(b) else 6

        CHUNKS = [3, 3, 3, 2, 2, 2, 1, 0]
        KEYS = {(1, 5): 0, (1, 6): 1, (1, 7): 2, (2, 0): 3}

        def head_blocks(eng, b):
            return eng.tensor_tensor(qbd[:, b % 2, :].rearrange("p (h q) -> p h q", q=S),
                                     bc(qT1[:, b * S:(b + 1) * S].unsqueeze(1), [P, NH, S]),
                                     bc(headmask[:, :].unsqueeze(2), [P, NH, S]), ALU.mult)

        def row_of(name):
            return T[name].rearrange("(a n) -> a n", a=1)

        @block.sync
        def _(sp):
            def load_ctx(b, c):
                sp.dma_start(cx[:, c * NQ:(c + 1) * NQ, :],
                             ctx_d[bass.ds(b, 1), c * NQ * P:(c + 1) * NQ * P, :]
                             .rearrange("a (t p) d -> p (a t) d", p=P)).then_inc(mark("ctx%d" % c), 16)

            load_ctx(0, 0)
            sp.dma_start(w[:, W_IN:W_IN + H, :], T["L0_xattn_w_in"].rearrange("(h d) n -> d h n", h=H)) \
                .then_inc(mark("w_in"), 16)
            for n, name in ((G_, "L0_xattn_ln_g"), (B_, "L0_xattn_ln_b")):
                sp.dma_start(rows[:, n, :], row_of(name).to_broadcast([P, P])).then_inc(mark("gain_in"), 16)
            for c in range(1, QUADS):
                load_ctx(0, c)
            sp.dma_start(xs[:, :, :], x_d.rearrange("b s d -> s b d")).then_inc(mark("x_in"), 16)
            sp.dma_start(w[:, W_OUT:W_OUT + H, :], T["L0_xattn_w_out"].rearrange("n (h d) -> n h d", h=H)) \
                .then_inc(mark("w_all"), 16)
            for n, name in ((WQ, "L0_attn_Wq"), (WK, "L0_attn_Wk"), (WV, "L0_attn_Wv"), (WO, "L0_attn_Wo"),
                            (WFC, "L1_xattn_W_fc"), (WQ1, "L1_attn_Wq"), (WV1, "L1_attn_Wv")):
                sp.dma_start(w[:, n, :], T[name]).then_inc(mark("w_all"), 16)
            sp.dma_start(w[:, WP1:WP1 + 2, :], T["L0_xattn_wp_w1"].rearrange("n (a d) -> n a d", a=2)) \
                .then_inc(mark("w_all"), 16)
            sp.dma_start(small[0:E, 0, :], T["L0_ffn_router_w"]).then_inc(mark("w_all"), 16)
            sp.dma_start(small[0:3, 1, :], T["L0_xattn_wp_w2"]).then_inc(mark("w_all"), 16)
            sp.dma_start(rw1[:, :], T["L1_ffn_router_w"]).then_inc(mark("w_all"), 16)
            for n, name in ((BOUT, "L0_xattn_b_out"),
                            (BV, "L0_attn_bv"), (BO, "L0_attn_bo"), (BFC, "L1_xattn_b_fc"),
                            (WPB1, "L0_xattn_wp_b1"), (WPG, "L0_xattn_wp_ln_g"), (WPB, "L0_xattn_wp_ln_b")):
                sp.dma_start(rows[:, n, :], row_of(name).to_broadcast([P, P])).then_inc(mark("rows_in"), 16)
            for n, name in ((QW, "L1_attn_q_norm_w"), (VW, "L1_attn_v_norm_w")):
                sp.dma_start(rows[:, n, :], T[name].rearrange("(a h) d -> a (h d)", a=1).to_broadcast([P, P])) \
                    .then_inc(mark("rows_in"), 16)
            sp.dma_start(wpb2[:, :], row_of("L0_xattn_wp_b2").to_broadcast([P, 3])).then_inc(mark("w_all"), 16)
            sp.dma_start(rb1[:, :], row_of("L1_ffn_router_b").to_broadcast([P, E])).then_inc(mark("w_all"), 16)
            with nc.allow_non_contiguous_dma(reason="two bias vectors, one element a partition"):
                for n, name in enumerate(("L0_attn_bq", "L0_attn_bk")):
                    sp.dma_start(bcol[:, n:n + 1], T[name].rearrange("(n a) -> n a", a=1)) \
                        .then_inc(mark("w_all"), 16)
            with sp.Fori(1, B) as b:
                for c in range(QUADS):
                    sp.wait_ge(*at("k_row", (b - 1) * QUADS + (c + 1)))
                    load_ctx(b, c)

            def load_mask(b):
                sp.dma_start(mask_i[b % 2], mask_d[b, 0, :, :]).then_inc(mark("mask%d" % b), 16)

            load_mask(0)
            sp.wait_ge(*at("k_row", B * QUADS))
            load_mask(1)

            def load_expert0(e, p):
                sp.dma_start(raw1[:, p, :].rearrange("p (c d) -> p c d", c=FC),
                             T["L0_ffn_w1"][bass.ds(e, 1), :, :]
                             .rearrange("a (c p) d -> p (a c) d", p=P)).then_inc(mark("w1_0_%d" % p), 16)
                sp.dma_start(raw2[:, p, :], T["L0_ffn_w2"][bass.ds(e, 1), :, :]
                             .rearrange("a d n -> d (a n)")).then_inc(mark("w2_0_%d" % p), 16)

            def load_keys(b):
                for c in range(QUADS):
                    sp.dma_start(cx2[:, c * NQ:(c + 1) * NQ, :],
                                 ctx_d[bass.ds(b, 1), c * NQ * P:(c + 1) * NQ * P, :]
                                 .rearrange("a (t p) d -> p (a t) d", p=P)).then_inc(mark("cx2"), 16)

            def build_blocks(g):
                for j in range(HG):
                    for t, src in enumerate((ctxT_hi, ctxT_hi, ctxT_lo)):
                        r = 32 * j + 2 + HD * t
                        k0 = (HG * g + j) * HD
                        sp.dma_start(kp[r:r + HD, g, :].bitcast(F32), src[k0:k0 + HD, :].bitcast(F32)) \
                            .then_inc(mark("kp%d" % g), 16)

            sp.wait_ge(*at("x1"))
            load_keys(0)
            for p in range(2):
                load_expert0(p, p)
            for b in range(2, B):
                sp.wait_ge(*at("maskb", b - 1))
                load_mask(b)
            sp.wait_ge(*at("kp_ones"))
            sp.wait_ge(*at("ct_lo", QUADS))
            for i in range(1, E // 2):
                for p in range(2):
                    sp.wait_ge(*at("e0_T%d" % p, i * 2))
                    load_expert0(i * 2 + p, p)
                build_blocks(i - 1)
            build_blocks(G - 1)
            with sp.Fori(2, B + 1) as b1:
                b = b1 - 1
                sp.wait_ge(*at("ct_ps", b * QUADS))
                sp.wait_ge(*at("vaug", b * G))
                load_keys(b)
                sp.wait_ge(*at("ct_lo", b * QUADS + QUADS))
                for g in range(G):
                    sp.wait_ge(*at("st_unit%d" % g, b))
                    build_blocks(g)
            sp.wait_ge(*at("orow", B * G))

            def load_expert(e, p):
                sp.dma_start(wide1[:, p, :], T["L1_ffn_w1"][bass.ds(e, 1), :, :]
                             .rearrange("a d n -> d (a n)")).then_inc(mark("w1_1_%d" % p), 16)

            for p in range(2):
                load_expert(p, p)
            for n in range(2):
                sp.dma_start(w2_all[:, n * E // 2:(n + 1) * E // 2, :].rearrange("p e (c d) -> p (e c) d", c=FC),
                             T["L1_ffn_w2"][n * E // 2:(n + 1) * E // 2, :, :]
                             .rearrange("e (c p) d -> p (e c) d", p=P)).then_inc(mark("w2_1"), 16)
            with sp.Fori(1, E // 2) as i:
                for p in range(2):
                    sp.wait_ge(*at("e1_lo", i * 2 + p - 1))
                    load_expert(i * 2 + p, p)
            sp.wait_ge(*at("x6"))
            sp.dma_start(out.rearrange("b s d -> s b d"), xs[:, :, :]).then_inc(mark("out"), 16)
            sp.wait_ge(*at("out", 16))

        @block.gpsimd
        def _(pool):
            start(pool, "pool")
            ch = Chain(pool, sem("pool_chain"))
            ch(pool.memset(ident[:, :], 0.0))
            pool.memset(offdiag[:, :], 1.0)
            pool.memset(neghalf[:, :], -0.5)
            pool.memset(ones[:, :], 1.0)
            pool.memset(headmask[:, :], 1.0)
            pool.memset(groupmask[:, :], 0.0)
            ch(pool.memset(causal[:, :], 1.0))
            ch(pool.affine_select(out=ident[:, :], in_=ident[:, :], compare_op=ALU.not_equal, fill=1.0,
                                  base=0, pattern=[[-1, P]], channel_multiplier=1))
            pool.affine_select(out=offdiag[:, :], in_=offdiag[:, :], compare_op=ALU.not_equal, fill=0.0,
                               base=0, pattern=[[-1, P]], channel_multiplier=1)
            pool.affine_select(out=causal[:, :], in_=causal[:, :], compare_op=ALU.is_ge, fill=0.0,
                               base=0, pattern=[[1, P]], channel_multiplier=-1)
            ch(pool.affine_select(out=headmask[:, :], in_=headmask[:, :], compare_op=ALU.is_ge, fill=0.0,
                                  base=0, pattern=[[-HD, NH]], channel_multiplier=1))
            ch(pool.affine_select(out=headmask[:, :], in_=headmask[:, :], compare_op=ALU.is_ge, fill=0.0,
                                  base=HD - 1, pattern=[[HD, NH]], channel_multiplier=-1))
            for j in range(HG):
                ch(pool.memset(groupmask[32 * j:32 * j + 32, j:j + 1], 1.0))
            pool.iota(lastfirst[:, :], pattern=[[-1, E]], base=E, channel_multiplier=0,
                      allow_small_or_imprecise_dtypes=True)
            ch(pool.iota(gauss[:, :], pattern=[[1, S]], base=-(S // 2), channel_multiplier=0,
                         allow_small_or_imprecise_dtypes=True))
            pool.tensor_copy(identb[:, :], ident[:, :]).then_inc(mark("consts"), 1)
            pool.memset(vaug[:, :, :, 0:HG * VC].bitcast(F32), 1.0)
            ch(pool.memset(vaug[:, :, :, HG * VC:2 * HG * VC].bitcast(F32), 0.0))

            def rstd_of(name):
                pool.wait_ge(*at(name + "_var"))
                pool.tensor_tensor(rstd[:, :], vpe[:, :], neghalf[:, 0:B], ALU.pow) \
                    .then_inc(mark(name + "_rstd"), 1)

            pool.wait_ge(*at("gain_in", 32))

            with pool.Fori(0, B) as b:
                ch.loop(b, QUADS)
                for c in range(QUADS):
                    pool.wait_ge(*at("k_row", b * QUADS + (c + 1)))
                    xq = X[:, c * NQ:(c + 1) * NQ, :]
                    ch(pool.tensor_tensor(xq, xq, bc(rows[:, G_:G_ + 1, :], [P, NQ, D]), ALU.mult))
                    pool.tensor_tensor(xq, xq, bc(rows[:, B_:B_ + 1, :], [P, NQ, D]), ALU.add) \
                        .then_inc(mark("k_x"), 1)
                ch.end_loop(B)
            rstd_of("ln0")
            rstd_of("ln0b")
            pool.wait_ge(*at("q_mean"))
            for b in range(B):
                pool.wait_ge(*at("fq", b + 1))
                if b >= 2:
                    pool.wait_ge(*at("cov_b", b - 1))
                pool.tensor_tensor(qc[:, b % 2, :].rearrange("p (h d) -> p h d", h=H),
                                   fq[:, b, :].rearrange("p (h d) -> p h d", h=H),
                                   bc(q1[:, b * H:(b + 1) * H].unsqueeze(2), [P, H, D]), ALU.subtract) \
                    .then_inc(mark("qc"), 1)
            pool.wait_ge(*at("wp_var"))
            pool.tensor_tensor(h8r[:, 0:1], h8m[:, 1:2], neghalf[0:8, 0:1], ALU.pow).then_inc(mark("wp_rstd"), 1)
            ch(pool.memset(kp[:, :, :].bitcast(F32), 0.0))
            for j in range(HG):
                if j == 2:
                    rstd_of("ln1")
                    pool.wait_ge(*at("ln1_rstd"))
                ones_rows = pool.memset(kp[32 * j:32 * j + 2, :, :].bitcast(F32), 1.0)
                if j < HG - 1:
                    ch(ones_rows)
            ones_rows.then_inc(mark("kp_ones"), 1)
            pool.wait_ge(*at("kp_ones"))
            rstd_of("ln2")

            def parts(g):
                src = cx2[:, :, g * HG * HD:(g + 1) * HG * HD].rearrange("p t (j d) -> p t j d", j=HG)
                hi, lo = (vaug[:, g, :, a * HG * VC:(a + 1) * HG * VC]
                          .rearrange("p t (j c) -> p t j c", j=HG)[:, :, :, 0:HD] for a in range(2))
                return src, hi, lo

            def values_hi(g):
                src, hi, lo = parts(g)
                ch(pool.tensor_tensor(hi, src, bc(ones[:, 0:1].unsqueeze(2).unsqueeze(3), [P, KT, HG, HD]),
                                      ALU.mult))

            def values_lo(g):
                src, hi, lo = parts(g)
                pool.tensor_tensor(lo, src, hi.bitcast(F32), ALU.subtract).then_inc(mark("vaug"), 1)

            def unit(b, g):
                cur = not (static(b) and b == B - 1 and g == G)
                if not cur:
                    return
                N0 = (b * G + g) * (KT // 2)
                for t in range(KT // 2):
                    half = slice(HG * S, 2 * HG * S)
                    pool.wait_ge(*at("phi", N0 + t + 1))
                    pool.tensor_tensor(p_lo[:, t % 2, half], pexp[:, t % 2, half],
                                       p_hi[:, t % 2, half].bitcast(F32), ALU.subtract) \
                        .then_inc(mark("plo_pool"), 1)
                    if not static(b) and t == 5:
                        if g == 1:
                            pool.wait_ge(*at("cx2", (b + 1) * (16 * QUADS) + 16 * QUADS))
                        pool.wait_ge(*at("orow", b * G + g))
                        values_hi(g - 1)
                    if not static(b) and t == 6:
                        values_lo(g - 1)

            pool.wait_ge(*at("cx2", 16 * QUADS))
            for g in range(G):
                values_hi(g)
                values_lo(g)
            pool.wait_ge(*at("x3"))
            qpv = qpack[:, :, :].rearrange("p n (j r) -> p (n j) r", j=HG)
            pool.memset(qpv[:, :, 0:2], 0.0)
            pool.memset(qpv[:, :, 2 + 3 * HD:], 0.0).then_inc(mark("qpack_0"), 1)
            rstd_of("ln3")
            phase_c(pool, unit, ch, G)
            rstd_of("ln4")
            pool.wait_ge(*at("q1_T"))
            for b in range(1, B):
                if b >= 2:
                    pool.wait_ge(*at("s1_ps", b - 1))
                head_blocks(pool, b).then_inc(mark("qbd"), 1)
            rstd_of("ln5")

        @block.scalar
        def _(act):
            start(act, "act")

            def copy(dst, src, wait, value, done):
                act.wait_ge(*at(wait, value))
                act.activation(dst, src, ACT.Copy).then_inc(mark(done), 1)

            for k in range(2):
                copy(wT[:, 4 * k:4 * k + 4, :], PS[:, k, :].rearrange("p (a n) -> p a n", a=4),
                     "wT_ps", k + 1, "wT")
            def rows_sd(G1):
                act.wait_ge(*at("k_var", G1 + 1))
                act.activation(krstd[:, :], kvpe[:, :], ACT.Sqrt).then_inc(mark("k_sd"), 1)

            def xt(G1, c1):
                act.wait_ge(*at("xt_ps", G1 + 1))
                act.activation(XT_hi[:, c1 % 2, :], PS[:, 0, :], ACT.Copy).then_inc(mark("xt"), 1)

            def squares(b, c, j):
                t = c * NQ + j
                act.wait_ge(*at("f_ps", b * KT + (t + 1)))
                if not (isinstance(b, int) and t < 2):
                    act.wait_ge(*at("ssum", b * KT + (t - 1)))
                act.activation(sq[:, j % 2, :], PS[:, 1 + 2 * (j % 2):3 + 2 * (j % 2), :]
                               .rearrange("p a n -> p (a n)"), ACT.Square).then_inc(mark("sq"), 1)

            def step(b, c, prev, cur, nxt):
                G0 = b * QUADS + c
                if cur:
                    squares(b, c, 0)
                    squares(b, c, 1)
                if quad_after(b, c):
                    rows_sd(G0 + 2)
                if cur:
                    squares(b, c, 2)
                    squares(b, c, 3)
                if nxt:
                    xt(G0 + 1, c + 1)
                if cur:
                    act.wait_ge(*at("ssum", (G0 + 1) * NQ))
                    act.activation(kw[:, :, :], ss[:, :, :], ACT.Sqrt).then_inc(mark("k_norm"), 1)
                if c == QUADS:
                    act.wait_ge(*at("a_ps", b * KT + KT))
                    act.activation(a_all[:, bass.ds(b, 1), :].rearrange("p a n -> p (a n)"),
                                   PS[:, 5:7, :].rearrange("p a n -> p (a n)"), ACT.Copy).then_inc(mark("a_ev"), 1)

            rows_sd(0)
            act.wait_ge(*at("wT", 2))
            act.activation(w_hi, wT[:, W_IN:W_IN + H, :].rearrange("p h d -> p (h d)"), ACT.Copy) \
                .then_inc(mark("w_hi"), 1)
            xt(0, 0)
            rows_sd(1)
            phase_a(act, step)

            for k in range(2, 7):
                m = min(4, NW - 4 * k)
                copy(wT[:, 4 * k:4 * k + m, :], PS[:, k % 2, 0:m * P].rearrange("p (a n) -> p a n", a=m),
                     "wT_ps", k + 1, "wT")
            copy(xnT[:, :], PS[:, 2, :], "xq_T_ps", 1, "xq_T")
            for b in range(B):
                f_ps = PS[:, 4 + 2 * (b % 2):6 + 2 * (b % 2), :].rearrange("p a n -> p (a n)")
                act.wait_ge(*at("fq_ps", b + 1))
                if b >= 2:
                    act.wait_ge(*at("q_ssum", b - 1))
                act.activation(q_sq[b % 2], f_ps, ACT.Square).then_inc(mark("q_sq"), 1)
                act.activation(fq[:, b, :], f_ps, ACT.Copy).then_inc(mark("fq"), 1)
            act.wait_ge(*at("q_ss"))
            act.activation(qinv[:, :], qss[:, :], ACT.Sqrt).then_inc(mark("q_norm"), 1)
            for h in range(H):
                copy(fqT[:, h, :], PS[:, h % 2, :], "fqT_ps", h + 1, "fqT")
            copy(comb[:, 0:4, :], PS[:, 4, :].rearrange("p (a n) -> p a n", a=4), "comb_ps", 1, "comb")
            copy(comb[:, 4:8, :], PS[:, 5, :].rearrange("p (a n) -> p a n", a=4), "comb_ps", 1, "comb")
            act.wait_ge(*at("cov_ss"))
            act.activation(sm8[:, 2:3], sm8[:, 0:1], ACT.Sqrt).then_inc(mark("cov_norm"), 1)
            act.wait_ge(*at("cov_norm"))
            act.activation(sm8[:, 3:4], sm8[:, 2:3], ACT.Exp, scale=-5.0 / (D * D) / (B * S)) \
                .then_inc(mark("decorr"), 1)
            for h in range(5):
                copy(fqT[:, h, :], PS[:, Z_BANKS[h % 3], :], "zt_ps", h + 1, "zt")
            act.wait_ge(*at("wp_logit"))
            act.activation(sm8[:, 8:11], sm8[:, 4:7], ACT.Exp).then_inc(mark("wp_exp"), 1)
            for h in range(5, H):
                copy(fqT[:, h, :], PS[:, Z_BANKS[h % 3], :], "zt_ps", h + 1, "zt")

            def mask_turned(b):
                for n in (2 * b, 2 * b + 1):
                    copy(maskT[:, 8 * n:8 * n + 8, :],
                         PS[:, 6 + n % 2, :].bitcast(BF16).rearrange("p (a n) -> p a n", a=8),
                         "maskT_ps", n + 1, "maskT")

            def key_hi(b, n):
                if n == 0 and not static(b):
                    for g in range(G):
                        act.wait_ge(*at("kp%d" % g, b * (16 * 3 * HG)))
                act.wait_ge(*at("ct_ps", b * QUADS + (n + 1)))
                act.activation(ctxT_hi[:, n * NQ * P:(n + 1) * NQ * P], PS[:, key_bank(b, n), :], ACT.Copy) \
                    .then_inc(mark("ct_hi"), 1)

            act.wait_ge(*at("gauss_sq"))
            act.activation(gauss[:, :], gauss[:, :], ACT.Exp, scale=-0.5).then_inc(mark("gauss"), 1)
            copy(xnT[:, :], PS[:, 0, :], "ln1_T_ps", 1, "ln1_T")
            mask_turned(0)
            mask_turned(1)
            act.wait_ge(*at("sc_max"))
            act.activation(sc[:, :, :], sc[:, :, :], ACT.Exp).then_inc(mark("sc_exp"), 1)
            mask_turned(2)
            copy(pT[:, :], PS[:, 0, :], "pT_ps", 1, "pT")
            copy(oT[:, :], PS[:, 1, :], "oT_ps", 1, "oT")
            mask_turned(3)
            key_hi(0, 0)
            key_hi(0, 1)

            copy(xnT[:, :], PS[:, 0, :], "ln2_T_ps", 1, "ln2_T")
            copy(x2_hi, PS[:, 0, :], "ln2_T_ps", 1, "x2_hi")
            act.wait_ge(*at("r0_max"))
            act.activation(pr[:, :, :], lg[:, :, :], ACT.Exp).then_inc(mark("r0_exp"), 1)
            key_hi(0, 2)
            key_hi(0, 3)

            act.activation(warm[:, 0:1], ones[:, 0:1], ACT.Gelu)

            def step0(i, p):
                e, par = i * 2 + p, p % 2
                if not stage(i, p)[0]:
                    return
                act.wait_ge(*at("e0_y%d" % par, i + p // 2))
                act.wait_ge(*at("e0_T_ps", e * 2 + 1))
                act.activation(w1T_hi[:, par, :], PS[:, 0, :], ACT.Copy).then_inc(mark("e0_T%d" % par), 1)
                act.wait_ge(*at("e0_T_ps", e * 2 + 2))
                act.activation(w2T[:, par, :], PS[:, 1, :], ACT.Copy).then_inc(mark("e0_T%d" % par), 1)
                for c in range(FC):
                    act.wait_ge(*at("e0_h_ps", e * FC + (c + 1)))
                    act.activation(hT[:, par, c * B * S:(c + 1) * B * S], PS[:, 2 + c, :], ACT.Gelu) \
                        .then_inc(mark("e0_h"), 1)

            experts(act, step0)

            for k in range(B):
                copy(qTall[:, 4 * k:4 * k + 4, :], PS[:, k, :].rearrange("p (a n) -> p a n", a=4),
                     "qTall_ps", k + 1, "qTall")
            act.activation(warm[:, 1:2], ones[:, 0:1], ACT.Exp)

            def unit(b, g):
                U = b * G + g
                cur = not (static(b) and b == B - 1 and g == G)
                prev = not (static(b) and g == 0)
                for t in range(KT // 2):
                    N = U * (KT // 2) + t
                    if cur:
                        act.wait_ge(*at("st_ps", N + 1))
                        if not (static(N) and N < 2):
                            act.wait_ge(*at("plo_dve", N - 1))
                            act.wait_ge(*at("plo_pool", N - 1))
                        act.activation(pexp[:, t % 2, :], PS[:, 2 * (t % 2):2 * (t % 2) + 2, :]
                                       .rearrange("p a n -> p (a n)"), ACT.Exp, scale=float(D) ** -0.5) \
                            .then_inc(mark("pexp"), 1)
                        act.wait_ge(*at("pexp", N + 1))
                        if not (static(N) and N < 2):
                            act.wait_ge(*at("pv", N - 1))
                        act.activation(p_hi[:, t % 2, :], pexp[:, t % 2, :], ACT.Copy).then_inc(mark("phi"), 1)
                    if not static(b) and (g, t) in KEYS:
                        key_hi(b + 1, KEYS[g, t])
                    if prev and t == 2:
                        act.wait_ge(*at("pv", U * (KT // 2)))
                        act.activation(o_t[0:2 * HG * VC, :], PS[0:2 * HG * VC, 6 + (g - 1) % 2, :], ACT.Copy) \
                            .then_inc(mark("o_t"), 1)

            phase_c(act, unit)
            copy(oT[:, :], PS[:, 0, :], "xo_T_ps", 1, "xo_T")

            copy(xT1[:, :], PS[:, 0, :], "ln4_T_ps", 1, "ln4_T")
            for bank, name, dst in ((1, "rms_q_ps", t1r), (2, "rms_v_ps", v1r)):
                act.wait_ge(*at(name))
                act.activation(dst[:, :, :].rearrange("p b d -> p (b d)"), PS[:, bank, :], ACT.Square) \
                    .then_inc(mark("rms_sq"), 1)
            act.wait_ge(*at("rms_ms"))
            act.activation(q_rms[:, :], q_ms[:, :], ACT.Sqrt).then_inc(mark("rms_sd"), 1)
            copy(qT1[:, :], PS[:, 3, :], "q1_T_ps", 1, "q1_T")

            def wide_parts(i, p):
                e = i * 2 + p
                if static(e) and e >= E:
                    return
                act.wait_ge(*at("w1_1_%d" % (p % 2), (i + p // 2) * 16 + 16))
                if not (static(e) and e < 2):
                    act.wait_ge(*at("e1_h_ps", (e - 1) * FC))
                act.activation(wide_hi[:, p % 2, :], wide1[:, p % 2, :], ACT.Copy).then_inc(mark("e1_hi"), 1)

            wide_parts(0, 0)
            copy(xnT[:, :], PS[:, 0, :], "ln5_T_ps", 1, "ln5_T")
            act.wait_ge(*at("ln5_T"))
            act.activation(x5_hi, xnT[:, :], ACT.Copy).then_inc(mark("x5_hi"), 1)
            act.wait_ge(*at("r1_max"))
            act.activation(pr[:, :, :], lg[:, :, :], ACT.Exp).then_inc(mark("r1_exp"), 1)
            act.activation(warm[:, 2:3], ones[:, 0:1], ACT.Silu)

            def step1(i, p):
                if not stage(i, p)[0]:
                    return
                wide_parts(i, p + 1)
                for c in range(FC):
                    n = (i * 2 + p) * FC + c
                    act.wait_ge(*at("e1_h_ps", n + 1))
                    if not (static(n) and n < 2):
                        act.wait_ge(*at("e1_h", n - 1))
                    act.activation(sil[:, c % 2, :], PS[:, 2 * (c % 2), :], ACT.Silu).then_inc(mark("e1_sil"), 1)

            experts(act, step1)

        @block.vector
        def _(dve):
            start(dve, "dve")
            ch = Chain(dve, sem("dve_chain"))

            def layer_norm_stats(src, name):
                for b in range(B):
                    ins = dve.bn_stats(stats[:, b, :], src[:, b, :])
                ch(ins)
                for b in range(B):
                    ins = dve.bn_aggr(mv[:, b, :], stats[:, b, :])
                ch(ins)
                dve.tensor_scalar(vpe[:, :], mv[:, :, 1], EPS, None, ALU.add).then_inc(mark(name + "_var"), 1)

            def layer_norm(src, dst, name, beside=None):
                layer_norm_stats(src, name)
                if beside:
                    beside()
                dve.wait_ge(*at(name + "_rstd"))
                for b in range(B):
                    ins = dve.tensor_scalar(dst[:, b, :], src[:, b, :], mv[:, b, 0:1], rstd[:, b:b + 1],
                                            ALU.subtract, ALU.mult)
                ins.then_inc(mark(name), 1)
                dve.wait_ge(*at(name))

            def queries_normed():
                dve.wait_ge(*at("x_in", 16))
                layer_norm(xs, xn, "ln0")
                layer_norm_stats(xn, "ln0b")

            def queries_scaled():
                dve.wait_ge(*at("ln0b_rstd"))
                dve.wait_ge(*at("gain_in", 32))
                for b in range(B):
                    ins = dve.tensor_scalar(xn[:, b, :], xn[:, b, :], mv[:, b, 0:1], rstd[:, b:b + 1],
                                            ALU.subtract, ALU.mult)
                ch(ins)
                ch(dve.tensor_tensor(xn[:, :, :], xn[:, :, :], bc(rows[:, G_:G_ + 1, :], [P, B, D]), ALU.mult))
                dve.tensor_tensor(xn[:, :, :], xn[:, :, :], bc(rows[:, B_:B_ + 1, :], [P, B, D]), ALU.add) \
                    .then_inc(mark("xq"), 1)

            def norm_stats(b, c):
                dve.wait_ge(*at("ctx%d" % (c % QUADS), (b + c // QUADS) * 16 + 16))
                for j in range(NQ):
                    ins = dve.bn_stats(kst[:, j, :], cx[:, c % QUADS * NQ + j, :])
                ch(ins)
                dve.memset(gate[:, 0:1], 0.0)
                for j in range(NQ):
                    ins = dve.bn_aggr(kmv[:, j, :], kst[:, j, :])
                ch(ins)
                dve.tensor_scalar(kvpe[:, :], kmv[:, :, 1], EPS, None, ALU.add).then_inc(mark("k_var"), 1)

            def norm_rows(b, c):
                dve.wait_ge(*at("k_sd", b * QUADS + (c + 1)))
                ch(dve.reciprocal(krstd[:, :], krstd[:, :]))
                for j in range(NQ):
                    t = c % QUADS * NQ + j
                    ins = dve.tensor_scalar(X[:, t, :], cx[:, t, :], kmv[:, j, 0:1], krstd[:, j:j + 1],
                                            ALU.subtract, ALU.mult)
                ins.then_inc(mark("k_row"), 1)

            def turned_lo(b, c):
                dve.wait_ge(*at("xt", b * QUADS + c + 1))
                dve.tensor_tensor(XT_lo[:, c % 2, :], PS[:, 0, :], XT_hi[:, c % 2, :].bitcast(F32), ALU.subtract) \
                    .then_inc(mark("xt_lo"), 1)

            def sum_squares(b, c, j):
                dve.wait_ge(*at("sq", b * KT + (c * NQ + j + 1)))
                dve.tensor_reduce(out=ss[:, j, :], in_=sq[:, j % 2, :].rearrange("p (h d) -> p h d", h=H),
                                  axis=AX.X, op=ALU.add).then_inc(mark("ssum"), 1)

            def ratio(b, c, k):
                G0 = b * QUADS + c
                if k == 0:
                    dve.wait_ge(*at("ssum", b * KT + (c + 1) * NQ))
                    dve.wait_ge(*at("msum", G0 + 1))
                    m = msum[:, c % 2, :, :]
                    ins = dve.tensor_tensor(kt1[:, :, :], m, m, ALU.mult)
                else:
                    dve.wait_ge(*at("k_ratio", G0 * 6 + k))
                if k == 1:
                    ins = dve.scalar_tensor_tensor(kt2[:, :, :], kt1[:, :, :], -1.0 / D, ss[:, :, :],
                                                   ALU.mult, ALU.add)
                if k == 2:
                    ins = dve.tensor_scalar(kt2[:, :, :], kt2[:, :, :], 1.0 / (D - 1), None, ALU.mult)
                if k == 3:
                    ins = dve.tensor_scalar(kt1[:, :, :], kt2[:, :, :], 1.0, None, ALU.add)
                if k == 4:
                    ins = dve.reciprocal(kt1[:, :, :], kt1[:, :, :])
                if k == 5:
                    ins = dve.tensor_scalar(kt2[:, :, :], kt2[:, :, :], 1.0, 2.0, ALU.min, ALU.mult)
                if k == 6:
                    ins = dve.tensor_tensor(kr[:, c % 2, :, 0:H], kt2[:, :, :], kt1[:, :, :], ALU.mult)
                ins.then_inc(mark("kr" if k == 6 else "k_ratio"), 1)

            def scaled(b, c, j):
                if not (isinstance(b, int) and c == 0):
                    dve.wait_ge(*at("a_ps", b * KT + ((c - 1) * NQ + j + 1)))
                dve.tensor_tensor(Y[:, j, :].rearrange("p (h d) -> p h d", h=H),
                                  bc(X[:, c * NQ + j:c * NQ + j + 1, :], [P, H, D]),
                                  bc(kw[:, j, :].unsqueeze(2), [P, H, D]), ALU.mult).then_inc(mark("y"), 1)

            def step(b, c, prev, cur, nxt):
                G0 = b * QUADS + c
                if cur:
                    dve.wait_ge(*at("mean_ps", G0 + 1))
                    dve.tensor_reduce(out=msum[:, c % 2, :, :],
                                      in_=PS[:, 0, 0:2 * NQ * H].rearrange("p (n a h) -> p n h a", n=NQ, a=2),
                                      axis=AX.X, op=ALU.add).then_inc(mark("msum"), 1)
                if prev:
                    ratio(b, c - 1, 2)
                    dve.wait_ge(*at("k_norm", G0))
                    ch(dve.reciprocal(kw[:, :, :], kw[:, :, :]))
                    ratio(b, c - 1, 3)
                    dve.wait_ge(*at("k_x", G0))
                    scaled(b, c - 1, 0)
                    ratio(b, c - 1, 4)
                if nxt:
                    norm_rows(b, c + 1)
                if prev:
                    ratio(b, c - 1, 5)
                    scaled(b, c - 1, 1)
                    ratio(b, c - 1, 6)
                if cur:
                    sum_squares(b, c, 0)
                if prev:
                    scaled(b, c - 1, 2)
                if cur:
                    sum_squares(b, c, 1)
                if quad_after(b, c):
                    norm_stats(b, c + 2)
                if prev:
                    scaled(b, c - 1, 3)
                if cur:
                    sum_squares(b, c, 2)
                if nxt:
                    turned_lo(b, c + 1)
                if cur:
                    sum_squares(b, c, 3)
                    ratio(b, c, 0)
                    ratio(b, c, 1)
                if static(b) and b == B - 1 and c == 2:
                    queries_normed()
                if static(b) and b == B - 1 and c == QUADS:
                    queries_scaled()
                if c == QUADS:
                    dve.wait_ge(*at("a_ps", b * KT + KT))
                    dve.tensor_copy(t_all[:, bass.ds(b, 1), :].rearrange("p a n -> p (a n)"), PS[:, 7, 0:H + 1]) \
                        .then_inc(mark("t_ev"), 1)

            norm_stats(0, 0)
            norm_rows(0, 0)
            dve.wait_ge(*at("wT", 2))
            dve.tensor_reduce(out=wbar[:, :], in_=wT[:, W_IN:W_IN + H, :], axis=AX.X, op=ALU.add) \
                .then_inc(mark("wbar"), 1)
            dve.wait_ge(*at("wbar"))
            ch(dve.tensor_copy(wbar_hi, wbar[:, :]))
            dve.tensor_tensor(wbar_lo, wbar[:, :], wbar_hi.bitcast(F32), ALU.subtract)
            dve.wait_ge(*at("w_hi"))
            dve.tensor_tensor(w_lo, wT[:, W_IN:W_IN + H, :].rearrange("p h d -> p (h d)"), w_hi.bitcast(F32),
                              ALU.subtract).then_inc(mark("wbar_lo"), 1)
            ch(dve.memset(kr[:, :, :, H:H + 1], 1.0))
            norm_stats(0, 1)
            turned_lo(0, 0)
            phase_a(dve, step, ch, QUADS * 4)
            dve.wait_ge(*at("t_ev", B))

            dve.wait_ge(*at("rows_in", 16 * (NB - 2)))
            ch(dve.tensor_scalar(gauss[:, :], gauss[:, :], 4.0 / S, None, ALU.mult))
            dve.wait_ge(*at("qsum_ps"))
            ch(dve.tensor_copy(qsum[:, :], PS[:, 3, 448:448 + B * H]))
            dve.tensor_scalar(q1[:, :], qsum[:, :], 1.0 / D, None, ALU.mult).then_inc(mark("q_mean"), 1)
            dve.wait_ge(*at("small_ps"))
            ch(dve.tensor_copy(rwT[:, :], PS[:, 3, 0:E]))
            dve.tensor_copy(wp2T[:, :], PS[:, 3, E:E + 3]).then_inc(mark("small_cp"), 1)
            dve.wait_ge(*at("q_mean"))
            ch(dve.tensor_tensor(q2[:, :], q1[:, :], qsum[:, :], ALU.mult))
            for b in range(B):
                dve.wait_ge(*at("q_sq", b + 1))
                dve.tensor_reduce(out=qss[:, b * H:(b + 1) * H], in_=q_sq[b % 2].rearrange("p (h d) -> p h d", h=H),
                                  axis=AX.X, op=ALU.add).then_inc(mark("q_ssum" if b < B - 1 else "q_ss"), 1)
            dve.wait_ge(*at("q_ss"))
            ch(dve.tensor_tensor(q2[:, :], qss[:, :], q2[:, :], ALU.subtract))
            ch(dve.tensor_scalar(q2[:, :], q2[:, :], 1.0 / (D - 1), None, ALU.mult))
            ch(dve.tensor_scalar(qratio[:, :], q2[:, :], 1.0, None, ALU.add))
            ch(dve.reciprocal(qratio[:, :], qratio[:, :]))
            ch(dve.tensor_scalar(q2[:, :], q2[:, :], 1.0, 2.0, ALU.min, ALU.mult))
            dve.tensor_tensor(qratio[:, :], qratio[:, :], q2[:, :], ALU.mult).then_inc(mark("qratio"), 1)
            dve.wait_ge(*at("q_norm"))
            ch(dve.reciprocal(qinv[:, :], qinv[:, :]))
            for b in range(B):
                hs = slice(b * H, b * H + H)
                fb = fq[:, b, :].rearrange("p (h d) -> p h d", h=H)
                dve.wait_ge(*at("qc", b + 1))
                dve.tensor_tensor(fb, fb, bc(qinv[:, hs].unsqueeze(2), [P, H, D]), ALU.mult) \
                    .then_inc(mark("fq_unit"), 1)
            dve.wait_ge(*at("cov_b", B))
            ch(dve.tensor_tensor(sqb[:, :].rearrange("p (h d) -> p h d", h=H),
                                 PS[:, 6:8, :].rearrange("p a (h d) -> p (a h) d", d=D),
                                 bc(offdiag[:, :].unsqueeze(1), [P, H, D]), ALU.mult))
            ch(dve.tensor_tensor(sqb[:, :], sqb[:, :], sqb[:, :], ALU.mult))
            dve.tensor_reduce(out=covsum[:, :], in_=sqb[:, :].rearrange("p (h d) -> p h d", h=H),
                              axis=AX.X, op=ALU.add).then_inc(mark("covsum"), 1)
            dve.tensor_reduce(out=meanx[:, 0:1], in_=xnT[:, :], axis=AX.X, op=ALU.add)
            ch(dve.tensor_reduce(out=meanx[:, 1:2], in_=t_all[:, :, H], axis=AX.X, op=ALU.add))
            ch(dve.tensor_scalar(meanx[:, 0:1], meanx[:, 0:1], 1.0 / (B * S), None, ALU.mult))
            dve.tensor_scalar(meanx[:, 1:2], meanx[:, 1:2], 1.0 / (B * S2), None, ALU.mult) \
                .then_inc(mark("meanx"), 1)
            dve.wait_ge(*at("cov_tot"))
            dve.tensor_copy(sm8[:, 0:1], PS[0:8, 3, 300:301]).then_inc(mark("cov_ss"), 1)
            dve.wait_ge(*at("feats_ps"))
            dve.tensor_copy(feats[:, :].rearrange("p (a h) -> p h a", a=2),
                            PS[:, 3, 0:2 * H].rearrange("p (h a) -> p h a", a=2)).then_inc(mark("feats"), 1)
            dve.wait_ge(*at("h1_ps"))
            ch(dve.tensor_tensor(h8[:, 0, :], PS[0:8, 3, 128:256], rows[0:8, WPB1, :], ALU.add))
            ch(dve.bn_stats(h8s[:, :], h8[:, 0, :]))
            ch(dve.bn_aggr(h8m[:, :], h8s[:, :]))
            dve.tensor_scalar(h8m[:, 1:2], h8m[:, 1:2], EPS, None, ALU.add).then_inc(mark("wp_var"), 1)
            dve.wait_ge(*at("wp_rstd"))
            ch(dve.tensor_scalar(h8[:, 1, :], h8[:, 0, :], h8m[:, 0:1], h8r[:, 0:1], ALU.subtract, ALU.mult))
            ch(dve.tensor_tensor(h8[:, 1, :], h8[:, 1, :], rows[0:8, WPG, :], ALU.mult))
            ch(dve.tensor_tensor(h8[:, 1, :], h8[:, 1, :], rows[0:8, WPB, :], ALU.add))
            dve.tensor_scalar(h8[:, 2, :], h8[:, 1, :], 0.0, None, ALU.max).then_inc(mark("h1"), 1)
            dve.wait_ge(*at("h1T_ps"))
            dve.tensor_copy(h1T[:, :], PS[:, 3, 256:256 + H]).then_inc(mark("h1T"), 1)
            dve.wait_ge(*at("wp_ps"))
            ch(dve.tensor_tensor(sm8[:, 4:7], PS[0:8, 3, 310:313], wpb2[0:8, :], ALU.add))
            ch(dve.tensor_reduce(out=sm8[:, 7:8], in_=sm8[:, 4:7], axis=AX.X, op=ALU.max))
            dve.tensor_scalar(sm8[:, 4:7], sm8[:, 4:7], sm8[:, 7:8], None, ALU.subtract) \
                .then_inc(mark("wp_logit"), 1)
            dve.wait_ge(*at("wp_exp"))
            ch(dve.tensor_reduce(out=sm8[:, 7:8], in_=sm8[:, 8:11], axis=AX.X, op=ALU.add))
            ch(dve.reciprocal(sm8[:, 7:8], sm8[:, 7:8]))
            ch(dve.tensor_scalar(sm8[:, 8:11], sm8[:, 8:11], sm8[:, 7:8], None, ALU.mult))
            dve.wait_ge(*at("decorr"))
            ch(dve.tensor_tensor(sm8[:, 11:12], sm8[:, 9:10], sm8[:, 3:4], ALU.mult))
            dve.tensor_tensor(sm8[:, 11:12], sm8[:, 11:12], sm8[:, 8:9], ALU.add).then_inc(mark("coef8"), 1)
            dve.wait_ge(*at("coef_ps"))
            ch(dve.tensor_copy(coef[:, :], PS[:, 3, 320:320 + 2 * H]))
            dve.tensor_tensor(wt_t[:, :, :], t_all[:, :, 0:H], bc(coef[:, H:2 * H].unsqueeze(1), [P, B, H]),
                              ALU.mult).then_inc(mark("coef"), 1)
            dve.tensor_tensor(gauss[:, :], gauss[:, :], gauss[:, :], ALU.mult).then_inc(mark("gauss_sq"), 1)
            dve.wait_ge(*at("coef"))
            for h in range(H):
                dve.wait_ge(*at("u_ps", h + 1))
                if h >= 2:
                    dve.wait_ge(*at("out0_ps", h - 1))
                az, ratios = (PS[:, bank, :] for bank in U_BANKS[h % 2])
                for b in range(B):
                    ins = dve.tensor_scalar(tmpU[:, h % 2, b * S:(b + 1) * S], ratios[:, b * S:(b + 1) * S],
                                            wt_t[:, b, h:h + 1], None, ALU.mult)
                ch(ins)
                dve.scalar_tensor_tensor(tmpU[:, h % 2, :], az, coef[:, h:h + 1], tmpU[:, h % 2, :],
                                         ALU.mult, ALU.add).then_inc(mark("u"), 1)
            ch(dve.tensor_tensor(xs[:, :, :], xs[:, :, :], bc(rows[:, BOUT:BOUT + 1, :], [P, B, D]), ALU.add))
            dve.wait_ge(*at("out0_ps", H))
            for b in range(B):
                ins = dve.tensor_tensor(xs[:, b, :], xs[:, b, :], PS[:, [0, 1, 4, 5][b], 0:D], ALU.add)
            ins.then_inc(mark("x1"), 1)
            dve.wait_ge(*at("x1"))

            def mask_numbers(b):
                dve.wait_ge(*at("mask%d" % b, 16))
                dve.tensor_scalar(maskb[:, b, :], mask_i[b % 2], 0.0, MASKED, ALU.is_equal, ALU.mult) \
                    .then_inc(mark("maskb"), 1)

            def key_lo(b, n):
                dve.wait_ge(*at("ct_hi", b * QUADS + (n + 1)))
                dve.tensor_tensor(ctxT_lo[:, n * NQ * P:(n + 1) * NQ * P], PS[:, key_bank(b, n), :],
                                  ctxT_hi[:, n * NQ * P:(n + 1) * NQ * P].bitcast(F32), ALU.subtract) \
                    .then_inc(mark("ct_lo"), 1)

            layer_norm(xs, xn, "ln1", lambda: mask_numbers(0))
            mask_numbers(1)
            dve.wait_ge(*at("qk_ps"))
            dve.tensor_scalar(qT[:, :], PS[:, 1, :], bcol[:, 0:1], None, ALU.add)
            dve.tensor_scalar(kT[:, :], PS[:, 2, :], bcol[:, 1:2], None, ALU.add).then_inc(mark("qk"), 1)
            dve.wait_ge(*at("v_ps"))
            dve.tensor_tensor(vv[:, :, :], PS[:, 3, :].rearrange("p (b d) -> p b d", b=B),
                              bc(rows[:, BV:BV + 1, :], [P, B, D]), ALU.add).then_inc(mark("v0"), 1)
            mask_numbers(2)
            dve.wait_ge(*at("sc_ps"))
            dve.wait_ge(*at("gauss"))
            ch(dve.scalar_tensor_tensor(sc[:, :, :], PS[:, 4, :].rearrange("p (b d) -> p b d", b=B),
                                        float(D) ** -0.5, bc(gauss[:, :].unsqueeze(1), [P, B, S]),
                                        ALU.mult, ALU.mult))
            ch(dve.tensor_reduce(out=s4[:, :], in_=sc[:, :, :], axis=AX.X, op=ALU.max))
            dve.tensor_tensor(sc[:, :, :], sc[:, :, :], bc(s4[:, :].unsqueeze(2), [P, B, S]), ALU.subtract) \
                .then_inc(mark("sc_max"), 1)
            dve.wait_ge(*at("sc_exp"))
            ch(dve.tensor_reduce(out=s4[:, :], in_=sc[:, :, :], axis=AX.X, op=ALU.add))
            ch(dve.reciprocal(r4[:, :], s4[:, :]))
            dve.tensor_tensor(sc[:, :, :], sc[:, :, :], bc(r4[:, :].unsqueeze(2), [P, B, S]), ALU.mult) \
                .then_inc(mark("probs"), 1)

            def add_rows(bank, bias, done):
                ch(dve.tensor_tensor(xs[:, :, :], xs[:, :, :], bc(rows[:, bias:bias + 1, :], [P, B, D]), ALU.add))
                dve.wait_ge(*at(done))
                ch(dve.tensor_tensor(xs[:, :, :], xs[:, :, :], PS[:, bank, :].rearrange("p (b d) -> p b d", b=B),
                                     ALU.add))

            mask_numbers(3)
            add_rows(2, BO, "o0_ps")

            def best(src, dst):
                ch(dve.tensor_reduce(out=s4[:, :], in_=src, axis=AX.X, op=ALU.max))
                ch(dve.tensor_tensor(dst, src, bc(s4[:, :].unsqueeze(2), [P, B, E]), ALU.is_equal))
                ch(dve.tensor_tensor(dst, dst, bc(lastfirst[:, :].unsqueeze(1), [P, B, E]), ALU.mult))
                ch(dve.tensor_reduce(out=s4[:, :], in_=dst, axis=AX.X, op=ALU.max))
                ch(dve.tensor_tensor(dst, dst, bc(s4[:, :].unsqueeze(2), [P, B, E]), ALU.is_equal))

            def router_softmax(name, bias):
                dve.wait_ge(*at(name + "_ps"))
                src = PS[:, 1, 0:B * E].rearrange("p (b e) -> p b e", b=B)
                if bias is None:
                    ch(dve.tensor_copy(lg[:, :, :], src))
                else:
                    ch(dve.tensor_tensor(lg[:, :, :], src, bc(bias.unsqueeze(1), [P, B, E]), ALU.add))
                ch(dve.tensor_reduce(out=s4[:, :], in_=lg[:, :, :], axis=AX.X, op=ALU.max))
                dve.tensor_tensor(lg[:, :, :], lg[:, :, :], bc(s4[:, :].unsqueeze(2), [P, B, E]), ALU.subtract) \
                    .then_inc(mark(name + "_max"), 1)
                dve.wait_ge(*at(name + "_exp"))
                ch(dve.tensor_reduce(out=s4[:, :], in_=pr[:, :, :], axis=AX.X, op=ALU.add))
                ch(dve.reciprocal(r4[:, :], s4[:, :]))
                ch(dve.tensor_tensor(pr[:, :, :], pr[:, :, :], bc(r4[:, :].unsqueeze(2), [P, B, E]), ALU.mult))

            layer_norm(xs, xn, "ln2")
            key_lo(0, 0)
            key_lo(0, 1)
            dve.wait_ge(*at("x2_hi"))
            dve.tensor_tensor(x2_lo, PS[:, 0, :], x2_hi.bitcast(F32), ALU.subtract).then_inc(mark("x2_lo"), 1)
            router_softmax("r0", None)
            best(pr[:, :, :], oh[:, :, :])
            ch(dve.scalar_tensor_tensor(lg[:, :, :], oh[:, :, :], -4.0, pr[:, :, :], ALU.mult, ALU.add))
            best(lg[:, :, :], oh2[:, :, :])
            ch(dve.tensor_tensor(oh[:, :, :], oh[:, :, :], oh2[:, :, :], ALU.add))
            ch(dve.tensor_tensor(wgt[:, :, :], oh[:, :, :].rearrange("p b e -> p e b"),
                                 pr[:, :, :].rearrange("p b e -> p e b"), ALU.mult))

            key_lo(0, 2)
            key_lo(0, 3)

            def combine(e, par, n, layer):
                dve.wait_ge(*at("e%d_y%d" % (layer, par), n))
                ch(dve.tensor_tensor(ytmp[:, :].rearrange("p (b d) -> p b d", b=B),
                                     PS[:, 6 + par, :].rearrange("p (b d) -> p b d", b=B),
                                     bc(wgt[:, bass.ds(e, 1), :].rearrange("p a b -> p (a b)").unsqueeze(2),
                                        [P, B, D]), ALU.mult))
                dve.tensor_tensor(acc[:, :], acc[:, :], ytmp[:, :], ALU.add) \
                    .then_inc(mark("e%d_add%d" % (layer, par)), 1)
                dve.wait_ge(*at("e%d_add%d" % (layer, par), n))

            ch(dve.memset(acc[:, :], 0.0))

            def step0(i, p):
                cur, prev = stage(i, p)
                if cur:
                    dve.wait_ge(*at("e0_T%d" % (p % 2), (i + p // 2) * 2 + 1))
                    dve.tensor_tensor(w1T_lo[:, p % 2, :], PS[:, 0, :], w1T_hi[:, p % 2, :].bitcast(F32),
                                      ALU.subtract).then_inc(mark("e0_lo"), 1)
                if prev:
                    combine(i * 2 + (p - 1), (p + 1) % 2, i + (p + 1) // 2, 0)

            experts(dve, step0, ch)
            dve.tensor_tensor(xs[:, :, :], xs[:, :, :], acc[:, :].rearrange("p (b d) -> p b d", b=B), ALU.add) \
                .then_inc(mark("x3"), 1)
            dve.wait_ge(*at("x3"))

            layer_norm(xs, xn, "ln3", lambda: dve.memset(nm[:, :], 0.0))
            qr_hi = q_one[:, :].bitcast(F32R)
            ch(dve.tensor_copy(qr_hi, xn[:, :, :].rearrange("p b d -> p (b d)")))
            qv = qpack[:, :, :].rearrange("p (b g) (j r) -> p b (g j) r", g=G, j=HG)
            hi_v = q_one[:, :].rearrange("p (b h d) -> p b h d", b=B, d=HD)
            xn_v = xn[:, :, :].rearrange("p b (h d) -> p b h d", d=HD)
            for b in range(B):
                dve.tensor_copy(qv[:, b, :, 2:2 + HD], hi_v[:, b])
                dve.tensor_copy(qv[:, b, :, 2 + 2 * HD:2 + 3 * HD], hi_v[:, b])
                dve.tensor_tensor(qv[:, b, :, 2 + HD:2 + 2 * HD], xn_v[:, b], hi_v[:, b], ALU.subtract) \
                    .then_inc(mark("qpack"), 1)

            bm = bc(groupmask[:, :].unsqueeze(2), [P, HG, S])

            def q_blocks(n_dyn, par):
                dve.tensor_tensor(qp1[:, par, :].rearrange("p (j q) -> p j q", j=HG),
                                  bc(qTall[:, bass.ds(n_dyn, 1), :], [P, HG, S]), bm, ALU.mult) \
                    .then_inc(mark("qp1"), 1)

            def chunk_max(mask, C0, c):
                dve.wait_ge(*at("smx_ps", C0 + (c + 1)))
                if not (static(C0) and C0 + c < 2):
                    dve.wait_ge(*at("smx", C0 + c - 1))
                k0 = c % HC * 512
                dve.memset(gate[:, 1 + c % 2:2 + c % 2], 0.0)
                dve.tensor_tensor_reduce(out=junk[c % 2], in0=PS[:, 4 + c % 2, :], in1=mask[:, k0:k0 + 512],
                                         scale=1.0, scalar=LOWEST, op0=ALU.add, op1=ALU.max,
                                         accum_out=mx[:, c:c + 1]).then_inc(mark("smx"), 1)

            def q_max(U1):
                dve.wait_ge(*at("smx", U1 * HC * HG))
                nv = nm[:, :].rearrange("p (j r) -> p j r", j=HG)
                ch(dve.tensor_reduce(out=nmax[:, :], in_=mx[:, :].rearrange("p (j a) -> p j a", a=HC),
                                     axis=AX.X, op=ALU.max, negate=True))
                ch(dve.tensor_copy(nv[:, :, 0].bitcast(F32R), nmax[:, :]))
                dve.tensor_tensor(nv[:, :, 1], nmax[:, :], nv[:, :, 0], ALU.subtract).then_inc(mark("nm"), 1)

            def q_shift(n_dyn, U1, par):
                dve.wait_ge(*at("nmT_ps", U1))
                ch(dve.tensor_tensor(qs2[:, :], PS[:, 4, 0:P],
                                     qTall[:, bass.ds(n_dyn, 1), :].rearrange("p a n -> p (a n)"), ALU.add))
                dve.tensor_tensor(qp2[:, par, :].rearrange("p (j q) -> p j q", j=HG),
                                  bc(qs2[:, :].unsqueeze(1), [P, HG, S]), bm, ALU.mult).then_inc(mark("qp2"), 1)

            def finish_unit(b, g):
                dve.wait_ge(*at("o_t_ps", b * G + g + 1))
                R = 2 * HG * VC + VC
                hi, lo = (PS[:, 6 + g % 2, a * HG * VC:a * HG * VC + (HG - 1) * R + VC + (R - VC)]
                          .rearrange("p (j r) -> p j r", r=R)[:, :, 0:VC] for a in range(2))
                ch(dve.tensor_copy(osum[:, :, :], hi))
                ch(dve.tensor_tensor(osum[:, :, :], lo, osum[:, :, :], ALU.add))
                ch(dve.reciprocal(rec4[:, :], osum[:, :, HD]))
                dve.tensor_tensor(orow[:, bass.ds(b, 1), g * HG * HD:(g + 1) * HG * HD]
                                  .rearrange("p a (j d) -> p (a j) d", d=HD), osum[:, :, 0:HD],
                                  bc(rec4[:, :].unsqueeze(2), [P, HG, HD]), ALU.mult).then_inc(mark("orow"), 1)
                dve.wait_ge(*at("orow", b * G + g + 1))

            dve.wait_ge(*at("qTall"))
            q_blocks(0, 0)
            for c in range(HC * HG):
                chunk_max(maskb[:, 0, :], 0, c)
            dve.wait_ge(*at("qTall", B))
            q_blocks(1, 1)
            q_max(1)
            q_shift(0, 1, 0)
            ch(dve.tensor_copy(mnow[:, :], maskb[:, 0, :]))

            def rest(b, g, t):
                dve.wait_ge(*at("phi", (b * G + g) * (KT // 2) + t + 1))
                dve.tensor_tensor(p_lo[:, t % 2, 0:HG * S], pexp[:, t % 2, 0:HG * S],
                                  p_hi[:, t % 2, 0:HG * S].bitcast(F32), ALU.subtract).then_inc(mark("plo_dve"), 1)

            def unit(b, g):
                U = b * G + g
                cur = not (static(b) and b == B - 1 and g == G)
                prev = not (static(b) and g == 0)
                follow = cur and not (static(b) and b == B - 1 and g == G - 1)
                c = 0
                for t in range(KT // 2):
                    if prev and t == 0:
                        rest(b, g - 1, KT // 2 - 1)
                    if follow:
                        for k in range(CHUNKS[t]):
                            chunk_max(mnow if (g + 1) % G else mnext, (U + 1) * HC * HG, c)
                            c += 1
                            if cur and k == 0 and t > 0:
                                rest(b, g, t - 1)
                    if cur and t > 0 and not (follow and CHUNKS[t]):
                        rest(b, g, t - 1)
                    if not static(b) and (g, t) in KEYS:
                        key_lo(b + 1, KEYS[g, t])
                    if t == 5 and not (static(b) and b == B - 1 and g + 2 >= G):
                        q_blocks(U + 2, g % 2)
                    if follow and t == 6:
                        q_max(U + 2)
                    if follow and t == 7:
                        q_shift(U + 1, U + 2, (g + 1) % 2)
                    if prev and t == 4:
                        finish_unit(b, g - 1)
                    if not static(b) and t == 3 and g in (1, 3):
                        ch(dve.tensor_copy((mnext if g == 1 else mnow)[:, :],
                                           maskb[:, bass.ds(b + 1, 1), :].rearrange("p a n -> p (a n)")))

            phase_c(dve, unit, ch, G * 6 + 2)
            add_rows(1, BFC, "fc_ps")

            layer_norm(xs, xn, "ln4")
            for n, src in enumerate((t1r, v1r)):
                dve.wait_ge(*at("rms_sq", n + 1))
                ins = dve.tensor_reduce(out=q_ms[:, n * B * NH:(n + 1) * B * NH],
                                        in_=src[:, :, :].rearrange("p b (h d) -> p (b h) d", d=HD),
                                        axis=AX.X, op=ALU.add)
            ch(ins)
            dve.tensor_scalar(q_ms[:, :], q_ms[:, :], 1.0 / HD, RMS_EPS, ALU.mult, ALU.add) \
                .then_inc(mark("rms_ms"), 1)
            dve.wait_ge(*at("rms_sd"))
            ch(dve.reciprocal(q_rms[:, :], q_rms[:, :]))
            for n, (name, dst, wrow) in enumerate((("rms_q", q1r, QW), ("rms_v", v1r, VW))):
                ch(dve.tensor_tensor(dst[:, :, :].rearrange("p b (h d) -> p (b h) d", d=HD),
                                     PS[:, 1 + n, :].rearrange("p (h d) -> p h d", d=HD),
                                     bc(q_rms[:, n * B * NH:(n + 1) * B * NH].unsqueeze(2), [P, B * NH, HD]),
                                     ALU.mult))
                dve.tensor_tensor(dst[:, :, :], dst[:, :, :], bc(rows[:, wrow:wrow + 1, :], [P, B, D]),
                                  ALU.mult).then_inc(mark(name), 1)
            ch(dve.tensor_reduce(out=pairmask[:, :], in_=headmask[:, :].rearrange("p (g j) -> p j g", g=G),
                                 axis=AX.X, op=ALU.add))

            dve.wait_ge(*at("q1_T"))
            head_blocks(dve, 0).then_inc(mark("qbd0"), 1)

            def keep_causal(b):
                dve.wait_ge(*at("s1_ps", b + 1))
                if b >= 2:
                    dve.wait_ge(*at("o1_ps", b - 1))
                dve.tensor_tensor(sT1[:, b % 2, :].rearrange("p (h q) -> p h q", q=S),
                                  PS[:, 4:8, :].rearrange("p a (h q) -> p (a h) q", q=S),
                                  bc(causal[:, :].unsqueeze(1), [P, NH, S]), ALU.mult).then_inc(mark("s1"), 1)

            def pick(b):
                dve.wait_ge(*at("o1_ps", b + 1))
                if b >= 1:
                    dve.wait_ge(*at("o1_own", b))
                ch(dve.tensor_tensor(own[:, :].rearrange("p (j q) -> p j q", j=HG),
                                     PS[:, 1 + b % 2, :].rearrange("p (j q) -> p j q", j=HG),
                                     bc(pairmask[:, :].unsqueeze(2), [P, HG, S]), ALU.mult))
                if b >= 1:
                    dve.wait_ge(*at("o1_T", b))
                dve.tensor_reduce(out=o1s[:, :], in_=own[:, :].rearrange("p (j q) -> p q j", j=HG),
                                  axis=AX.X, op=ALU.add).then_inc(mark("o1_own"), 1)

            for b in range(B):
                keep_causal(b)
                if b >= 1:
                    pick(b - 1)
            pick(B - 1)
            dve.wait_ge(*at("o1_T", B))
            ch(dve.tensor_tensor(xs[:, :, :], xs[:, :, :], PS[:, 0, :].rearrange("p (b d) -> p b d", b=B), ALU.add))

            def wide_rest(i, p):
                e = i * 2 + p
                if static(e) and e >= E:
                    return
                dve.wait_ge(*at("e1_hi", e + 1))
                dve.tensor_tensor(wide_lo[:, p % 2, :], wide1[:, p % 2, :], wide_hi[:, p % 2, :].bitcast(F32),
                                  ALU.subtract).then_inc(mark("e1_lo"), 1)

            layer_norm(xs, xn, "ln5", lambda: wide_rest(0, 0))
            dve.wait_ge(*at("x5_hi"))
            dve.tensor_tensor(x5_lo, xnT[:, :], x5_hi.bitcast(F32), ALU.subtract).then_inc(mark("x5_lo"), 1)
            router_softmax("r1", rb1[:, :])
            best(pr[:, :, :], oh[:, :, :])
            ch(dve.tensor_tensor(wgt[:, :, :], oh[:, :, :].rearrange("p b e -> p e b"),
                                 pr[:, :, :].rearrange("p b e -> p e b"), ALU.mult))
            ch(dve.memset(acc[:, :], 0.0))

            def step1(i, p):
                cur, prev = stage(i, p)
                if cur:
                    wide_rest(i, p + 1)
                    for c in range(FC):
                        dve.wait_ge(*at("e1_sil", (i * 2 + p) * FC + c + 1))
                        if c == 0:
                            dve.wait_ge(*at("e1_y%d" % (p % 2), i + p // 2))
                        dve.tensor_tensor(hT[:, p % 2, c * B * S:(c + 1) * B * S], sil[:, c % 2, :],
                                          PS[:, 2 * (c % 2) + 1, :], ALU.mult).then_inc(mark("e1_h"), 1)
                if prev:
                    combine(i * 2 + (p - 1), (p + 1) % 2, i + (p + 1) // 2, 1)

            experts(dve, step1, ch)
            dve.tensor_tensor(xs[:, :, :], xs[:, :, :], acc[:, :].rearrange("p (b d) -> p b d", b=B), ALU.add) \
                .then_inc(mark("x6"), 1)

        @block.tensor
        def _(pe):
            start(pe, "pe")

            def mm(dst, lhsT, rhs, start=True, stop=True):
                return pe.matmul(dst, lhsT, rhs, start=start, stop=stop, skip_group_check=True)

            def turn(dst, src, n=P):
                return pe.transpose(dst, src, ident[0:n, 0:n])

            def turn_rows(src, bank, wait, done):
                pe.wait_ge(*at(wait))
                for b in range(B):
                    ins = turn(PS[:, bank, b * P:(b + 1) * P], src[:, b, :])
                ins.then_inc(mark(done), 1)

            pe.wait_ge(*at("consts"))
            pe.wait_ge(*at("w_in", 16))
            for k in range(2):
                for n in range(4):
                    ins = turn(PS[:, k, n * P:(n + 1) * P], w[:, 4 * k + n, :])
                ins.then_inc(mark("wT_ps"), 1)
            pe.wait_ge(*at("wT", 2))
            pe.wait_ge(*at("wbar"))

            w_in_T = wT[:, W_IN:W_IN + H, :].rearrange("p h d -> p (h d)")

            def turn_x(G1, c1):
                pe.wait_ge(*at("k_x", G1 + 1))
                if not isinstance(G1, int) or G1 > 0:
                    pe.wait_ge(*at("msum", G1))
                for j in range(NQ):
                    ins = turn(PS[:, 0, j * P:(j + 1) * P], X[:, c1 % QUADS * NQ + j, :])
                ins.then_inc(mark("xt_ps"), 1)

            def sums(b, c, j):
                t = c * NQ + j
                pe.wait_ge(*at("y", b * KT + (t + 1)))
                if t == 0:
                    pe.wait_ge(*at("a_ev", b))
                    pe.wait_ge(*at("t_ev", b))
                xr = X[:, t, :]
                mm(PS[:, 5, :], xr, Y[:, j, 0:512], t == 0, t == KT - 1)
                ins = mm(PS[:, 6, :], xr, Y[:, j, 512:1024], t == 0, t == KT - 1)
                if j == 1:
                    pe.wait_ge(*at("kr", b * QUADS + c + 1))
                    mm(PS[:, 7, 0:H + 1], X[:, t - 1, :], kr[:, c % 2, 0, :], c == 0, False)
                if j >= 1:
                    ins = mm(PS[:, 7, 0:H + 1], xr, kr[:, c % 2, j, :], False, t == KT - 1)
                ins.then_inc(mark("a_ps"), 1)

            def project(b, c, j):
                t = c * NQ + j
                if not (isinstance(b, int) and t < 2):
                    pe.wait_ge(*at("sq", b * KT + (t - 1)))
                hi, lo = (a[:, c % 2, j * P:(j + 1) * P] for a in (XT_hi, XT_lo))
                f0 = 1 + 2 * (j % 2)
                for n in range(2):
                    mm(PS[:, f0 + n, :], hi, w_hi[:, n * 512:(n + 1) * 512], True, False)
                    mm(PS[:, f0 + n, :], hi, w_lo[:, n * 512:(n + 1) * 512], False, False)
                for n in range(2):
                    ins = mm(PS[:, f0 + n, :], lo, w_hi[:, n * 512:(n + 1) * 512], False, True)
                ins.then_inc(mark("f_ps"), 1)

            def step(b, c, prev, cur, nxt):
                G0 = b * QUADS + c
                if cur:
                    pe.wait_ge(*at("xt_lo", G0 + 1))
                    for n in range(NQ):
                        hi, lo = (a[:, c % 2, n * P:(n + 1) * P] for a in (XT_hi, XT_lo))
                        mm(PS[:, 0, 2 * n * H:2 * (n + 1) * H], hi, wbar_parts, True, False)
                        ins = mm(PS[:, 0, 2 * n * H:(2 * n + 1) * H], lo, wbar_hi, False, True)
                    ins.then_inc(mark("mean_ps"), 1)
                    project(b, c, 0)
                    project(b, c, 1)
                if prev:
                    sums(b, c - 1, 0)
                if cur:
                    project(b, c, 2)
                if prev:
                    sums(b, c - 1, 1)
                if cur:
                    project(b, c, 3)
                if nxt:
                    turn_x(G0 + 1, c + 1)
                if prev:
                    sums(b, c - 1, 2)
                    sums(b, c - 1, 3)

            turn_x(0, 0)
            pe.wait_ge(*at("wbar_lo"))
            phase_a(pe, step)

            pe.wait_ge(*at("w_all", 16 * 16))
            for k in range(2, 7):
                if k >= 4:
                    pe.wait_ge(*at("wT", k - 1))
                for n in range(4):
                    if 4 * k + n < NW:
                        ins = turn(PS[:, k % 2, n * P:(n + 1) * P], w[:, 4 * k + n, :])
                ins.then_inc(mark("wT_ps"), 1)
            pe.wait_ge(*at("a_ev", B))
            pe.wait_ge(*at("t_ev", B))
            turn_rows(xn, 2, "xq", "xq_T_ps")
            turn(PS[:, 3, 0:E], small[0:E, 0, :], E)
            turn(PS[:, 3, E:E + 3], small[0:3, 1, :], 3).then_inc(mark("small_ps"), 1)
            pe.wait_ge(*at("xq_T"))
            for b in range(B):
                ins = mm(PS[:, 3, 448 + b * H:448 + (b + 1) * H], xnT[:, b * S:(b + 1) * S], wbar[:, :])
            ins.then_inc(mark("qsum_ps"), 1)
            for b in range(B):
                if b >= 2:
                    pe.wait_ge(*at("fq", b - 1))
                for n in range(2):
                    ins = mm(PS[:, 4 + 2 * (b % 2) + n, :], xnT[:, b * S:(b + 1) * S],
                             w_in_T[:, n * 512:(n + 1) * 512])
                ins.then_inc(mark("fq_ps"), 1)

            pe.wait_ge(*at("wT", 7))
            pe.wait_ge(*at("fq", B - 1))
            for h in range(H):
                ins = mm(PS[:, 4 + h // 4, (h % 4) * D:(h % 4 + 1) * D], w[:, W_IN + h, :], wT[:, W_OUT + h, :])
            ins.then_inc(mark("comb_ps"), 1)
            pe.wait_ge(*at("fq", B))
            pe.wait_ge(*at("small_cp"))
            for b in range(B):
                pe.wait_ge(*at("qc", b + 1))
                for h in range(H):
                    qc_h = qc[:, b % 2, h * D:(h + 1) * D]
                    ins = mm(PS[:, 6 + h // 4, (h % 4) * D:(h % 4 + 1) * D], qc_h, qc_h,
                             b == 0 and h % 4 == 0, b == B - 1)
                ins.then_inc(mark("cov_b"), 1)
            pe.wait_ge(*at("fq_unit", B))
            for h in range(H):
                if h >= 2:
                    pe.wait_ge(*at("fqT", h - 1))
                for b in range(B):
                    ins = turn(PS[:, h % 2, b * S:(b + 1) * S], fq[:, b, h * D:(h + 1) * D])
                ins.then_inc(mark("fqT_ps"), 1)

            def z_of(h):
                if h == 0:
                    pe.wait_ge(*at("fqT", H))
                    pe.wait_ge(*at("comb", 2))
                if h >= 3:
                    pe.wait_ge(*at("zt", h - 2))
                mm(PS[:, Z_BANKS[h % 3], :], w[:, W_IN + h, :], fqT[:, h, :]).then_inc(mark("zt_ps"), 1)

            pe.wait_ge(*at("covsum"))
            mm(PS[0:8, 3, 300:301], covsum[:, :], ones[:, 0:1]).then_inc(mark("cov_tot"), 1)
            pe.wait_ge(*at("meanx"))
            pe.wait_ge(*at("cov_ss"))
            for h in range(H):
                ins = mm(PS[:, 3, 2 * h:2 * h + 2], wT[:, W_IN + h, :], meanx[:, :])
            ins.then_inc(mark("feats_ps"), 1)
            z_of(0)
            pe.wait_ge(*at("feats"))
            mm(PS[0:8, 3, 128:256], feats[:, 0:H], wT[:, WP1, :], True, False)
            mm(PS[0:8, 3, 128:256], feats[:, H:2 * H], wT[:, WP1 + 1, :], False, True).then_inc(mark("h1_ps"), 1)
            for h in range(1, 5):
                z_of(h)
            pe.wait_ge(*at("h1"))
            turn(PS[:, 3, 256:256 + H], h8[:, 2, :], 8).then_inc(mark("h1T_ps"), 1)
            pe.wait_ge(*at("h1T"))
            mm(PS[0:8, 3, 310:313], h1T[:, :], wp2T[:, :]).then_inc(mark("wp_ps"), 1)
            for h in range(5, H):
                z_of(h)
            pe.wait_ge(*at("coef8"))
            mm(PS[:, 3, 320:320 + H], sm8[:, 11:12].to_broadcast([8, P]), ident[0:8, 0:8])
            mm(PS[:, 3, 320 + H:320 + 2 * H], sm8[:, 10:11].to_broadcast([8, P]), ident[0:8, 0:8]) \
                .then_inc(mark("coef_ps"), 1)
            pe.wait_ge(*at("coef"))

            def out_of(h):
                pe.wait_ge(*at("u", h + 1))
                for b, bank in enumerate((0, 1, 4, 5)):
                    ins = mm(PS[:, bank, 0:D], tmpU[:, h % 2, b * S:(b + 1) * S], comb[:, h, :], h == 0, h == H - 1)
                ins.then_inc(mark("out0_ps"), 1)

            pe.wait_ge(*at("zt", H))
            for h in range(H):
                if h >= 2:
                    pe.wait_ge(*at("u", h - 1))
                az, ratios = (PS[:, bank, :] for bank in U_BANKS[h % 2])
                for b in range(B):
                    mm(az[:, b * S:(b + 1) * S], a_all[:, b, h * D:(h + 1) * D], fqT[:, h, b * S:(b + 1) * S])
                    ins = mm(ratios[:, b * S:(b + 1) * S],
                             qratio[:, b * H + h:b * H + h + 1].to_broadcast([P, P]), ident[:, :])
                ins.then_inc(mark("u_ps"), 1)
                if h >= 1:
                    out_of(h - 1)
            out_of(H - 1)
            pe.wait_ge(*at("x1"))

            def turn_mask(b):
                for n in (2 * b, 2 * b + 1):
                    pe.wait_ge(*at("maskb", b + 1))
                    if n >= 2:
                        pe.wait_ge(*at("maskT", n - 1))
                    pb = PS[:, 6 + n % 2, :].bitcast(BF16)
                    for a in range(8):
                        k0 = (n % 2 * 8 + a) * P
                        ins = pe.transpose(pb[:, a * P:(a + 1) * P], maskb[:, b, k0:k0 + P], identb[:, :])
                    ins.then_inc(mark("maskT_ps"), 1)

            def turn_keys(b, n):
                pe.wait_ge(*at("cx2", b * (16 * QUADS) + 16 * QUADS))
                if not static(b):
                    pe.wait_ge(*at("ct_lo", b * QUADS + n))
                elif n >= 2:
                    pe.wait_ge(*at("ct_lo", n - 1))
                for a in range(NQ):
                    ins = turn(PS[:, key_bank(b, n), a * P:(a + 1) * P], cx2[:, n * NQ + a, :])
                ins.then_inc(mark("ct_ps"), 1)

            turn_rows(xn, 0, "ln1", "ln1_T_ps")
            turn_mask(0)
            pe.wait_ge(*at("ln1_T"))
            mm(PS[:, 1, :], wT[:, WQ, :], xnT[:, :])
            mm(PS[:, 2, :], wT[:, WK, :], xnT[:, :]).then_inc(mark("qk_ps"), 1)
            for b in range(B):
                ins = mm(PS[:, 3, b * D:(b + 1) * D], xnT[:, b * S:(b + 1) * S], wT[:, WV, :])
            ins.then_inc(mark("v_ps"), 1)
            turn_mask(1)
            pe.wait_ge(*at("qk"))
            for b in range(B):
                ins = mm(PS[:, 4, b * S:(b + 1) * S], qT[:, b * S:(b + 1) * S], kT[:, b * S:(b + 1) * S])
            ins.then_inc(mark("sc_ps"), 1)
            turn_mask(2)
            turn_rows(sc, 0, "probs", "pT_ps")
            pe.wait_ge(*at("pT"))
            pe.wait_ge(*at("v0"))
            for b in range(B):
                ins = mm(PS[:, 1, b * S:(b + 1) * S], vv[:, b, :], pT[:, b * S:(b + 1) * S])
            ins.then_inc(mark("oT_ps"), 1)
            turn_mask(3)
            pe.wait_ge(*at("oT"))
            for b in range(B):
                ins = mm(PS[:, 2, b * D:(b + 1) * D], oT[:, b * S:(b + 1) * S], wT[:, WO, :])
            ins.then_inc(mark("o0_ps"), 1)
            pe.wait_ge(*at("maskT", 2 * B))
            turn_keys(0, 0)
            turn_keys(0, 1)

            def route(name, weights):
                for b in range(B):
                    ins = mm(PS[:, 1, b * E:(b + 1) * E], xnT[:, b * S:(b + 1) * S], weights)
                ins.then_inc(mark(name + "_ps"), 1)

            def expert_rows(par, b, done, w2=None):
                w2 = w2T[:, par, :] if w2 is None else w2
                for c in range(FC):
                    ins = mm(PS[:, 6 + par, b * D:(b + 1) * D],
                             hT[:, par, c * B * S + b * S:c * B * S + (b + 1) * S],
                             w2[:, c * D:(c + 1) * D], c == 0, c == FC - 1)
                if b == B - 1:
                    ins.then_inc(mark(done), 1)

            turn_rows(xn, 0, "ln2", "ln2_T_ps")
            pe.wait_ge(*at("ln2_T"))
            route("r0", rwT[:, :])
            turn_keys(0, 2)
            turn_keys(0, 3)
            pe.wait_ge(*at("x2_lo"))
            pe.wait_ge(*at("r0_max"))

            def step0(i, p):
                e, par, n = i * 2 + p, p % 2, i + p // 2
                cur, prev = stage(i, p)
                if cur:
                    pe.wait_ge(*at("w1_0_%d" % par, n * 16 + 16))
                    if prev:
                        pe.wait_ge(*at("e0_T%d" % (1 - par), (i + (p + 1) // 2) * 2))
                        pe.wait_ge(*at("e0_lo", e))
                    for c in range(FC):
                        ins = turn(PS[:, 0, c * P:(c + 1) * P], raw1[:, par, c * P:(c + 1) * P])
                    ins.then_inc(mark("e0_T_ps"), 1)
                    pe.wait_ge(*at("w2_0_%d" % par, n * 16 + 16))
                    for c in range(FC):
                        ins = turn(PS[:, 1, c * P:(c + 1) * P], raw2[:, par, c * P:(c + 1) * P])
                    ins.then_inc(mark("e0_T_ps"), 1)
                if prev:
                    pe.wait_ge(*at("e0_h", e * FC))
                    pe.wait_ge(*at("e0_add%d" % (1 - par), i + (p - 1) // 2))
                for c in range(FC):
                    if prev:
                        expert_rows(1 - par, c, "e0_y%d" % (1 - par))
                    if cur:
                        if c == 0:
                            pe.wait_ge(*at("e0_T%d" % par, n * 2 + 1))
                        hi, lo = (part[:, par, c * P:(c + 1) * P] for part in (w1T_hi, w1T_lo))
                        mm(PS[:, 2 + c, :], hi, x2_hi, True, False)
                        mm(PS[:, 2 + c, :], hi, x2_lo, False, False)
                        if c == 0:
                            pe.wait_ge(*at("e0_lo", e + 1))
                        mm(PS[:, 2 + c, :], lo, x2_hi, False, True).then_inc(mark("e0_h_ps"), 1)
                if not prev:
                    pe.wait_ge(*at("ct_lo", QUADS))

            experts(pe, step0)

            pe.wait_ge(*at("x3"))

            def turn_queries(b):
                pe.wait_ge(*at("qpack", b + 1))
                for a in range(G):
                    ins = turn(PS[:, b, a * P:(a + 1) * P], qpack[:, b * G + a, :])
                ins.then_inc(mark("qTall_ps"), 1)

            pe.wait_ge(*at("qpack_0"))
            turn_queries(0)
            turn_queries(1)

            def scores_for_max(C0, par, g, c):
                if not (static(C0) and C0 + c < 2):
                    pe.wait_ge(*at("smx", C0 + c - 1))
                j, k0 = c // HC, c % HC * 512
                mm(PS[:, 4 + c % 2, :], qp1[:, par, j * S:(j + 1) * S], kp[:, g, k0:k0 + 512]) \
                    .then_inc(mark("smx_ps"), 1)

            def scores(b, g, t, beside):
                U = b * G + g
                N = U * (KT // 2) + t
                if t == 0:
                    pe.wait_ge(*at("qp2", U + 1))
                if not (static(N) and N < 2):
                    pe.wait_ge(*at("pexp", N - 1))
                for a in range(2):
                    kt = 2 * t + a
                    bank = 2 * (t % 2) + a
                    ins = mm(PS[:, bank, :], kp[:, g % G, kt * P:(kt + 1) * P], qp2[:, g % 2, :], True, False)
                    if kt == KT - 1:
                        ins.then_inc(mark("st_unit%d" % (g % G)), 1)
                    ins = mm(PS[:, bank, :].rearrange("p (j q) -> p j q", j=HG), identb[:, :],
                             maskT[:, bass.ds((b + g // G) * KT + kt, 1), :].to_broadcast([P, HG, S]), False, True)
                    if a == 0:
                        beside()
                ins.then_inc(mark("st_ps"), 1)

            def weigh(b, g, t, beside):
                U = b * G + g
                N = U * (KT // 2) + t
                if t == 0:
                    pe.wait_ge(*at("vaug", U + 1))
                    if not static(b) and g == 2:
                        pe.wait_ge(*at("ct_lo", (b + 1) * QUADS + QUADS))
                    if not (static(U) and U < 2):
                        pe.wait_ge(*at("orow", U - 1))
                dst = PS[0:2 * HG * VC, 6 + g % 2, :]
                pe.wait_ge(*at("phi", N + 1))
                for a in range(2):
                    mm(dst, vaug[:, g % G, 2 * t + a, :], p_hi[:, t % 2, a * HG * S:(a + 1) * HG * S],
                       t == 0 and a == 0, False)
                beside()
                for a, made in enumerate(("plo_dve", "plo_pool")):
                    pe.wait_ge(*at(made, N + 1))
                    ins = mm(dst, vaug[:, g % G, 2 * t + a, :], p_lo[:, t % 2, a * HG * S:(a + 1) * HG * S],
                             False, t == KT // 2 - 1 and a == 1)
                ins.then_inc(mark("pv"), 1)

            def unit(b, g):
                U = b * G + g
                cur = not (static(b) and b == B - 1 and g == G)
                prev = not (static(b) and g == 0)
                follow = cur and not (static(b) and b == B - 1 and g == G - 1)
                g1 = (g + 1) % G
                done = [0]

                def chunk(t):
                    c = done[0]
                    if not follow or c >= sum(CHUNKS[:t + 1]):
                        return
                    if c == 0:
                        pe.wait_ge(*at("kp%d" % g1, (b + (g + 1) // G) * (16 * 3 * HG) + 16 * 3 * HG))
                        pe.wait_ge(*at("qp1", U + 2))
                        pe.wait_ge(*at("qp2", U + 1))
                    scores_for_max((U + 1) * HC * HG, (g + 1) % 2, g1, c)
                    done[0] += 1

                for t in range(KT // 2):
                    def beside():
                        chunk(t)

                    if prev and t == 0:
                        weigh(b, g - 1, KT // 2 - 2, lambda: None)
                    if cur:
                        scores(b, g, t, beside)
                        beside()
                    if t >= 2:
                        if cur:
                            weigh(b, g, t - 2, beside)
                    elif prev and t == 1:
                        weigh(b, g - 1, KT // 2 - 1, beside)
                    beside()
                    if follow and t == 7:
                        pe.wait_ge(*at("nm", U + 2))
                        turn(PS[:, 4, 0:P], nm[:, :]).then_inc(mark("nmT_ps"), 1)
                    if prev and t == 3:
                        pe.wait_ge(*at("o_t", U))
                        for j in range(HG):
                            ins = turn(PS[:, 6 + (g - 1) % 2, j * 2 * HG * VC:(j + 1) * 2 * HG * VC],
                                       o_t[0:2 * HG * VC, j * S:(j + 1) * S], 2 * HG * VC)
                        ins.then_inc(mark("o_t_ps"), 1)
                    if not static(b) and (g, t) in KEYS:
                        if KEYS[g, t] == 0:
                            pe.wait_ge(*at("orow", U))
                        turn_keys(b + 1, KEYS[g, t])
                assert not follow or done[0] == HC * HG

            pe.wait_ge(*at("kp0", 16 * 3 * HG))
            pe.wait_ge(*at("qp1"))
            for c in range(HC * HG):
                if c in (2, 4):
                    turn_queries(1 + c // 2)
                scores_for_max(0, 0, 0, c)
            pe.wait_ge(*at("qTall", B))
            pe.wait_ge(*at("nm"))
            turn(PS[:, 4, 0:P], nm[:, :]).then_inc(mark("nmT_ps"), 1)
            phase_c(pe, unit)
            pe.wait_ge(*at("orow", B * G))
            for b in range(B):
                ins = turn(PS[:, 0, b * S:(b + 1) * S], orow[:, b, :])
            ins.then_inc(mark("xo_T_ps"), 1)
            pe.wait_ge(*at("xo_T"))
            for b in range(B):
                ins = mm(PS[:, 1, b * D:(b + 1) * D], oT[:, b * S:(b + 1) * S], wT[:, WFC, :])
            ins.then_inc(mark("fc_ps"), 1)

            turn_rows(xn, 0, "ln4", "ln4_T_ps")
            pe.wait_ge(*at("ln4_T"))
            for bank, n, name in ((1, WQ1, "rms_q_ps"), (2, WV1, "rms_v_ps")):
                for b in range(B):
                    ins = mm(PS[:, bank, b * D:(b + 1) * D], xT1[:, b * S:(b + 1) * S], wT[:, n, :])
                ins.then_inc(mark(name), 1)
            turn_rows(q1r, 3, "rms_q", "q1_T_ps")
            pe.wait_ge(*at("q1_T"))
            pe.wait_ge(*at("rms_v"))

            def causal_scores(b):
                pe.wait_ge(*(at("qbd", b) if b >= 1 else at("qbd0")))
                if b >= 1:
                    pe.wait_ge(*at("s1", b))
                for k in range(4):
                    ins = mm(PS[:, 4 + k, :], xT1[:, b * S:(b + 1) * S],
                             qbd[:, b % 2, k * HG * S:(k + 1) * HG * S])
                ins.then_inc(mark("s1_ps"), 1)

            def causal_rows(b):
                pe.wait_ge(*at("s1", b + 1))
                if b >= 2:
                    pe.wait_ge(*at("o1_own", b - 1))
                for g in range(G):
                    r = g * HG * HD
                    ins = pe.matmul(PS[r:r + HG * HD, 1 + b % 2, :], v1r[:, b, r:r + HG * HD],
                                    sT1[:, b % 2, g * HG * S:(g + 1) * HG * S], start=True, stop=True,
                                    skip_group_check=True)
                ins.then_inc(mark("o1_ps"), 1)

            def causal_turn(b):
                pe.wait_ge(*at("o1_own", b + 1))
                turn(PS[:, 0, b * D:(b + 1) * D], o1s[:, :]).then_inc(mark("o1_T"), 1)

            causal_scores(0)
            for b in range(B):
                if b + 1 < B:
                    causal_scores(b + 1)
                causal_rows(b)
                if b >= 1:
                    causal_turn(b - 1)
            causal_turn(B - 1)

            turn_rows(xn, 0, "ln5", "ln5_T_ps")
            pe.wait_ge(*at("ln5_T"))
            route("r1", rw1[:, :])
            pe.wait_ge(*at("r1_max"))

            def step1(i, p):
                e, par, n = i * 2 + p, p % 2, i + p // 2
                cur, prev = stage(i, p)
                if cur:
                    pe.wait_ge(*at("e1_lo", e + 1))
                for c in range(FC):
                    if cur:
                        if not (static(e) and e * FC + c < 2):
                            pe.wait_ge(*at("e1_h", e * FC + (c - 1)))
                        for a in range(2):
                            dst = PS[:, 2 * (c % 2) + a, :]
                            hi, lo = (part[:, par, (a * FC + c) * P:(a * FC + c + 1) * P]
                                      for part in (wide_hi, wide_lo))
                            mm(dst, hi, x5_hi, True, False)
                            mm(dst, hi, x5_lo, False, False)
                            ins = mm(dst, lo, x5_hi, False, True)
                        ins.then_inc(mark("e1_h_ps"), 1)
                    if prev:
                        if c == 0:
                            pe.wait_ge(*at("e1_h", e * FC))
                            pe.wait_ge(*at("e1_add%d" % (1 - par), i + (p - 1) // 2))
                        expert_rows(1 - par, c, "e1_y%d" % (1 - par),
                                    w2_all[:, bass.ds(e - 1, 1), :].rearrange("p a n -> p (a n)"))

            pe.wait_ge(*at("w2_1", 32))
            pe.wait_ge(*at("x5_lo"))
            experts(pe, step1)


_INS = ["x", "ctx_1024", "mask_Bx1xSxS2_ik1", "L0_xattn_ln_g", "L0_xattn_ln_b", "L0_xattn_w_in",
        "L0_xattn_wp_w1", "L0_xattn_wp_b1", "L0_xattn_wp_ln_g", "L0_xattn_wp_ln_b", "L0_xattn_wp_w2",
        "L0_xattn_wp_b2", "L0_xattn_w_out", "L0_xattn_b_out", "L0_attn_Wq", "L0_attn_bq", "L0_attn_Wk",
        "L0_attn_bk", "L0_attn_Wv", "L0_attn_bv", "L0_attn_Wo", "L0_attn_bo", "L0_ffn_router_w",
        "L0_ffn_w1", "L0_ffn_w2", "L1_xattn_W_fc", "L1_xattn_b_fc", "L1_attn_Wq", "L1_attn_Wv",
        "L1_attn_q_norm_w", "L1_attn_v_norm_w", "L1_ffn_router_w", "L1_ffn_router_b", "L1_ffn_w1",
        "L1_ffn_w2"]


def kernel(**inputs):
    import numpy as _np
    import concourse.bacc as _bacc
    from concourse import mybir as _mybir
    from concourse.bass_utils import run_bass_kernel_spmd as _run

    nc = _bacc.Bacc("TRN2", target_bir_lowering=False, num_devices=1)
    arrays, tensors = {}, {}
    for name in _INS:
        a = _np.ascontiguousarray(inputs[name])
        arrays[f"in_{name}"] = a
        tensors[name] = nc.dram_tensor(f"in_{name}", a.shape, _mybir.dt.from_np(a.dtype),
                                       kind="ExternalInput").ap()
    out = nc.dram_tensor("out_x", inputs["x"].shape, _mybir.dt.float32, kind="ExternalOutput").ap()
    perceiver_two_layers(nc, tensors, out)
    r = _run(nc, [arrays], core_ids=[0])
    return r.results[0]["out_x"]
```
